# Optimizing a Trainium2 kernel written in Bass

```python
import numpy as np
import jax
import jax.numpy as jnp

def _softmax(x, axis=-1):
    return jax.nn.softmax(x, axis=axis)
def _gelu(x):
    return jax.nn.gelu(x, approximate=True)
def _silu(x):
    return jax.nn.silu(x)
def _sigmoid(x):
    return jax.nn.sigmoid(x)
def _layernorm(x, axis=-1, eps=1e-5):
    m = jnp.mean(x, axis=axis, keepdims=True)
    v = jnp.var(x, axis=axis, keepdims=True)
    return (x - m) / jnp.sqrt(v + eps)
def _scatter_add(tgt, idx, src, axis=0):
    return tgt.at[idx].add(src)
def _segment_sum(src, seg, n):
    return jax.ops.segment_sum(src, seg, n)

kernel_name = 'mk_adj_resnorm_d2_adj_256_554312'

def setup_inputs(seed: int = 0):
    np.random.seed(seed)
    _w = jnp.asarray
    def _rec_inputs():
        import jax
        import jax.numpy as jnp
        _gk = jax.random.key(seed)
        x = -0.0002928 + 1 * jax.random.normal(jax.random.fold_in(_gk, 1), (128, 128, 256), jnp.float32)
        _a = jax.random.bernoulli(jax.random.fold_in(_gk, 2), 0.03125, (128, 128, 128))
        _af = _a.astype(jnp.float32)
        _af = _af * jax.random.uniform(jax.random.fold_in(_gk, 3), (128, 128, 128), jnp.float32, 0.05, 0.999995)
        adj = _af
        return x, adj
    x, adj = _rec_inputs()
    def _L0_gnn_setup():
        import jax, jax.numpy as jnp
        import numpy as np
        B, N, D = (4, 4096, 256)
        DENSITY = 0.02
        key = jax.random.key(seed)
        kx, ka1, ka2, kwt, kbt, kwh, kth = jax.random.split(key, 7)
        x = jax.random.normal(kx, (B, N, D), dtype=jnp.float32)
        mask = jax.random.uniform(ka1, (B, N, N)) < DENSITY
        vals = jax.random.uniform(ka2, (B, N, N), dtype=jnp.float32)
        adj = jnp.where(mask, vals, 0.0).astype(jnp.float32)
        s = 0.02
        W_t = s * jax.random.normal(kwt, (D, D), dtype=jnp.float32)
        b_t = s * jax.random.normal(kbt, (D,), dtype=jnp.float32)
        W_h = s * jax.random.normal(kwh, (D, D), dtype=jnp.float32)
        theta = s * jax.random.normal(kth, (D, D), dtype=jnp.float32)
        return {'x': x, 'adj': adj, 'W_t': W_t, 'b_t': b_t, 'W_h': W_h, 'theta': theta}
    _L0_gnn_all = _L0_gnn_setup()
    _L0_gnn_in = {k: v for k, v in _L0_gnn_all.items() if k in ('W_t', 'b_t', 'W_h', 'theta', )}
    del _L0_gnn_all

    def _L1_gnn_setup():
        import jax, jax.numpy as jnp
        import numpy as np
        from jax import lax
        DIM = 256
        EPS = 1e-05

        def _bn(h, g, b, m, v):
            scale = g / jnp.sqrt(v + EPS)
            return h * scale[None, :, None] + (b - m * scale)[None, :, None]

        def _conv1d(h, w, pad):
            return lax.conv_general_dilated(h, w, window_strides=(1,), padding=[(pad, pad)], dimension_numbers=('NCH', 'OIH', 'NCH'))
        key = jax.random.key(seed)
        ks = jax.random.split(key, 16)
        bs, n, d = (16, 2048, DIM)
        s = 0.05
        return {'x': jax.random.normal(ks[0], (bs, n, d), jnp.float32), 'mask': jnp.ones((bs, n, n), jnp.float32), 'w_se': jax.random.normal(ks[1], (3, d), jnp.float32) * s, 'b_se': jnp.zeros((3,), jnp.float32), 'conv1_w': jax.random.normal(ks[2], (d, d, 1), jnp.float32) * s, 'bn1_g': jnp.ones((d,), jnp.float32), 'bn1_b': jnp.zeros((d,), jnp.float32), 'bn1_m': jnp.zeros((d,), jnp.float32), 'bn1_v': jnp.ones((d,), jnp.float32), 'conv2_w': jax.random.normal(ks[3], (d, d, 17), jnp.float32) * s, 'bn2_g': jnp.ones((d,), jnp.float32), 'bn2_b': jnp.zeros((d,), jnp.float32), 'bn2_m': jnp.zeros((d,), jnp.float32), 'bn2_v': jnp.ones((d,), jnp.float32), 'w_msg': jax.random.normal(ks[4], (d, d), jnp.float32) * s, 'b_msg': jnp.zeros((d,), jnp.float32), 'w_ih': jax.random.normal(ks[5], (3 * d, 2 * d), jnp.float32) * s, 'b_ih': jnp.zeros((3 * d,), jnp.float32), 'w_hh': jax.random.normal(ks[6], (3 * d, d), jnp.float32) * s, 'b_hh': jnp.zeros((3 * d,), jnp.float32)}
    _L1_gnn_all = _L1_gnn_setup()
    _L1_gnn_in = {k: v for k, v in _L1_gnn_all.items() if k in ('w_se', 'b_se', 'conv1_w', 'bn1_g', 'bn1_b', 'bn1_m', 'bn1_v', 'conv2_w', 'bn2_g', 'bn2_b', 'bn2_m', 'bn2_v', 'w_msg', 'b_msg', 'w_ih', 'b_ih', 'w_hh', 'b_hh', )}
    del _L1_gnn_all

    return {
        "x": x,
        "adj": adj,
        "L0_gnn_W_t": _L0_gnn_in["W_t"],
        "L0_gnn_b_t": _L0_gnn_in["b_t"],
        "L0_gnn_W_h": _L0_gnn_in["W_h"],
        "L0_gnn_theta": _L0_gnn_in["theta"],
        "L1_gnn_w_se": _L1_gnn_in["w_se"],
        "L1_gnn_b_se": _L1_gnn_in["b_se"],
        "L1_gnn_conv1_w": _L1_gnn_in["conv1_w"],
        "L1_gnn_bn1_g": _L1_gnn_in["bn1_g"],
        "L1_gnn_bn1_b": _L1_gnn_in["bn1_b"],
        "L1_gnn_bn1_m": _L1_gnn_in["bn1_m"],
        "L1_gnn_bn1_v": _L1_gnn_in["bn1_v"],
        "L1_gnn_conv2_w": _L1_gnn_in["conv2_w"],
        "L1_gnn_bn2_g": _L1_gnn_in["bn2_g"],
        "L1_gnn_bn2_b": _L1_gnn_in["bn2_b"],
        "L1_gnn_bn2_m": _L1_gnn_in["bn2_m"],
        "L1_gnn_bn2_v": _L1_gnn_in["bn2_v"],
        "L1_gnn_w_msg": _L1_gnn_in["w_msg"],
        "L1_gnn_b_msg": _L1_gnn_in["b_msg"],
        "L1_gnn_w_ih": _L1_gnn_in["w_ih"],
        "L1_gnn_b_ih": _L1_gnn_in["b_ih"],
        "L1_gnn_w_hh": _L1_gnn_in["w_hh"],
        "L1_gnn_b_hh": _L1_gnn_in["b_hh"],
    }

def reference(x, adj, L0_gnn_W_t, L0_gnn_b_t, L0_gnn_W_h, L0_gnn_theta, L1_gnn_w_se, L1_gnn_b_se, L1_gnn_conv1_w, L1_gnn_bn1_g, L1_gnn_bn1_b, L1_gnn_bn1_m, L1_gnn_bn1_v, L1_gnn_conv2_w, L1_gnn_bn2_g, L1_gnn_bn2_b, L1_gnn_bn2_m, L1_gnn_bn2_v, L1_gnn_w_msg, L1_gnn_b_msg, L1_gnn_w_ih, L1_gnn_b_ih, L1_gnn_w_hh, L1_gnn_b_hh):
    import jax
    import jax.numpy as jnp
    def _L0_gnn_ref(x, adj, W_t, b_t, W_h, theta):
        import jax, jax.numpy as jnp
        import numpy as np
        B, N, D = (4, 4096, 256)
        DENSITY = 0.02
        in_degrees = jnp.sum(adj, axis=-1)
        norm = jnp.power(in_degrees + 1e-06, -0.5)[..., None]
        f_hom = jnp.einsum('bnd,de->bne', x, theta) * norm
        f_hom = jnp.einsum('bnm,bmd->bnd', adj, f_hom) * norm
        f_het = jnp.einsum('bnd,de->bne', x, W_h)
        gate = jax.nn.sigmoid(jnp.einsum('bnd,de->bne', x, W_t) + b_t)
        out = gate * f_hom + (1.0 - gate) * f_het
        return jax.nn.elu(out)

    def _L1_gnn_ref(x, mask, w_se, b_se, conv1_w, bn1_g, bn1_b, bn1_m, bn1_v, conv2_w, bn2_g, bn2_b, bn2_m, bn2_v, w_msg, b_msg, w_ih, b_ih, w_hh, b_hh):
        import jax, jax.numpy as jnp
        import numpy as np
        from jax import lax
        DIM = 256
        EPS = 1e-05

        def _bn(h, g, b, m, v):
            scale = g / jnp.sqrt(v + EPS)
            return h * scale[None, :, None] + (b - m * scale)[None, :, None]

        def _conv1d(h, w, pad):
            return lax.conv_general_dilated(h, w, window_strides=(1,), padding=[(pad, pad)], dimension_numbers=('NCH', 'OIH', 'NCH'))
        d = x.shape[-1]
        xc = jnp.transpose(x, (0, 2, 1))
        h = _bn(_conv1d(xc, conv1_w, 0), bn1_g, bn1_b, bn1_m, bn1_v)
        h = jax.nn.relu(h)
        h = _bn(_conv1d(h, conv2_w, 8), bn2_g, bn2_b, bn2_m, bn2_v)
        x_conv = jnp.transpose(jax.nn.relu(h + xc), (0, 2, 1))
        s = x @ w_se.T + b_se
        sq = jnp.sum(s * s, axis=-1)
        dist = sq[:, :, None] + sq[:, None, :] - 2.0 * jnp.einsum('bnd,bmd->bnm', s, s)
        A = jnp.exp(-dist) * mask
        msg = jax.nn.relu(x @ w_msg.T + b_msg)
        x_nmp = jnp.einsum('bnm,bmd->bnd', A, msg)
        x_in = jnp.concatenate([x_conv, x_nmp], axis=-1)
        gi = x_in @ w_ih.T + b_ih
        gh = x @ w_hh.T + b_hh
        gi_r, gi_z, gi_n = (gi[..., :d], gi[..., d:2 * d], gi[..., 2 * d:])
        gh_r, gh_z, gh_n = (gh[..., :d], gh[..., d:2 * d], gh[..., 2 * d:])
        r = jax.nn.sigmoid(gi_r + gh_r)
        z = jax.nn.sigmoid(gi_z + gh_z)
        nn_ = jnp.tanh(gi_n + r * gh_n)
        return (1.0 - z) * nn_ + z * x

    x = _layernorm(x + _L0_gnn_ref(x, adj, L0_gnn_W_t, L0_gnn_b_t, L0_gnn_W_h, L0_gnn_theta), axis=-1)
    x = _layernorm(x + _L1_gnn_ref(x, adj, L1_gnn_w_se, L1_gnn_b_se, L1_gnn_conv1_w, L1_gnn_bn1_g, L1_gnn_bn1_b, L1_gnn_bn1_m, L1_gnn_bn1_v, L1_gnn_conv2_w, L1_gnn_bn2_g, L1_gnn_bn2_b, L1_gnn_bn2_m, L1_gnn_bn2_v, L1_gnn_w_msg, L1_gnn_b_msg, L1_gnn_w_ih, L1_gnn_b_ih, L1_gnn_w_hh, L1_gnn_b_hh), axis=-1)
    return x


_drawn_inputs = setup_inputs


def setup_inputs(seed=0):
    import zlib

    import numpy as np

    out = dict(_drawn_inputs(seed))
    spreads = {'L1_gnn_b_se': (0.0, 0.8),
     'L1_gnn_bn1_g': (1.0, 0.2),
     'L1_gnn_bn1_b': (0.0, 0.1),
     'L1_gnn_bn1_m': (0.0, 0.1),
     'L1_gnn_bn1_v': (1.0, 0.535),
     'L1_gnn_bn2_g': (1.0, 0.2),
     'L1_gnn_bn2_b': (0.0, 0.571),
     'L1_gnn_bn2_m': (0.0, 0.47),
     'L1_gnn_bn2_v': (1.0, 0.588),
     'L1_gnn_b_msg': (0.0, 0.8),
     'L1_gnn_b_ih': (0.0, 0.332),
     'L1_gnn_b_hh': (0.0, 0.413)}
    factors = {'L0_gnn_b_t': 8.0}
    for name, (base, spread) in spreads.items():
        noise = np.random.default_rng([zlib.crc32(name.encode()), seed]).standard_normal(out[name].shape)
        drawn = base * np.exp(spread * noise) if base else spread * noise
        out[name] = jnp.asarray(drawn.astype(out[name].dtype))
    for name, factor in factors.items():
        out[name] = (out[name] * factor).astype(out[name].dtype)
    return out
```

```python
from contextlib import ExitStack

import numpy as np

import concourse.bass as bass
from concourse import mybir

F32 = mybir.dt.float32
F32R = mybir.dt.float32r
ALU = mybir.AluOpType
ACT = mybir.ActivationFunctionType
AX_X = mybir.AxisListType.X

P = 128
D = 256
KD = D // P
EPS = 1e-5


def reached(eng, sem, count):
    if isinstance(count, int) and count <= 0:
        return
    eng.wait_ge(sem, count)


def pipeline(eng, units, stages, step):
    first = stages + stages % 2
    for i in range(first):
        step(i, i % 2, lambda s, i=i: 0 <= i - s < units)
    with eng.Fori(first // 2, units // 2) as two:
        step(two * 2, 0, lambda s: True)
        step(two * 2 + 1, 1, lambda s: True)
    for i in range(units, units + stages - 1):
        step(i, i % 2, lambda s, i=i: 0 <= i - s < units)


def phase_a(nc, G, x_n, x_t, adj_n, adj_t, w0, b_t, x1_t):
    pairs = G // 2
    with ExitStack() as ctx:
        def sb(name, shape, dt=F32):
            return ctx.enter_context(nc.sbuf_tensor("a_" + name, shape, dt))

        def sem(name):
            return ctx.enter_context(nc.semaphore("a_" + name))

        w_raw = sb("w_raw", [P, KD, 3 * D])
        w_hi = sb("w_hi", [P, KD, 3 * D], F32R)
        w_lo = sb("w_lo", [P, KD, 3 * D], F32R)
        bt_row = sb("bt_row", [P, 2, D])
        ident = sb("ident", [P, P])
        neg_half = sb("neg_half", [P, 2])
        xn = sb("xn", [P, 2, 2, D])
        xt = sb("xt", [P, 2, KD, 2 * P])
        an = sb("an", [P, 2, 2, P])
        at = sb("at", [P, 2, 2, P])
        xh = sb("xh", [P, 2, KD, 2 * P], F32R)
        xl = sb("xl", [P, 2, KD, 2 * P], F32R)
        ah = sb("ah", [P, 2, 2, P], F32R)
        al = sb("al", [P, 2, 2, P], F32R)
        fh = sb("fh", [P, 2, 2, D], F32R)
        fl = sb("fl", [P, 2, 2, D], F32R)
        deg = sb("deg", [P, 2, 2])
        deg_eps = sb("deg_eps", [P, 2, 2])
        norm = sb("norm", [P, 2, 2])
        het = sb("het", [P, 2, 2, D])
        pre = sb("pre", [P, 2, 2, D])
        gate = sb("gate", [P, 2, 2, D])
        diff = sb("diff", [P, 2, D])
        gd = sb("gd", [P, 2, D])
        mix = sb("mix", [P, 2, D])
        below = sb("below", [P, 2, D])
        ex = sb("ex", [P, 2, D])
        em1 = sb("em1", [P, 2, D])
        res = sb("res", [P, 2, D])
        y = sb("y", [P, 2, D])
        stats = sb("stats", [P, 2, 6])
        mv = sb("mv", [P, 2, 2])
        var_eps = sb("var_eps", [P, 2])
        rstd = sb("rstd", [P, 2])
        x1 = sb("x1", [P, 2, 2, D])
        x1t = sb("x1t", [P, 2, KD, 2 * P])

        ps_hh = ctx.enter_context(nc.psum_tensor("a_ps_hh", [P, 4, 2 * D], F32))
        ps_g = ctx.enter_context(nc.psum_tensor("a_ps_g", [P, 2, 2, D], F32))
        ps_hom = ctx.enter_context(nc.psum_tensor("a_ps_hom", [P, 2, D], F32))
        ps_t = ctx.enter_context(nc.psum_tensor("a_ps_t", [P, KD, 2 * P], F32))

        s_w = sem("weights_loaded")
        s_wh = sem("weights_high")
        s_wl = sem("weights_low")
        s_id0 = sem("identity_zeroed")
        s_id = sem("identity_ready")
        s_half = sem("half_ready")
        s_in = [sem("pair_loaded0"), sem("pair_loaded1")]
        s_xn = [sem("x_loaded0"), sem("x_loaded1")]
        s_xh = sem("x_high")
        s_ah = sem("adj_high")
        s_xl = sem("x_low")
        s_al = sem("adj_low")
        s_deg = sem("degree")
        s_dege = sem("degree_eps")
        s_norm = sem("norm")
        s_proj = sem("projected")
        s_fh = sem("f_high")
        s_fl = sem("f_low")
        s_het = sem("het_copied")
        s_pre = sem("gate_biased")
        s_gate = sem("gate_ready")
        s_hom = sem("hom_done")
        s_diff = sem("diff_done")
        s_gd = sem("gated_diff")
        s_mix = sem("mixed")
        s_below = sem("mix_clamped")
        s_ex = sem("exp_done")
        s_em1 = sem("exp_minus_one")
        s_res = sem("residual_added")
        s_y = sem("y_done")
        s_bn = sem("bn_stats_done")
        s_mv = sem("mean_var")
        s_ve = sem("var_eps_done")
        s_rstd = sem("rstd_done")
        s_x1 = sem("x1_done")
        s_tr = sem("transposed")
        s_x1t = sem("x1t_copied")
        s_out = [sem("x1t_stored0"), sem("x1t_stored1")]
        block = ctx.enter_context(nc.Block())

        @block.sync
        def _(sp):
            sp.dma_start(w_raw[:, :, :], w0).then_inc(s_w, 16)
            sp.dma_start(bt_row[:, 0, :], b_t.partition_broadcast(P)).then_inc(s_w, 16)
            sp.dma_start(bt_row[:, 1, :], b_t.partition_broadcast(P)).then_inc(s_w, 16)

            def step(i, u, live):
                if live(0):
                    p = i
                    reached(sp, s_xl, p - 1)
                    reached(sp, s_al, p - 1)
                    reached(sp, s_deg, p - 1)
                    sp.dma_start(xt[:, u], x_t[:, :, bass.ts(p, 2 * P)]).then_inc(s_in[u], 16)
                    sp.dma_start(an[:, u], adj_n[:, bass.ts(p, 2 * P)].rearrange("p (b m) -> p b m", b=2)).then_inc(s_in[u], 16)
                    sp.dma_start(at[:, u], adj_t[:, bass.ts(p, 2 * P)].rearrange("p (b m) -> p b m", b=2)).then_inc(s_in[u], 16)
                if live(2):
                    p = i - 2
                    reached(sp, s_res, p - 1)
                    sp.dma_start(xn[:, u], x_n[:, bass.ts(p, 2 * D)].rearrange("p (b d) -> p b d", b=2)).then_inc(s_xn[u], 16)
                if live(4):
                    p = i - 4
                    reached(sp, s_x1t, p + 1)
                    sp.dma_start(x1_t[:, :, bass.ts(p, 2 * P)], x1t[:, u]).then_inc(s_out[u], 16)

            pipeline(sp, pairs, 5, step)
            for u in range(2):
                sp.wait_ge(s_out[u], 16 * (pairs // 2))

        def loaded(eng, sems, per_pair, p, u):
            reached(eng, sems[u], (p + (2 - u)) * (8 * per_pair))

        @block.scalar
        def _(act):
            act.wait_ge(s_w, 48)
            nc.scalar.activation(w_hi[:, :, :], w_raw[:, :, :], ACT.Copy).then_inc(s_wh, 1)

            def step(i, u, live):
                if live(1):
                    p, v = i - 1, 1 - u
                    loaded(act, s_in, 3, p, v)
                    reached(act, s_proj, p - 1)
                    nc.scalar.activation(xh[:, v], xt[:, v], ACT.Copy).then_inc(s_xh, 1)
                    reached(act, s_hom, p - 1)
                    nc.scalar.activation(ah[:, v], at[:, v], ACT.Copy).then_inc(s_ah, 1)
                if live(3):
                    p = i - 3
                    reached(act, s_below, p + 1)
                    reached(act, s_em1, p)
                    nc.scalar.activation(ex[:, :, :], below[:, :, :], ACT.Exp).then_inc(s_ex, 1)
                    reached(act, s_ex, p + 1)
                    reached(act, s_res, p)
                    nc.scalar.activation(em1[:, :, :], ex[:, :, :], ACT.Copy, bias=-1.0).then_inc(s_em1, 1)
                if live(2):
                    p, v = i - 2, u
                    reached(act, s_proj, p + 1)
                    reached(act, s_norm, p + 1)
                    reached(act, s_hom, p - 1)
                    for b in range(2):
                        nc.scalar.activation(fh[:, v, b], ps_hh[:, 2 * v + b, 0:D], ACT.Copy,
                                             scale=norm[:, v, b:b + 1]).then_inc(s_fh, 1)
                    reached(act, s_mix, p - 1)
                    nc.scalar.activation(het[:, v], ps_hh[:, 2 * v:2 * v + 2, D:2 * D], ACT.Copy).then_inc(s_het, 1)
                    reached(act, s_pre, p + 1)
                    reached(act, s_gd, p - 1)
                    nc.scalar.activation(gate[:, v], pre[:, v], ACT.Tanh, scale=0.5).then_inc(s_gate, 1)
                if live(4):
                    p, v = i - 4, u
                    reached(act, s_tr, p + 1)
                    reached(act, s_out[v], (p - v) * 8)
                    nc.scalar.activation(x1t[:, v], ps_t[:, :, :], ACT.Copy).then_inc(s_x1t, 1)

            pipeline(act, pairs, 5, step)

        @block.gpsimd
        def _(pool):
            nc.gpsimd.memset(ident[:, :], 0.0).then_inc(s_id0, 1)
            nc.gpsimd.memset(neg_half[:, :], -0.5).then_inc(s_half, 1)
            pool.wait_ge(s_id0, 1)
            nc.gpsimd.affine_select(out=ident[:, :], in_=ident[:, :], compare_op=ALU.not_equal, fill=1.0,
                                    base=0, pattern=[[-1, P]], channel_multiplier=1).then_inc(s_id, 1)
            pool.wait_ge(s_half, 1)

            def step(i, u, live):
                if live(3):
                    p = i - 3
                    reached(pool, s_em1, p + 1)
                    reached(pool, s_y, p)
                    loaded(pool, s_xn, 1, p, 1 - u)
                    nc.gpsimd.tensor_tensor(res[:, :, :], em1[:, :, :], xn[:, 1 - u], ALU.add).then_inc(s_res, 1)
                if live(1):
                    p, v = i - 1, 1 - u
                    reached(pool, s_dege, p + 1)
                    reached(pool, s_diff, 2 * p - 2)
                    nc.gpsimd.tensor_tensor(norm[:, v], deg_eps[:, v], neg_half[:, :], ALU.pow).then_inc(s_norm, 1)
                    reached(pool, s_xh, p + 1)
                    nc.gpsimd.tensor_tensor(xl[:, v], xt[:, v], xh[:, v].bitcast(F32), ALU.subtract).then_inc(s_xl, 1)
                    reached(pool, s_ah, p + 1)
                    nc.gpsimd.tensor_tensor(al[:, v], at[:, v], ah[:, v].bitcast(F32), ALU.subtract).then_inc(s_al, 1)
                if live(3):
                    p = i - 3
                    reached(pool, s_ve, p + 1)
                    reached(pool, s_x1, p)
                    nc.gpsimd.tensor_tensor(rstd[:, :], var_eps[:, :], neg_half[:, :], ALU.pow).then_inc(s_rstd, 1)

            pipeline(pool, pairs, 5, step)

        @block.vector
        def _(dve):
            dve.wait_ge(s_wh, 1)
            nc.vector.tensor_tensor(w_lo[:, :, :], w_raw[:, :, :], w_hi[:, :, :].bitcast(F32), ALU.subtract).then_inc(s_wl, 1)

            def step(i, u, live):
                if live(3):
                    p, v = i - 3, 1 - u
                    reached(dve, s_hom, p + 1)
                    reached(dve, s_het, p + 1)
                    for b in range(2):
                        nc.vector.scalar_tensor_tensor(diff[:, b], ps_hom[:, b], norm[:, v, b:b + 1], het[:, v, b],
                                                       ALU.mult, ALU.subtract).then_inc(s_diff, 1)
                if live(1):
                    q, w = i - 1, 1 - u
                    loaded(dve, s_in, 3, q, w)
                    reached(dve, s_dege, q)
                    nc.vector.tensor_reduce(deg[:, w], an[:, w], AX_X, ALU.add).then_inc(s_deg, 1)
                if live(3):
                    reached(dve, s_gate, p + 1)
                    reached(dve, s_diff, 2 * p + 2)
                    nc.vector.scalar_tensor_tensor(gd[:, :, :], gate[:, v], 1.0, diff[:, :, :],
                                                   ALU.add, ALU.mult).then_inc(s_gd, 1)
                if live(1):
                    q = i - 1
                    reached(dve, s_deg, q + 1)
                    reached(dve, s_norm, q - 1)
                    nc.vector.tensor_scalar(deg_eps[:, w], deg[:, w], 1e-6, None, ALU.add).then_inc(s_dege, 1)
                if live(3):
                    reached(dve, s_gd, p + 1)
                    nc.vector.scalar_tensor_tensor(mix[:, :, :], gd[:, :, :], 0.5, het[:, v],
                                                   ALU.mult, ALU.add).then_inc(s_mix, 1)
                    reached(dve, s_mix, p + 1)
                    reached(dve, s_ex, p)
                    nc.vector.tensor_scalar(below[:, :, :], mix[:, :, :], 0.0, None, ALU.min).then_inc(s_below, 1)
                if live(2):
                    q, w = i - 2, u
                    reached(dve, s_proj, q + 1)
                    reached(dve, s_gate, q - 1)
                    nc.vector.tensor_tensor(pre[:, w], ps_g[:, w], bt_row[:, :, :], ALU.add).then_inc(s_pre, 1)
                if live(2):
                    reached(dve, s_het, q + 1)
                    for b in range(2):
                        nc.vector.scalar_tensor_tensor(fl[:, w, b], ps_hh[:, 2 * w + b, 0:D], norm[:, w, b:b + 1],
                                                       fh[:, w, b].bitcast(F32), ALU.mult, ALU.subtract).then_inc(s_fl, 1)
                if live(3):
                    reached(dve, s_res, p + 1)
                    nc.vector.scalar_tensor_tensor(y[:, :, :], mix[:, :, :], 0.0, res[:, :, :],
                                                   ALU.max, ALU.add).then_inc(s_y, 1)
                    reached(dve, s_y, p + 1)
                    for b in range(2):
                        nc.vector.bn_stats(stats[:, b], y[:, b]).then_inc(s_bn, 1)
                    dve.wait_ge(s_wh, 1)
                    reached(dve, s_bn, 2 * p + 2)
                    for b in range(2):
                        nc.vector.bn_aggr(mv[:, b], stats[:, b]).then_inc(s_mv, 1)
                    reached(dve, s_mv, 2 * p + 2)
                    nc.vector.tensor_scalar(var_eps[:, :], mv[:, :, 1], EPS, None, ALU.add).then_inc(s_ve, 1)
                    reached(dve, s_rstd, p + 1)
                    reached(dve, s_tr, p - 1)
                    for b in range(2):
                        last = nc.vector.tensor_scalar(x1[:, v, b], y[:, b], mv[:, b, 0:1], rstd[:, b:b + 1],
                                                       ALU.subtract, ALU.mult)
                        if b == 1:
                            last.then_inc(s_x1, 1)

            pipeline(dve, pairs, 5, step)

        @block.tensor
        def _(pe):
            pe.wait_ge(s_wl, 1)
            pe.wait_ge(s_id, 1)

            def step(i, u, live):
                if live(2):
                    p, v = i - 2, u
                    reached(pe, s_xh, p + 1)
                    reached(pe, s_xl, p + 1)
                    reached(pe, s_het, p - 1)
                    reached(pe, s_fl, 2 * p - 2)
                    reached(pe, s_pre, p - 1)
                    for b in range(2):
                        cols = slice(b * P, b * P + P)
                        for out, part in ((ps_hh[:, 2 * v + b, :], slice(0, 2 * D)), (ps_g[:, v, b, :], slice(2 * D, 3 * D))):
                            terms = [(xx, ww, k) for k in range(KD) for xx, ww in ((xl, w_hi), (xh, w_lo), (xh, w_hi))]
                            for n, (xx, ww, k) in enumerate(terms):
                                last = nc.tensor.matmul(out, xx[:, v, k, cols], ww[:, k, part],
                                                        start=(n == 0), stop=(n == len(terms) - 1))
                    last.then_inc(s_proj, 1)
                if live(3):
                    p, v = i - 3, 1 - u
                    reached(pe, s_fl, 2 * p + 2)
                    reached(pe, s_fh, 2 * p + 2)
                    reached(pe, s_ah, p + 1)
                    reached(pe, s_al, p + 1)
                    reached(pe, s_diff, 2 * p)
                    for b in range(2):
                        terms = ((al, fh), (ah, fl), (ah, fh))
                        for n, (aa, ff) in enumerate(terms):
                            last = nc.tensor.matmul(ps_hom[:, b], aa[:, v, b], ff[:, v, b], start=(n == 0), stop=(n == 2))
                    last.then_inc(s_hom, 1)
                if live(4):
                    p, v = i - 4, u
                    reached(pe, s_x1, p + 1)
                    reached(pe, s_x1t, p)
                    for b in range(2):
                        for k in range(KD):
                            last = nc.tensor.transpose(ps_t[:, k, b * P:b * P + P], x1[:, v, b, k * P:k * P + P], ident[:, :])
                    last.then_inc(s_tr, 1)

            pipeline(pe, pairs, 5, step)


def phase_b(nc, G, x1_t, w_c1, w_c2, bn1, bn2, xc_t):
    B = 8
    HB = B // 2
    T, HT = B * P, HB * P
    groups = G // B
    TAPS = w_c2.shape[2]
    PAD = (TAPS - 1) // 2
    Q = (TAPS + 2) // 3
    HALF = P // 2
    HW = HALF + PAD
    SW = HW - 1
    EDGE = PAD // 2
    assert TAPS == 3 * Q - 1 and PAD % 2 == 0
    PRODUCTS = ((0, 0, Q), (0, 1, Q - 1), (1, 0, Q), (2, 0, Q))
    BASE = (0, Q, 2 * Q - 1, 3 * Q - 1)
    NW = 4 * Q - 1
    NSEQ = 3
    with ExitStack() as ctx:
        def sb(name, shape, dt=F32):
            return ctx.enter_context(nc.sbuf_tensor("b_" + name, shape, dt))

        def sem(name):
            return ctx.enter_context(nc.semaphore("b_" + name))

        w2_h = sb("w2_h", [P, NW, KD, D], F32R)
        w2_l = sb("w2_l", [P, NW, KD, D], F32R)
        w1_h = sb("w1_h", [P, KD, D], F32R)
        w1_l = sb("w1_l", [P, KD, D], F32R)
        seq_h = sb("seq_h", [P, NSEQ, KD, 2, B, SW], F32R)
        seq_l = sb("seq_l", [P, NSEQ, KD, 2, B, SW], F32R)
        hp = sb("hp", [P, KD, 2, B, HW])
        seq = sb("seq", [P, 2, B, SW])
        x = sb("x", [P, 2, KD, HT])
        xh = sb("xh", [P, KD, HT], F32R)
        xl = sb("xl", [P, KD, HT], F32R)
        acc = sb("acc", [P, KD, 2, B, HALF])
        t = sb("t", [P, KD, T])
        xr = sb("xr", [P, KD, T])
        raw = xr[:, :, :].rearrange("p u (z o) -> p u z o", o=D)
        fsum = t[:, :, :].rearrange("p u (z o) -> p u z o", o=D)
        bn = sb("bn", [P, 2, 4, KD])
        ve = sb("ve", [P, 2, KD])
        rs = sb("rs", [P, 2, KD])
        scale = sb("scale", [P, 2, KD])
        mscale = sb("mscale", [P, 2, KD])
        shift = sb("shift", [P, 2, KD])
        neg_half = sb("neg_half", [P, 2, KD])

        ps_c1 = ctx.enter_context(nc.psum_tensor("b_ps_c1", [P, KD, HT], F32))
        ps_c2 = ctx.enter_context(nc.psum_tensor("b_ps_c2", [P, 4, B * HALF], F32))

        s_w1 = sem("conv1_weights_loaded")
        s_bnl = sem("bn_loaded")
        s_raw = [sem("taps_loaded0"), sem("taps_loaded1")]
        s_half = sem("half_ready")
        s_pad = sem("padding_zeroed")
        s_c = sem("bn_steps")
        s_rs = sem("bn_rsqrt")
        s_w1h = sem("conv1_weights_high")
        s_w1l = sem("conv1_weights_low")
        s_f02 = sem("taps_0_2_summed")
        s_fpm = sem("filter_sums")
        s_fh = sem("filter_high")
        s_fl = sem("filter_low")
        s_x = [sem("x1_half0_loaded"), sem("x1_half1_loaded")]
        s_xh = sem("x1_high")
        s_xl = sem("x1_low")
        s_c1 = sem("conv1_done")
        s_hp = sem("conv1_activated")
        s_seq = sem("sequence_made")
        s_sh = sem("sequence_high")
        s_sl = sem("sequence_low")
        s_c2 = sem("conv2_product_done")
        s_ev = sem("even_started")
        s_od = sem("odd_started")
        s_m1 = sem("m1_added")
        s_m2 = sem("m2_added")
        s_xr = sem("residual_loaded")
        s_t = sem("residual_added")
        s_xc = sem("xconv_ready")
        s_out = [sem("xconv_stored0"), sem("xconv_stored1")]
        block = ctx.enter_context(nc.Block())

        SEQ_FREE = (4, 6, 8)

        @block.sync
        def _(sp):
            sp.dma_start(x[:, 0, :, 0:D], w_c1).then_inc(s_w1, 16)
            for n, vectors in enumerate((bn1, bn2)):
                sp.dma_start(bn[:, n], vectors).then_inc(s_bnl, 16)
            for n in range(Q * KD):
                q, k = n // KD, n % KD
                taps = min(3, TAPS - 3 * q)
                reached(sp, s_fl, 4 * (n - 1))
                sp.dma_start(raw[:, n % 2, 0:taps, :], w_c2[:, k, 3 * q:3 * q + taps, :]).then_inc(s_raw[n % 2], 16)
            sp.wait_ge(s_fl, 4 * Q * KD)
            sp.wait_ge(s_w1l, 1)

            def step(i, u, live):
                if live(0):
                    g = i
                    reached(sp, s_xl, 2 * g - 1)
                    sp.dma_start(x[:, 0], x1_t[:, :, bass.ds(g * T, HT)]).then_inc(s_x[0], 16)
                if live(2):
                    g = i - 2
                    reached(sp, s_t, 4 * g)
                    sp.dma_start(xr[:, :, :], x1_t[:, :, bass.ts(g, T)]).then_inc(s_xr, 16)
                if live(0):
                    g = i
                    reached(sp, s_xl, 2 * g)
                    sp.dma_start(x[:, 1], x1_t[:, :, bass.ds(g * T + HT, HT)]).then_inc(s_x[1], 16)
                if live(2):
                    g = i - 2
                    for mt in range(KD):
                        reached(sp, s_xc, 2 * g + mt + 1)
                        sp.dma_start(xc_t[:, mt, bass.ts(g, T)], t[:, mt]).then_inc(s_out[mt], 16)

            pipeline(sp, groups, 3, step)
            for mt in range(KD):
                sp.wait_ge(s_out[mt], 16 * groups)

        @block.scalar
        def _(act):
            act.wait_ge(s_w1, 16)
            nc.scalar.activation(w1_h[:, :, :], x[:, 0, :, 0:D], ACT.Copy).then_inc(s_w1h, 1)
            for n in range(Q * KD):
                q, k, w = n // KD, n % KD, n % 2
                act.wait_ge(s_raw[w], 16 * (n // 2 + 1))
                nc.scalar.activation(w2_h[:, BASE[0] + q, k], raw[:, w, 0], ACT.Copy).then_inc(s_fh, 1)
                if q < Q - 1:
                    nc.scalar.activation(w2_h[:, BASE[1] + q, k], raw[:, w, 2], ACT.Copy).then_inc(s_fh, 1)
                for e in range(2):
                    reached(act, s_fpm, 2 * n + e + 1)
                    nc.scalar.activation(w2_h[:, BASE[2 + e] + q, k], fsum[:, w, 1 + e], ACT.Copy, scale=0.5).then_inc(s_fh, 1)
            act.wait_ge(s_c, 5)
            act.wait_ge(s_pad, 1)

            def high(g, n):
                s, k = n // 2, n % 2
                reached(act, s_seq, 6 * g + n + 1)
                reached(act, s_c2, 8 * g - 8 + SEQ_FREE[s])
                nc.scalar.activation(seq_h[:, s, k], seq[:, :, :, :], ACT.Copy).then_inc(s_sh, 1)

            def split_x(g, h):
                reached(act, s_x[h], 16 * g + 16)
                reached(act, s_c1, 2 * (2 * g + h))
                nc.scalar.activation(xh[:, :, :], x[:, h], ACT.Copy).then_inc(s_xh, 1)

            def conv1_out(g, h):
                for mt in range(KD):
                    reached(act, s_c1, 2 * (2 * g + h) + mt + 1)
                    reached(act, s_seq, 6 * g)
                    nc.scalar.activation(hp[:, mt, :, h * HB:h * HB + HB, EDGE:EDGE + HALF],
                                         ps_c1[:, mt].rearrange("p (b i r) -> p r b i", b=HB, r=2), ACT.Relu,
                                         bias=shift[:, 0, mt:mt + 1], scale=scale[:, 0, mt:mt + 1]).then_inc(s_hp, 1)

            def step(i, u, live):
                gf, gc = i - 1, i - 2
                if live(2):
                    for n in (4, 5):
                        high(gc, n)
                    for mt in range(KD):
                        reached(act, s_c2, 8 * gc + mt + 1)
                        reached(act, s_t, 4 * gc - 2 + 2 * mt)
                        nc.scalar.activation(acc[:, mt, 0], ps_c2[:, mt].rearrange("p (b i) -> p b i", b=B), ACT.Copy).then_inc(s_ev, 1)
                if live(1):
                    conv1_out(gf, 0)
                    split_x(gf, 1)
                if live(2):
                    for mt in range(KD):
                        reached(act, s_c2, 8 * gc + 2 + mt + 1)
                        nc.scalar.activation(acc[:, mt, 1], ps_c2[:, 2 + mt].rearrange("p (b i) -> p b i", b=B), ACT.Copy,
                                             scale=-1.0).then_inc(s_od, 1)
                if live(1):
                    conv1_out(gf, 1)
                if live(0):
                    split_x(i, 0)
                if live(1):
                    for n in range(4):
                        high(gf, n)
                if live(2):
                    for mt in range(KD):
                        reached(act, s_t, 4 * gc + 2 * mt + 2)
                        nc.scalar.activation(t[:, mt], t[:, mt], ACT.Relu, bias=shift[:, 1, mt:mt + 1]).then_inc(s_xc, 1)

            pipeline(act, groups, 3, step)

        @block.gpsimd
        def _(pool):
            nc.gpsimd.memset(neg_half[:, :, :], -0.5).then_inc(s_half, 1)
            nc.gpsimd.memset(hp[:, :, :, :, :], 0.0).then_inc(s_pad, 1)
            pool.wait_ge(s_half, 1)
            pool.wait_ge(s_c, 1)
            nc.gpsimd.tensor_tensor(rs[:, :, :], ve[:, :, :], neg_half[:, :, :], ALU.pow).then_inc(s_rs, 1)

        @block.vector
        def _(dve):
            dve.wait_ge(s_bnl, 32)
            nc.vector.tensor_scalar(ve[:, :, :], bn[:, :, 3], EPS, None, ALU.add).then_inc(s_c, 1)
            dve.wait_ge(s_rs, 1)
            nc.vector.tensor_tensor(scale[:, :, :], bn[:, :, 0], rs[:, :, :], ALU.mult).then_inc(s_c, 1)
            dve.wait_ge(s_c, 2)
            nc.vector.tensor_tensor(mscale[:, :, :], bn[:, :, 2], scale[:, :, :], ALU.mult).then_inc(s_c, 1)
            dve.wait_ge(s_c, 3)
            nc.vector.tensor_tensor(shift[:, :, :], bn[:, :, 1], mscale[:, :, :], ALU.subtract).then_inc(s_c, 2)
            dve.wait_ge(s_w1h, 1)
            nc.vector.tensor_tensor(w1_l[:, :, :], x[:, 0, :, 0:D], w1_h[:, :, :].bitcast(F32), ALU.subtract).then_inc(s_w1l, 1)
            highs = 0
            for n in range(Q * KD):
                q, k, w = n // KD, n % KD, n % 2
                last_triple = q == Q - 1
                dve.wait_ge(s_raw[w], 16 * (n // 2 + 1))
                outer = raw[:, w, 0]
                if not last_triple:
                    reached(dve, s_fpm, 2 * n)
                    nc.vector.tensor_tensor(fsum[:, w, 0], raw[:, w, 0], raw[:, w, 2], ALU.add).then_inc(s_f02, 1)
                    dve.wait_ge(s_f02, n + 1)
                    outer = fsum[:, w, 0]
                reached(dve, s_fl, 4 * (n - 1))
                for e, op in enumerate((ALU.add, ALU.subtract)):
                    nc.vector.tensor_tensor(fsum[:, w, 1 + e], outer, raw[:, w, 1], op).then_inc(s_fpm, 1)
                for side, source, factor in ((0, raw[:, w, 0], 1.0), (1, raw[:, w, 2], 1.0), (2, fsum[:, w, 1], 0.5), (3, fsum[:, w, 2], 0.5)):
                    if side == 1 and last_triple:
                        continue
                    highs += 1
                    dve.wait_ge(s_fh, highs)
                    if side >= 2:
                        dve.wait_ge(s_fpm, 2 * n + side - 1)
                    nc.vector.scalar_tensor_tensor(w2_l[:, BASE[side] + q, k], source, factor, w2_h[:, BASE[side] + q, k].bitcast(F32),
                                                   ALU.mult, ALU.subtract).then_inc(s_fl, 2 if last_triple and side == 0 else 1)

            def sequence(g, n):
                s, k = n // 2, n % 2
                reached(dve, s_sl, 6 * g + n)
                even, odd = hp[:, k, 0], hp[:, k, 1]
                if s == 0:
                    nc.vector.tensor_tensor(seq[:, :, :, :], hp[:, k, :, :, 0:SW], hp[:, k, :, :, 1:HW], ALU.subtract).then_inc(s_seq, 1)
                else:
                    op = ALU.add if s == 1 else ALU.subtract
                    nc.vector.tensor_tensor(seq[:, 0], even[:, :, 1:HW], odd[:, :, 0:SW], op)
                    nc.vector.tensor_tensor(seq[:, 1], odd[:, :, 1:HW], even[:, :, 1:HW], op).then_inc(s_seq, 1)
                reached(dve, s_sh, 6 * g + n + 1)
                reached(dve, s_seq, 6 * g + n + 1)
                nc.vector.tensor_tensor(seq_l[:, s, k], seq[:, :, :, :], seq_h[:, s, k].bitcast(F32), ALU.subtract).then_inc(s_sl, 1)

            def x_low(g, h):
                reached(dve, s_xh, 2 * g + h + 1)
                nc.vector.tensor_tensor(xl[:, :, :], x[:, h], xh[:, :, :].bitcast(F32), ALU.subtract).then_inc(s_xl, 1)

            def add_product(gc, pos, mt, signs, done):
                reached(dve, s_c2, 8 * gc + 2 * pos + mt + 1)
                reached(dve, s_ev, 2 * gc + mt + 1)
                reached(dve, s_od, 2 * gc + mt + 1)
                if pos == 3:
                    reached(dve, s_m1, 4 * gc + 2 * mt + 2)
                bank = ps_c2[:, (2 * pos + mt) % 4].rearrange("p (b i) -> p b i", b=B)
                for parity, op in enumerate(signs):
                    nc.vector.tensor_tensor(acc[:, mt, parity], acc[:, mt, parity], bank, op).then_inc(done, 1)

            def step(i, u, live):
                gf, gc = i - 1, i - 2
                if live(2):
                    for n in (4, 5):
                        sequence(gc, n)
                if live(1):
                    x_low(gf, 1)
                    reached(dve, s_hp, 4 * gf + 4)
                    for n in (0, 1):
                        sequence(gf, n)
                if live(2):
                    for mt in range(KD):
                        add_product(gc, 2, mt, (ALU.add, ALU.add), s_m1)
                if live(1):
                    for n in (2, 3):
                        sequence(gf, n)
                if live(0):
                    x_low(i, 0)
                if live(2):
                    reached(dve, s_xr, 16 * gc + 16)
                    for mt in range(KD):
                        add_product(gc, 3, mt, (ALU.add, ALU.subtract), s_m2)
                        reached(dve, s_m2, 4 * gc + 2 * mt + 2)
                        reached(dve, s_out[mt], 16 * gc)
                        for parity in range(2):
                            nc.vector.scalar_tensor_tensor(
                                t[:, mt].rearrange("p (b i r) -> p r (b i)", b=B, r=2)[:, parity],
                                acc[:, mt, parity].rearrange("p b i -> p (b i)"), scale[:, 1, mt:mt + 1],
                                xr[:, mt].rearrange("p (b i r) -> p r (b i)", b=B, r=2)[:, parity],
                                ALU.mult, ALU.add).then_inc(s_t, 1)

            pipeline(dve, groups, 3, step)

        @block.tensor
        def _(pe):
            pe.wait_ge(s_fl, 4 * Q * KD)
            pe.wait_ge(s_w1l, 1)

            def products(out, terms):
                passes = [q for sh, sl, mh, ml in terms for q in ((sl, mh), (sh, ml), (sh, mh))]
                for n, (stationary, moving) in enumerate(passes):
                    last = nc.tensor.matmul(out, stationary, moving, start=(n == 0), stop=(n == len(passes) - 1))
                return last

            def conv1(g, h):
                reached(pe, s_xl, 2 * g + h + 1)
                reached(pe, s_hp, 2 * (2 * g + h))
                for mt in range(KD):
                    cols = slice(mt * P, mt * P + P)
                    products(ps_c1[:, mt], [(w1_h[:, k, cols], w1_l[:, k, cols], xh[:, k], xl[:, k]) for k in range(KD)]).then_inc(s_c1, 1)

            def conv2(g, pos):
                s, first, triples = PRODUCTS[pos]
                reached(pe, s_sl, 6 * g + 2 * s + 2)
                for mt in range(KD):
                    if pos == 0:
                        reached(pe, s_m1, 4 * g - 2 + 2 * mt)
                    elif pos == 1:
                        reached(pe, s_m2, 4 * g - 2 + 2 * mt)
                    else:
                        reached(pe, (s_ev, s_od)[pos - 2], 2 * g + mt + 1)
                    cols = slice(mt * P, mt * P + P)
                    terms = []
                    for q in range(triples):
                        for k in range(KD):
                            parity, at = (3 * q + first) % 2, (3 * q + first) // 2
                            terms.append((w2_h[:, BASE[pos] + q, k, cols], w2_l[:, BASE[pos] + q, k, cols],
                                          seq_h[:, s, k, parity, :, at:at + HALF], seq_l[:, s, k, parity, :, at:at + HALF]))
                    products(ps_c2[:, (2 * pos + mt) % 4].rearrange("p (b i) -> p b i", b=B), terms).then_inc(s_c2, 1)

            def step(i, u, live):
                if live(2):
                    conv2(i - 2, 0)
                if live(1):
                    conv1(i - 1, 0)
                if live(2):
                    conv2(i - 2, 1)
                if live(1):
                    conv1(i - 1, 1)
                if live(2):
                    conv2(i - 2, 2)
                    conv2(i - 2, 3)

            pipeline(pe, groups, 3, step)


def phase_c(nc, G, x1_t, xc_t, adj_t, w_ih, w_hh, w_msg, w_se, b_ih, b_hh, b_msg, b_se, form, y_n):
    B = 4
    T = B * P
    groups = G // B
    NS = w_se.shape[-1]
    with ExitStack() as ctx:
        def sb(name, shape, dt=F32):
            return ctx.enter_context(nc.sbuf_tensor("c_" + name, shape, dt))

        def sem(name):
            return ctx.enter_context(nc.semaphore("c_" + name))

        wi_h = sb("wi_h", [P, 2 * KD, 3 * D], F32R)
        wi_l = sb("wi_l", [P, 2 * KD, 3 * D], F32R)
        wh_h = sb("wh_h", [P, KD, 3 * D], F32R)
        wh_l = sb("wh_l", [P, KD, 3 * D], F32R)
        wm_h = sb("wm_h", [P, KD, D], F32R)
        wm_l = sb("wm_l", [P, KD, D], F32R)
        ws_h = sb("ws_h", [P, KD, NS], F32R)
        ws_l = sb("ws_l", [P, KD, NS], F32R)
        wi_raw = sb("wi_raw", [P, 2 * KD, 3 * D])
        wh_raw = sb("wh_raw", [P, KD, 3 * D])
        wm_raw = sb("wm_raw", [P, KD, D])
        ws_raw = sb("ws_raw", [P, KD, NS])
        bi = sb("bi", [P, 3, KD])
        bh = sb("bh", [P, 3, KD])
        brz = sb("brz", [P, 2, KD])
        bsum = sb("bsum", [P, 2, KD])
        bm_row = sb("bm_row", [P, 2, D])
        bs = sb("bs", [NS, 1])
        fm = sb("fm", [NS, 6])
        lin = sb("lin", [NS, 2])
        con = sb("con", [NS, 2])
        ident = sb("ident", [P, P])
        neg_half = sb("neg_half", [P, B])

        x1 = sb("x1", [P, 2, KD, T])
        xg = sb("xg", [P, 2, KD, T])
        xc = sb("xc", [P, 2, KD, T])
        at = sb("at", [P, 2, B, P])
        xh = sb("xh", [P, 2, KD, T], F32R)
        xl = sb("xl", [P, 2, KD, T], F32R)
        ch = sb("ch", [P, 2, KD, T], F32R)
        cl = sb("cl", [P, 2, KD, T], F32R)
        sq = sb("sq", [NS, T])
        left0 = sb("left0", [NS, T])
        right0 = sb("right0", [NS, T])
        left = sb("left", [NS, T])
        right = sb("right", [NS, T])
        mpre = sb("mpre", [P, B, D])
        mh = sb("mh", [P, B, D], F32R)
        ml = sb("ml", [P, B, D], F32R)
        ea = sb("ea", [P, B, P])
        aa = sb("aa", [P, B, P])
        ah = sb("ah", [P, B, P], F32R)
        al = sb("al", [P, B, P], F32R)
        nh = sb("nh", [P, 2, KD, T], F32R)
        nl = sb("nl", [P, 2, KD, T], F32R)
        tr = sb("tr", [P, T])
        rr = sb("rr", [P, T])
        hn = sb("hn", [P, T])
        npre = sb("npre", [P, T])
        nn = sb("nn", [P, T])
        tz = sb("tz", [P, T])
        zz = sb("zz", [P, T])
        dd = sb("dd", [P, T])
        zd = sb("zd", [P, T])
        nx = sb("nx", [P, T])
        yt = sb("yt", [P, KD, T])
        nmean = sb("nmean", [P, B])
        stats = sb("stats", [P, B, 6])
        mv = sb("mv", [P, B, 2])
        var_eps = sb("var_eps", [P, B])
        rstd = sb("rstd", [P, B])
        shift = sb("shift", [P, B])
        yo = sb("yo", [P, B, D])

        ps_g = ctx.enter_context(nc.psum_tensor("c_ps_g", [P, 3, T], F32))
        ps_s = ctx.enter_context(nc.psum_tensor("c_ps_s", [P, T], F32))
        ps_m = ctx.enter_context(nc.psum_tensor("c_ps_m", [P, 2, T], F32))
        ps_y = ctx.enter_context(nc.psum_tensor("c_ps_y", [P, B, D], F32))

        s_w = sem("weights_loaded")
        s_wh = sem("weights_high")
        s_wl = sem("weights_low")
        s_c = sem("constants")
        s_c1 = sem("constants_first_step")
        s_id0 = sem("identity_zeroed")
        s_id = sem("identity_ready")
        s_half = sem("half_ready")
        s_x = [sem("x1_loaded0"), sem("x1_loaded1")]
        s_at = [sem("adj_loaded0"), sem("adj_loaded1")]
        s_xg = [sem("x1_again_loaded0"), sem("x1_again_loaded1")]
        s_xc = [sem("xconv_loaded0"), sem("xconv_loaded1")]
        s_xh = sem("x1_high")
        s_xl = sem("x1_low")
        s_ch = sem("xconv_high")
        s_cl = sem("xconv_low")
        s_s = sem("similarity_products")
        s_sact = sem("similarity_rows_scaled")
        s_lr = sem("similarity_rows")
        s_m = sem("message_products")
        s_mpre = sem("message_biased")
        s_mh = sem("message_high")
        s_ml = sem("message_low")
        s_d = sem("distances")
        s_ea = sem("similarity_exp")
        s_aa = sem("similarity_masked")
        s_ah = sem("similarity_high")
        s_al = sem("similarity_low")
        s_nm = sem("messages_summed")
        s_nh = sem("message_sum_high")
        s_nl = sem("message_sum_low")
        s_gr = sem("gate_r_product")
        s_gh = sem("gate_hn_product")
        s_gi = sem("gate_in_product")
        s_gz = sem("gate_z_product")
        s_tr = sem("r_tanh")
        s_rr = sem("r_done")
        s_hn = sem("r_times_hn")
        s_np = sem("n_argument")
        s_nn = sem("n_done")
        s_tz = sem("z_tanh")
        s_zz = sem("z_done")
        s_dd = sem("x_minus_n")
        s_zd = sem("z_times_difference")
        s_nx = sem("n_plus_x")
        s_yt = sem("result_transposed_layout")
        s_y = sem("result_on_nodes")
        s_bn = sem("bn_stats_done")
        s_mv = sem("mean_var")
        s_ve = sem("var_eps_done")
        s_rstd = sem("rstd_done")
        s_nmean = sem("mean_negated")
        s_sh = sem("shift_done")
        s_yo = sem("output_ready")
        s_out = sem("output_stored")
        block = ctx.enter_context(nc.Block())

        def loaded(eng, sems, per_group, g, u):
            reached(eng, sems[u], (g + (2 - u)) * (8 * per_group))

        @block.sync
        def _(sp):
            for dst, src in ((wi_raw[:, :, :], w_ih), (wh_raw[:, :, :], w_hh), (wm_raw[:, :, :], w_msg), (ws_raw[:, :, :], w_se),
                             (bi[:, :, :], b_ih), (bh[:, :, :], b_hh), (bs[:, :], b_se), (fm[:, :], form),
                             (bm_row[:, 0, :], b_msg.partition_broadcast(P)), (bm_row[:, 1, :], b_msg.partition_broadcast(P))):
                sp.dma_start(dst, src).then_inc(s_w, 16)

            def step(i, u, live):
                if live(0):
                    g = i
                    reached(sp, s_xl, g - 1)
                    sp.dma_start(x1[:, u], x1_t[:, :, bass.ts(g, T)]).then_inc(s_x[u], 16)
                if live(1):
                    g, v = i - 1, 1 - u
                    reached(sp, s_aa, g - 1)
                    sp.dma_start(at[:, v], adj_t[:, bass.ts(g, T)].rearrange("p (b m) -> p b m", b=B)).then_inc(s_at[v], 16)
                    reached(sp, s_cl, g - 1)
                    sp.dma_start(xc[:, v], xc_t[:, :, bass.ts(g, T)]).then_inc(s_xc[v], 16)
                if live(2):
                    g = i - 2
                    reached(sp, s_nx, 2 * g - 2)
                    sp.dma_start(xg[:, u], x1_t[:, :, bass.ts(g, T)]).then_inc(s_xg[u], 16)
                if live(4):
                    g = i - 4
                    reached(sp, s_yo, B * g + B)
                    sp.dma_start(y_n[:, bass.ts(g, B * D)].rearrange("p (b d) -> p b d", b=B), yo[:, :, :]).then_inc(s_out, 16)

            pipeline(sp, groups, 5, step)
            sp.wait_ge(s_out, 16 * groups)

        R_BANK, HN_BANK, IN_BANK, Z_BANK = (0, 1), (1, 2), (2, 0), (0, 1)

        @block.scalar
        def _(act):
            act.wait_ge(s_w, 160)
            for hi, raw in ((wi_h, wi_raw), (wh_h, wh_raw), (wm_h, wm_raw), (ws_h, ws_raw)):
                nc.scalar.activation(hi[:, :, :], raw[:, :, :], ACT.Copy).then_inc(s_wh, 1)
            act.wait_ge(s_c, 2)

            def r_tanh(g, j):
                reached(act, s_gr, 2 * g + j + 1)
                reached(act, s_rr, 2 * g + j)
                nc.scalar.activation(tr[:, :], ps_g[:, R_BANK[j], :], ACT.Tanh, bias=brz[:, 0, j:j + 1], scale=0.5).then_inc(s_tr, 1)

            def n_tanh(g, j):
                reached(act, s_np, 2 * g + j + 1)
                reached(act, s_dd, 2 * g + j)
                reached(act, s_nx, 2 * g + j)
                nc.scalar.activation(nn[:, :], npre[:, :], ACT.Tanh).then_inc(s_nn, 1)

            def z_tanh(g, j):
                reached(act, s_gz, 2 * g + j + 1)
                reached(act, s_zz, 2 * g + j)
                nc.scalar.activation(tz[:, :], ps_g[:, Z_BANK[j], :], ACT.Tanh, bias=brz[:, 1, j:j + 1], scale=0.5).then_inc(s_tz, 1)

            def step(i, u, live):
                ga, v = i - 2, u
                gg = i - 3
                if live(3):
                    r_tanh(gg, 0)
                if live(2):
                    reached(act, s_s, ga + 1)
                    reached(act, s_lr, 2 * ga)
                    nc.scalar.activation(sq[:, :], ps_s[0:NS, :], ACT.Square, bias=bs[:, 0:1]).then_inc(s_sact, 1)
                    for side, part in ((0, left0), (1, right0)):
                        nc.scalar.activation(part[:, :], ps_s[0:NS, :], ACT.Identity, bias=con[:, side:side + 1],
                                             scale=fm[:, 3 * side + 1:3 * side + 2]).then_inc(s_sact, 1)
                    reached(act, s_mpre, 2 * ga + 2)
                    reached(act, s_nm, ga)
                    nc.scalar.activation(mh[:, :, :], mpre[:, :, :], ACT.Relu).then_inc(s_mh, 1)
                if live(3):
                    n_tanh(gg, 0)
                if live(4):
                    go = i - 4
                    reached(act, s_sh, go + 1)
                    reached(act, s_out, 16 * go)
                    for b in range(B):
                        nc.scalar.activation(yo[:, b], ps_y[:, b], ACT.Identity, bias=shift[:, b:b + 1],
                                             scale=rstd[:, b:b + 1]).then_inc(s_yo, 1)
                if live(3):
                    z_tanh(gg, 0)
                if live(2):
                    loaded(act, s_xc, 1, ga, v)
                    reached(act, s_gz, 2 * ga - 2)
                    nc.scalar.activation(ch[:, v], xc[:, v], ACT.Copy).then_inc(s_ch, 1)
                    reached(act, s_d, ga + 1)
                    reached(act, s_aa, ga)
                    nc.scalar.activation(ea[:, :, :], ps_s[:, :].rearrange("p (b m) -> p b m", b=B), ACT.Exp).then_inc(s_ea, 1)
                    reached(act, s_aa, ga + 1)
                    reached(act, s_nm, ga)
                    nc.scalar.activation(ah[:, :, :], aa[:, :, :], ACT.Copy).then_inc(s_ah, 1)
                if live(3):
                    r_tanh(gg, 1)
                if live(2):
                    reached(act, s_nm, ga + 1)
                    reached(act, s_gz, 2 * ga - 2)
                    nc.scalar.activation(nh[:, v], ps_m[:, :, :], ACT.Copy).then_inc(s_nh, 1)
                if live(3):
                    n_tanh(gg, 1)
                    z_tanh(gg, 1)
                if live(1):
                    g, w = i - 1, 1 - u
                    loaded(act, s_x, 1, g, w)
                    reached(act, s_gz, 2 * g - 2)
                    nc.scalar.activation(xh[:, w], x1[:, w], ACT.Copy).then_inc(s_xh, 1)

            pipeline(act, groups, 5, step)

        @block.gpsimd
        def _(pool):
            nc.gpsimd.memset(ident[:, :], 0.0).then_inc(s_id0, 1)
            nc.gpsimd.memset(neg_half[:, :], -0.5).then_inc(s_half, 1)
            pool.wait_ge(s_id0, 1)
            nc.gpsimd.affine_select(out=ident[:, :], in_=ident[:, :], compare_op=ALU.not_equal, fill=1.0,
                                    base=0, pattern=[[-1, P]], channel_multiplier=1).then_inc(s_id, 1)
            pool.wait_ge(s_half, 1)

            def with_x(g, v, j):
                reached(pool, s_nn, 2 * g + j + 1)
                reached(pool, s_zd, 2 * g + j)
                nc.gpsimd.tensor_tensor(dd[:, :], xg[:, v, j], nn[:, :], ALU.subtract).then_inc(s_dd, 1)
                reached(pool, s_yt, 2 * g + j)
                nc.gpsimd.tensor_tensor(nx[:, :], xg[:, v, j], nn[:, :], ALU.add).then_inc(s_nx, 1)

            def step(i, u, live):
                if live(4):
                    go = i - 4
                    reached(pool, s_ve, go + 1)
                    reached(pool, s_yo, B * go)
                    nc.gpsimd.tensor_tensor(rstd[:, :], var_eps[:, :], neg_half[:, :], ALU.pow).then_inc(s_rstd, 1)
                if live(3):
                    g, w = i - 3, 1 - u
                    loaded(pool, s_xg, 1, g, w)
                    with_x(g, w, 0)
                if live(2):
                    ga, v = i - 2, u
                    reached(pool, s_ch, ga + 1)
                    nc.gpsimd.tensor_tensor(cl[:, v], xc[:, v], ch[:, v].bitcast(F32), ALU.subtract).then_inc(s_cl, 1)
                if live(3):
                    with_x(g, w, 1)

            pipeline(pool, groups, 5, step)

        @block.vector
        def _(dve):
            dve.wait_ge(s_w, 160)
            nc.vector.tensor_tensor(bsum[:, :, :], bi[:, 0:2, :], bh[:, 0:2, :], ALU.add).then_inc(s_c1, 1)
            for side in range(2):
                nc.vector.tensor_tensor(lin[:, side:side + 1], fm[:, 3 * side + 1:3 * side + 2], bs[:, :], ALU.mult).then_inc(s_c1, 1)
            dve.wait_ge(s_c1, 3)
            nc.vector.tensor_scalar(brz[:, :, :], bsum[:, :, :], 0.5, None, ALU.mult).then_inc(s_c, 1)
            for side in range(2):
                last = nc.vector.tensor_tensor(con[:, side:side + 1], lin[:, side:side + 1], fm[:, 3 * side + 2:3 * side + 3], ALU.add)
            last.then_inc(s_c, 1)
            dve.wait_ge(s_wh, 4)
            for lo, hi, raw in ((wi_l, wi_h, wi_raw), (wh_l, wh_h, wh_raw), (wm_l, wm_h, wm_raw), (ws_l, ws_h, ws_raw)):
                nc.vector.tensor_tensor(lo[:, :, :], raw[:, :, :], hi[:, :, :].bitcast(F32), ALU.subtract).then_inc(s_wl, 1)

            def r_and_hn(g, j):
                n = 2 * g + j
                reached(dve, s_tr, n + 1)
                reached(dve, s_hn, n)
                nc.vector.tensor_scalar(rr[:, :], tr[:, :], 0.5, 0.5, ALU.mult, ALU.add).then_inc(s_rr, 1)
                reached(dve, s_gh, n + 1)
                reached(dve, s_np, n)
                reached(dve, s_rr, n + 1)
                nc.vector.scalar_tensor_tensor(hn[:, :], ps_g[:, HN_BANK[j], :], bh[:, 2, j:j + 1], rr[:, :],
                                               ALU.add, ALU.mult).then_inc(s_hn, 1)

            def n_argument(g, j):
                n = 2 * g + j
                reached(dve, s_gi, n + 1)
                reached(dve, s_hn, n + 1)
                reached(dve, s_nn, n)
                nc.vector.scalar_tensor_tensor(npre[:, :], ps_g[:, IN_BANK[j], :], bi[:, 2, j:j + 1], hn[:, :],
                                               ALU.add, ALU.add).then_inc(s_np, 1)

            def result(g, j):
                n = 2 * g + j
                reached(dve, s_tz, n + 1)
                reached(dve, s_zd, n)
                nc.vector.tensor_scalar(zz[:, :], tz[:, :], 0.5, 0.5, ALU.mult, ALU.add).then_inc(s_zz, 1)
                reached(dve, s_dd, n + 1)
                reached(dve, s_zz, n + 1)
                reached(dve, s_yt, n)
                nc.vector.tensor_tensor(zd[:, :], zz[:, :], dd[:, :], ALU.mult).then_inc(s_zd, 1)
                reached(dve, s_nx, n + 1)
                reached(dve, s_zd, n + 1)
                reached(dve, s_y, g)
                nc.vector.tensor_tensor(yt[:, j], zd[:, :], nx[:, :], ALU.add).then_inc(s_yt, 1)

            def step(i, u, live):
                ga, v = i - 2, u
                gg, go = i - 3, i - 4
                if live(3):
                    r_and_hn(gg, 0)
                if live(4):
                    reached(dve, s_sh, go)
                    reached(dve, s_y, go + 1)
                    for b in range(B):
                        last = nc.vector.bn_stats(stats[:, b], ps_y[:, b])
                    last.then_inc(s_bn, 1)
                    dve.wait_ge(s_w, 160)
                    reached(dve, s_bn, go + 1)
                    for b in range(B):
                        last = nc.vector.bn_aggr(mv[:, b], stats[:, b])
                    last.then_inc(s_mv, 1)
                    reached(dve, s_mv, go + 1)
                    nc.vector.tensor_scalar(var_eps[:, :], mv[:, :, 1], EPS, None, ALU.add).then_inc(s_ve, 1)
                    nc.vector.tensor_scalar(nmean[:, :], mv[:, :, 0], -1.0, None, ALU.mult).then_inc(s_nmean, 1)
                if live(2):
                    reached(dve, s_sact, 3 * ga + 3)
                    reached(dve, s_d, ga)
                    for side, (part, row) in enumerate(((left0, left), (right0, right))):
                        nc.vector.scalar_tensor_tensor(row[:, :], sq[:, :], fm[:, 3 * side:3 * side + 1], part[:, :],
                                                       ALU.mult, ALU.add).then_inc(s_lr, 1)
                    reached(dve, s_m, ga + 1)
                    reached(dve, s_ml, ga)
                    for h in range(2):
                        nc.vector.tensor_tensor(mpre[:, 2 * h:2 * h + 2], ps_m[:, h].rearrange("p (b d) -> p b d", b=2),
                                                bm_row[:, :, :], ALU.add).then_inc(s_mpre, 1)
                if live(4):
                    reached(dve, s_rstd, go + 1)
                    reached(dve, s_nmean, go + 1)
                    nc.vector.tensor_tensor(shift[:, :], nmean[:, :], rstd[:, :], ALU.mult).then_inc(s_sh, 1)
                if live(3):
                    n_argument(gg, 0)
                if live(2):
                    reached(dve, s_mh, ga + 1)
                    nc.vector.scalar_tensor_tensor(ml[:, :, :], mpre[:, :, :], 0.0, mh[:, :, :].bitcast(F32),
                                                   ALU.max, ALU.subtract).then_inc(s_ml, 1)
                if live(3):
                    result(gg, 0)
                if live(2):
                    reached(dve, s_ea, ga + 1)
                    loaded(dve, s_at, 1, ga, v)
                    reached(dve, s_al, ga)
                    nc.vector.tensor_tensor(aa[:, :, :], ea[:, :, :], at[:, v], ALU.mult).then_inc(s_aa, 1)
                    reached(dve, s_ah, ga + 1)
                    nc.vector.tensor_tensor(al[:, :, :], aa[:, :, :], ah[:, :, :].bitcast(F32), ALU.subtract).then_inc(s_al, 1)
                if live(3):
                    r_and_hn(gg, 1)
                if live(2):
                    reached(dve, s_nh, ga + 1)
                    nc.vector.tensor_tensor(nl[:, v], ps_m[:, :, :], nh[:, v].bitcast(F32), ALU.subtract).then_inc(s_nl, 1)
                if live(3):
                    n_argument(gg, 1)
                    result(gg, 1)
                if live(1):
                    g, w = i - 1, 1 - u
                    reached(dve, s_xh, g + 1)
                    nc.vector.tensor_tensor(xl[:, w], x1[:, w], xh[:, w].bitcast(F32), ALU.subtract).then_inc(s_xl, 1)

            pipeline(dve, groups, 5, step)

        @block.tensor
        def _(pe):
            pe.wait_ge(s_wl, 4)
            pe.wait_ge(s_id, 1)

            def products(out, terms):
                passes = [q for sh, sl, mh_, ml_ in terms for q in ((sl, mh_), (sh, ml_), (sh, mh_))]
                for n, (stationary, moving) in enumerate(passes):
                    last = nc.tensor.matmul(out, stationary, moving, start=(n == 0), stop=(n == len(passes) - 1))
                return last

            def gate(bank, v, which, j, own, inputs):
                cols = slice(which * D + j * P, which * D + j * P + P)
                terms = []
                if own:
                    terms += [(wh_h[:, k, cols], wh_l[:, k, cols], xh[:, v, k], xl[:, v, k]) for k in range(KD)]
                if inputs:
                    terms += [(wi_h[:, k, cols], wi_l[:, k, cols], ch[:, v, k], cl[:, v, k]) for k in range(KD)]
                    terms += [(wi_h[:, KD + k, cols], wi_l[:, KD + k, cols], nh[:, v, k], nl[:, v, k]) for k in range(KD)]
                return products(ps_g[:, bank, :], terms)

            def step(i, u, live):
                ga, v = i - 2, u
                g, w = i - 3, 1 - u
                if live(3):
                    reached(pe, s_nl, g + 1)
                    reached(pe, s_cl, g + 1)
                    reached(pe, s_np, 2 * g)
                    gate(R_BANK[0], w, 0, 0, True, True).then_inc(s_gr, 1)
                    reached(pe, s_tz, 2 * g)
                    gate(HN_BANK[0], w, 2, 0, True, False).then_inc(s_gh, 1)
                if live(4):
                    go = i - 4
                    reached(pe, s_yt, 2 * go + 2)
                    reached(pe, s_yo, B * go)
                    for b in range(B):
                        for j in range(KD):
                            last = nc.tensor.transpose(ps_y[:, b, j * P:j * P + P], yt[:, j, b * P:b * P + P], ident[:, :])
                    last.then_inc(s_y, 1)
                if live(2):
                    reached(pe, s_xl, ga + 1)
                    reached(pe, s_ea, ga)
                    products(ps_s[0:NS, :], [(ws_h[:, k, :], ws_l[:, k, :], xh[:, v, k], xl[:, v, k]) for k in range(KD)]).then_inc(s_s, 1)
                    reached(pe, s_nl, ga)
                    for b in range(B):
                        cols = slice(b * P, b * P + P)
                        last = products(ps_m[:, b // 2, b % 2 * D:b % 2 * D + D],
                                        [(xh[:, v, k, cols], xl[:, v, k, cols], wm_h[:, k, :], wm_l[:, k, :]) for k in range(KD)])
                    last.then_inc(s_m, 1)
                if live(3):
                    reached(pe, s_hn, 2 * g)
                    gate(IN_BANK[0], w, 2, 0, False, True).then_inc(s_gi, 1)
                    reached(pe, s_tr, 2 * g + 1)
                    gate(Z_BANK[0], w, 1, 0, True, True).then_inc(s_gz, 1)
                if live(2):
                    reached(pe, s_lr, 2 * ga + 2)
                    for b in range(B):
                        cols = slice(b * P, b * P + P)
                        last = nc.tensor.matmul(ps_s[:, cols], left[:, cols], right[:, cols], start=True, stop=True)
                    last.then_inc(s_d, 1)
                if live(3):
                    reached(pe, s_hn, 2 * g + 1)
                    gate(R_BANK[1], w, 0, 1, True, True).then_inc(s_gr, 1)
                    reached(pe, s_np, 2 * g + 1)
                    gate(HN_BANK[1], w, 2, 1, True, False).then_inc(s_gh, 1)
                if live(2):
                    reached(pe, s_al, ga + 1)
                    reached(pe, s_ml, ga + 1)
                    for j in range(KD):
                        for b in range(B):
                            last = products(ps_m[:, j, b * P:b * P + P],
                                            [(mh[:, b, j * P:j * P + P], ml[:, b, j * P:j * P + P], ah[:, b], al[:, b])])
                    last.then_inc(s_nm, 1)
                if live(3):
                    reached(pe, s_tz, 2 * g + 1)
                    gate(IN_BANK[1], w, 2, 1, False, True).then_inc(s_gi, 1)
                    reached(pe, s_tr, 2 * g + 2)
                    gate(Z_BANK[1], w, 1, 1, True, True).then_inc(s_gz, 1)

            pipeline(pe, groups, 5, step)


def similarity_rows():
    rows = np.zeros((9, 6), np.float32)
    rows[0:3, 1], rows[0:3, 4] = 1.0, 2.0
    rows[3:6, 2], rows[3:6, 3] = 1.0, -1.0
    rows[6:9, 0], rows[6:9, 5] = -1.0, 1.0
    return rows


def kernel(**inputs):
    from concourse import bacc
    from concourse.bass_utils import run_bass_kernel_spmd

    a = {name: np.asarray(v) for name, v in inputs.items()}
    x, adj = a["x"], a["adj"]
    G = x.shape[0]

    def tiles(w):
        return w.T.reshape(-1, P, w.shape[0]).transpose(1, 0, 2)

    def vector(b, parts):
        return b.reshape(parts, KD, P).transpose(2, 0, 1)

    def bn(layer):
        return vector(np.concatenate([a[f"L1_gnn_bn{layer}_{v}"] for v in "gbmv"]), 4)

    laid_out = {
        "x_n": x.transpose(1, 0, 2).reshape(P, G * D),
        "x_t": x.transpose(2, 0, 1).reshape(KD, P, G * P).transpose(1, 0, 2),
        "adj_n": adj.transpose(1, 0, 2).reshape(P, G * P),
        "adj_t": adj.transpose(2, 0, 1).reshape(P, G * P),
        "w0": np.concatenate([a["L0_gnn_theta"], a["L0_gnn_W_h"], a["L0_gnn_W_t"]], 1).reshape(KD, P, 3 * D).transpose(1, 0, 2),
        "b_t": a["L0_gnn_b_t"],
        "w_c1": tiles(a["L1_gnn_conv1_w"][:, :, 0]),
        "w_c2": a["L1_gnn_conv2_w"].transpose(1, 2, 0).reshape(KD, P, -1, D).transpose(1, 0, 2, 3),
        "bn1": bn(1),
        "bn2": bn(2),
        "w_ih": tiles(a["L1_gnn_w_ih"]),
        "w_hh": tiles(a["L1_gnn_w_hh"]),
        "w_msg": tiles(a["L1_gnn_w_msg"]),
        "w_se": tiles(np.concatenate([a["L1_gnn_w_se"]] * 3, 0)),
        "b_ih": vector(a["L1_gnn_b_ih"], 3),
        "b_hh": vector(a["L1_gnn_b_hh"], 3),
        "b_msg": a["L1_gnn_b_msg"],
        "b_se": np.concatenate([a["L1_gnn_b_se"]] * 3).reshape(-1, 1),
        "form": similarity_rows(),
    }
    nc = bacc.Bacc("TRN2", target_bir_lowering=False, num_devices=1)
    arrays, d = {}, {}
    for name, v in laid_out.items():
        arrays[f"in_{name}"] = np.ascontiguousarray(v)
        d[name] = nc.dram_tensor(f"in_{name}", v.shape, F32, kind="ExternalInput").ap()
    x1_t = nc.dram_tensor("x1_t", (P, KD, G * P), F32, kind="Internal").ap()
    xc_t = nc.dram_tensor("xc_t", (P, KD, G * P), F32, kind="Internal").ap()
    y_n = nc.dram_tensor("out_y", (P, G * D), F32, kind="ExternalOutput").ap()
    phase_a(nc, G, d["x_n"], d["x_t"], d["adj_n"], d["adj_t"], d["w0"], d["b_t"], x1_t)
    phase_b(nc, G, x1_t, d["w_c1"], d["w_c2"], d["bn1"], d["bn2"], xc_t)
    phase_c(nc, G, x1_t, xc_t, d["adj_t"], d["w_ih"], d["w_hh"], d["w_msg"], d["w_se"], d["b_ih"], d["b_hh"],
            d["b_msg"], d["b_se"], d["form"], y_n)
    r = run_bass_kernel_spmd(nc, [arrays], core_ids=[0])
    return r.results[0]["out_y"].reshape(P, G, D).transpose(1, 0, 2)
```

```python
from contextlib import ExitStack

import numpy as np

import concourse.bass as bass
from concourse import mybir

F32 = mybir.dt.float32
F32R = mybir.dt.float32r
ALU = mybir.AluOpType
ACT = mybir.ActivationFunctionType
AX_X = mybir.AxisListType.X

P = 128
D = 256
KD = D // P
EPS = 1e-5


def reached(eng, sem, count):
    if isinstance(count, int) and count <= 0:
        return
    eng.wait_ge(sem, count)


def pipeline(eng, units, stages, step):
    first = stages + stages % 2
    for i in range(first):
        step(i, i % 2, lambda s, i=i: 0 <= i - s < units)
    with eng.Fori(first // 2, units // 2) as two:
        step(two * 2, 0, lambda s: True)
        step(two * 2 + 1, 1, lambda s: True)
    for i in range(units, units + stages - 1):
        step(i, i % 2, lambda s, i=i: 0 <= i - s < units)


def phase_a(nc, G, x_n, x_t, adj_n, adj_t, w0, b_t, x1_t):
    pairs = G // 2
    with ExitStack() as ctx:
        def sb(name, shape, dt=F32):
            return ctx.enter_context(nc.sbuf_tensor("a_" + name, shape, dt))

        def sem(name):
            return ctx.enter_context(nc.semaphore("a_" + name))

        w_raw = sb("w_raw", [P, KD, 3 * D])
        w_hi = sb("w_hi", [P, KD, 3 * D], F32R)
        w_lo = sb("w_lo", [P, KD, 3 * D], F32R)
        bt_raw = sb("bt_raw", [2, 2 * D])
        bt_h = sb("bt_h", [2, 2 * D])
        bt_hr = sb("bt_hr", [2, 2 * D], F32R)
        bt_l = sb("bt_l", [2, 2 * D])
        bt_rows = sb("bt_rows", [2, 2 * D], F32R)
        ones0 = sb("ones0", [2, P])
        ones = sb("ones", [2, P], F32R)
        ident = sb("ident", [P, P])
        neg_half = sb("neg_half", [P, 2])
        xt = sb("xt", [P, 2, KD, 2 * P])
        an = sb("an", [P, 2, 2, P])
        at = sb("at", [P, 2, 2, P])
        xn = sb("xn", [P, 2, 2, D])
        xh = sb("xh", [P, 2, KD, 2 * P], F32R)
        xl = sb("xl", [P, 2, KD, 2 * P], F32R)
        ah = sb("ah", [P, 2, 2, P], F32R)
        al = sb("al", [P, 2, 2, P], F32R)
        fh = sb("fh", [P, 2, 2, D], F32R)
        fl = sb("fl", [P, 2, 2, D], F32R)
        deg = sb("deg", [P, 2])
        deg_eps = sb("deg_eps", [P, 2])
        norm = sb("norm", [P, 2, 2])
        het = sb("het", [P, 2, 2, D])
        gate = sb("gate", [P, 2, 2, D])
        diff = sb("diff", [P, 2, D])
        gd = sb("gd", [P, 2, D])
        mix = sb("mix", [P, 2, 2, D])
        below = sb("below", [P, 2, 2, D])
        ex = sb("ex", [P, 2, D])
        em1 = sb("em1", [P, 2, D])
        res = sb("res", [P, 2, 2, D])
        y = sb("y", [P, 2, 2, D])
        stats = sb("stats", [P, 2, 6])
        mv = sb("mv", [P, 2, 2, 2])
        var_eps = sb("var_eps", [P, 2])
        rstd = sb("rstd", [P, 2, 2])
        x1 = sb("x1", [P, 2, 2, D])
        x1t = sb("x1t", [P, 2, KD, 2 * P])

        ps_hh = ctx.enter_context(nc.psum_tensor("a_ps_hh", [P, 4, 2 * D], F32))
        ps_g = ctx.enter_context(nc.psum_tensor("a_ps_g", [P, 2, 2, D], F32))
        ps_hom = ctx.enter_context(nc.psum_tensor("a_ps_hom", [P, 2, D], F32))
        ps_t = ctx.enter_context(nc.psum_tensor("a_ps_t", [P, KD, 2 * P], F32))

        s_w = sem("weights_loaded")
        s_wh = sem("weights_high")
        s_wl = sem("weights_low")
        s_bt = sem("b_t_rows")
        s_on = sem("ones_ready")
        s_id0 = sem("identity_zeroed")
        s_id = sem("identity_ready")
        s_half = sem("half_ready")
        s_in = [sem("x_adj_loaded0"), sem("x_adj_loaded1")]
        s_at = [sem("adj_t_loaded0"), sem("adj_t_loaded1")]
        s_xn = [sem("x_nodes_loaded0"), sem("x_nodes_loaded1")]
        s_xh = sem("x_high")
        s_xl = sem("x_low")
        s_ah = sem("adj_high")
        s_al = sem("adj_low")
        s_deg = sem("degree")
        s_dege = sem("degree_eps")
        s_norm = sem("norm")
        s_proj = sem("projected")
        s_gp = sem("gate_projected")
        s_fh = sem("f_high")
        s_fl = sem("f_low")
        s_het = sem("het_copied")
        s_gate = sem("gate_ready")
        s_hom = sem("hom_done")
        s_diff = sem("diff_done")
        s_gd = sem("gated_diff")
        s_mix = sem("mixed")
        s_below = sem("mix_clamped")
        s_ex = sem("exp_done")
        s_em1 = sem("exp_minus_one")
        s_res = sem("residual_added")
        s_y = sem("y_done")
        s_bn = sem("bn_stats_done")
        s_mv = sem("mean_var")
        s_ve = sem("var_eps_done")
        s_rstd = sem("rstd_done")
        s_x1 = sem("x1_done")
        s_tr = sem("transposed")
        s_x1t = sem("x1t_copied")
        s_out = [sem("x1t_stored0"), sem("x1t_stored1")]
        block = ctx.enter_context(nc.Block())

        STAGES = 8

        @block.sync
        def _(sp):
            sp.dma_start(w_raw[:, :, :], w0).then_inc(s_w, 16)
            for b in range(2):
                sp.dma_start(bt_raw[:, b * D:b * D + D], b_t.partition_broadcast(2)).then_inc(s_w, 16)

            def step(i, u, live):
                v = 1 - u
                if live(0):
                    p = i
                    reached(sp, s_xl, p - 1)
                    reached(sp, s_deg, p - 1)
                    sp.dma_start(xt[:, u], x_t[:, :, bass.ts(p, 2 * P)]).then_inc(s_in[u], 16)
                    sp.dma_start(an[:, u], adj_n[:, bass.ts(p, 2 * P)].rearrange("p (b m) -> p b m", b=2)).then_inc(s_in[u], 16)
                if live(1):
                    p = i - 1
                    reached(sp, s_al, p - 1)
                    sp.dma_start(at[:, v], adj_t[:, bass.ts(p, 2 * P)].rearrange("p (b m) -> p b m", b=2)).then_inc(s_at[v], 16)
                if live(3):
                    p = i - 3
                    reached(sp, s_res, p - 1)
                    sp.dma_start(xn[:, v], x_n[:, bass.ts(p, 2 * D)].rearrange("p (b d) -> p b d", b=2)).then_inc(s_xn[v], 16)
                if live(7):
                    p = i - 7
                    reached(sp, s_x1t, p + 1)
                    sp.dma_start(x1_t[:, :, bass.ts(p, 2 * P)], x1t[:, v]).then_inc(s_out[v], 16)

            pipeline(sp, pairs, STAGES, step)
            for u in range(2):
                sp.wait_ge(s_out[u], 16 * (pairs // 2))

        def loaded(eng, sems, per_pair, p, u):
            reached(eng, sems[u], (p + (2 - u)) * (8 * per_pair))

        @block.scalar
        def _(act):
            act.wait_ge(s_w, 48)
            nc.scalar.activation(w_hi[:, :, :], w_raw[:, :, :], ACT.Copy).then_inc(s_wh, 1)
            nc.scalar.activation(bt_hr[:, :], bt_raw[:, :], ACT.Copy).then_inc(s_wh, 1)
            act.wait_ge(s_on, 1)
            nc.scalar.activation(ones[:, :], ones0[:, :], ACT.Copy).then_inc(s_wh, 1)

            def step(i, u, live):
                v = 1 - u
                if live(4):
                    p = i - 4
                    reached(act, s_below, p + 1)
                    reached(act, s_em1, p)
                    nc.scalar.activation(ex[:, :, :], below[:, u], ACT.Exp).then_inc(s_ex, 1)
                if live(1):
                    p = i - 1
                    loaded(act, s_in, 2, p, v)
                    reached(act, s_gp, p - 1)
                    nc.scalar.activation(xh[:, v], xt[:, v], ACT.Copy).then_inc(s_xh, 1)
                if live(4):
                    p = i - 4
                    reached(act, s_ex, p + 1)
                    reached(act, s_res, p)
                    nc.scalar.activation(em1[:, :, :], ex[:, :, :], ACT.Copy, bias=-1.0).then_inc(s_em1, 1)
                if live(2):
                    p = i - 2
                    loaded(act, s_at, 1, p, u)
                    reached(act, s_hom, p - 1)
                    nc.scalar.activation(ah[:, u], at[:, u], ACT.Copy).then_inc(s_ah, 1)
                    reached(act, s_norm, p + 1)
                    for b in range(2):
                        reached(act, s_proj, 2 * p + b + 1)
                        nc.scalar.activation(fh[:, u, b], ps_hh[:, 2 * u + b, 0:D], ACT.Copy, scale=norm[:, u, b:b + 1]).then_inc(s_fh, 1)
                    reached(act, s_mix, p - 1)
                    nc.scalar.activation(het[:, u], ps_hh[:, 2 * u:2 * u + 2, D:2 * D], ACT.Copy).then_inc(s_het, 1)
                    reached(act, s_gp, p + 1)
                    reached(act, s_gd, p - 1)
                    nc.scalar.activation(gate[:, u], ps_g[:, u], ACT.Tanh, scale=0.5).then_inc(s_gate, 1)
                if live(7):
                    p = i - 7
                    reached(act, s_tr, p + 1)
                    reached(act, s_out[v], (p - v) * 8)
                    nc.scalar.activation(x1t[:, v], ps_t[:, :, :], ACT.Copy).then_inc(s_x1t, 1)

            pipeline(act, pairs, STAGES, step)

        @block.gpsimd
        def _(pool):
            nc.gpsimd.memset(ones0[:, :], 1.0).then_inc(s_on, 1)
            nc.gpsimd.memset(ident[:, :], 0.0).then_inc(s_id0, 1)
            nc.gpsimd.memset(neg_half[:, :], -0.5).then_inc(s_half, 1)
            pool.wait_ge(s_id0, 1)
            nc.gpsimd.affine_select(out=ident[:, :], in_=ident[:, :], compare_op=ALU.not_equal, fill=1.0,
                                    base=0, pattern=[[-1, P]], channel_multiplier=1).then_inc(s_id, 1)
            pool.wait_ge(s_half, 1)

            def step(i, u, live):
                v = 1 - u
                if live(1):
                    p = i - 1
                    reached(pool, s_xh, p + 1)
                    reached(pool, s_gp, p - 1)
                    nc.gpsimd.tensor_tensor(xl[:, v], xt[:, v], xh[:, v].bitcast(F32), ALU.subtract).then_inc(s_xl, 1)
                if live(4):
                    p = i - 4
                    loaded(pool, s_xn, 1, p, u)
                    reached(pool, s_em1, p + 1)
                    reached(pool, s_y, p - 1)
                    nc.gpsimd.tensor_tensor(res[:, u], em1[:, :, :], xn[:, u], ALU.add).then_inc(s_res, 1)
                if live(2):
                    p = i - 2
                    reached(pool, s_ah, p + 1)
                    reached(pool, s_hom, p - 1)
                    nc.gpsimd.tensor_tensor(al[:, u], at[:, u], ah[:, u].bitcast(F32), ALU.subtract).then_inc(s_al, 1)
                if live(5):
                    p = i - 5
                    reached(pool, s_ve, p + 1)
                    reached(pool, s_x1, p - 1)
                    nc.gpsimd.tensor_tensor(rstd[:, v], var_eps[:, :], neg_half[:, :], ALU.pow).then_inc(s_rstd, 1)
                if live(1):
                    p = i - 1
                    reached(pool, s_dege, p + 1)
                    reached(pool, s_diff, p - 1)
                    reached(pool, s_fl, p - 1)
                    nc.gpsimd.tensor_tensor(norm[:, v], deg_eps[:, :], neg_half[:, :], ALU.pow).then_inc(s_norm, 1)

            pipeline(pool, pairs, STAGES, step)

        @block.vector
        def _(dve):
            dve.wait_ge(s_wh, 3)
            nc.vector.tensor_tensor(w_lo[:, :, :], w_raw[:, :, :], w_hi[:, :, :].bitcast(F32), ALU.subtract).then_inc(s_wl, 1)
            nc.vector.tensor_tensor(bt_l[:, :], bt_raw[:, :], bt_hr[:, :].bitcast(F32), ALU.subtract).then_inc(s_bt, 1)
            dve.wait_ge(s_id, 1)
            nc.vector.tensor_scalar(bt_h[:, :], bt_hr[:, :].bitcast(F32), ident[0:2, 0:1], None, ALU.mult).then_inc(s_bt, 1)
            dve.wait_ge(s_bt, 2)
            nc.vector.scalar_tensor_tensor(bt_rows[:, :], bt_l[:, :], ident[0:2, 1:2], bt_h[:, :], ALU.mult, ALU.add).then_inc(s_bt, 1)

            def step(i, u, live):
                v = 1 - u
                p1, p2, p3, p5, p6 = i - 1, i - 2, i - 3, i - 5, i - 6
                if live(5):
                    reached(dve, s_x1, p5 - 1)
                    reached(dve, s_res, p5 + 1)
                    nc.vector.scalar_tensor_tensor(y[:, v], mix[:, v], 0.0, res[:, v], ALU.max, ALU.add).then_inc(s_y, 1)
                if live(3):
                    reached(dve, s_gd, p3)
                    reached(dve, s_hom, p3 + 1)
                    reached(dve, s_het, p3 + 1)
                    for b in range(2):
                        last = nc.vector.scalar_tensor_tensor(diff[:, b], ps_hom[:, b], norm[:, v, b:b + 1], het[:, v, b],
                                                              ALU.mult, ALU.subtract)
                    last.then_inc(s_diff, 1)
                if live(5):
                    reached(dve, s_mv, p5)
                    reached(dve, s_y, p5 + 1)
                    for b in range(2):
                        last = nc.vector.bn_stats(stats[:, b], y[:, v, b])
                    last.then_inc(s_bn, 1)
                if live(3):
                    reached(dve, s_mix, p3)
                    reached(dve, s_gate, p3 + 1)
                    reached(dve, s_diff, p3 + 1)
                    nc.vector.scalar_tensor_tensor(gd[:, :, :], gate[:, v], 1.0, diff[:, :, :], ALU.add, ALU.mult).then_inc(s_gd, 1)
                if live(5):
                    dve.wait_ge(s_wh, 3)
                    reached(dve, s_bn, p5 + 1)
                    for b in range(2):
                        last = nc.vector.bn_aggr(mv[:, v, b], stats[:, b])
                    last.then_inc(s_mv, 1)
                if live(3):
                    reached(dve, s_y, p3 - 1)
                    reached(dve, s_gd, p3 + 1)
                    nc.vector.scalar_tensor_tensor(mix[:, v], gd[:, :, :], 0.5, het[:, v], ALU.mult, ALU.add).then_inc(s_mix, 1)
                if live(5):
                    reached(dve, s_mv, p5 + 1)
                    reached(dve, s_rstd, p5)
                    nc.vector.tensor_scalar(var_eps[:, :], mv[:, v, :, 1], EPS, None, ALU.add).then_inc(s_ve, 1)
                if live(1):
                    loaded(dve, s_in, 2, p1, v)
                    reached(dve, s_dege, p1)
                    nc.vector.tensor_reduce(deg[:, :], an[:, v], AX_X, ALU.add).then_inc(s_deg, 1)
                if live(3):
                    reached(dve, s_mix, p3 + 1)
                    reached(dve, s_ex, p3 - 1)
                    nc.vector.tensor_scalar(below[:, v], mix[:, v], 0.0, None, ALU.min).then_inc(s_below, 1)
                if live(1):
                    reached(dve, s_deg, p1 + 1)
                    reached(dve, s_norm, p1)
                    nc.vector.tensor_scalar(deg_eps[:, :], deg[:, :], 1e-6, None, ALU.add).then_inc(s_dege, 1)
                if live(6):
                    reached(dve, s_rstd, p6 + 1)
                    reached(dve, s_tr, p6 - 1)
                    for b in range(2):
                        last = nc.vector.tensor_scalar(x1[:, u, b], y[:, u, b], mv[:, u, b, 0:1], rstd[:, u, b:b + 1],
                                                       ALU.subtract, ALU.mult)
                    last.then_inc(s_x1, 1)
                if live(2):
                    reached(dve, s_het, p2 + 1)
                    reached(dve, s_hom, p2 - 1)
                    for b in range(2):
                        last = nc.vector.scalar_tensor_tensor(fl[:, u, b], ps_hh[:, 2 * u + b, 0:D], norm[:, u, b:b + 1],
                                                              fh[:, u, b].bitcast(F32), ALU.mult, ALU.subtract)
                    last.then_inc(s_fl, 1)

            pipeline(dve, pairs, STAGES, step)

        @block.tensor
        def _(pe):
            pe.wait_ge(s_wl, 1)
            pe.wait_ge(s_bt, 3)

            def step(i, u, live):
                v = 1 - u
                if live(7):
                    p = i - 7
                    reached(pe, s_x1, p + 1)
                    reached(pe, s_x1t, p)
                    for b in range(2):
                        for k in range(KD):
                            last = nc.tensor.transpose(ps_t[:, k, b * P:b * P + P], x1[:, v, b, k * P:k * P + P], ident[:, :])
                    last.then_inc(s_tr, 1)
                if live(3):
                    p = i - 3
                    reached(pe, s_fl, p + 1)
                    reached(pe, s_al, p + 1)
                    reached(pe, s_diff, p)
                    for b in range(2):
                        for n, (aa, ff) in enumerate(((al, fh), (ah, fl), (ah, fh))):
                            last = nc.tensor.matmul(ps_hom[:, b], aa[:, v, b], ff[:, v, b], start=(n == 0), stop=(n == 2))
                    last.then_inc(s_hom, 1)
                if live(2):
                    p = i - 2
                    reached(pe, s_xl, p + 1)
                    reached(pe, s_fl, p - 1)
                    reached(pe, s_gate, p - 1)
                    terms = [(xx, ww, k) for k in range(KD) for xx, ww in ((xl, w_hi), (xh, w_lo), (xh, w_hi))]
                    for b in range(2):
                        for n, (xx, ww, k) in enumerate(terms):
                            last = nc.tensor.matmul(ps_hh[:, 2 * u + b, :], xx[:, u, k, b * P:b * P + P], ww[:, k, 0:2 * D],
                                                    start=(n == 0), stop=(n == len(terms) - 1))
                        last.then_inc(s_proj, 1)
                    nc.tensor.matmul(ps_g[:, u], ones[:, :], bt_rows[:, :].rearrange("p (b d) -> p b d", b=2), start=True, stop=False)
                    for b in range(2):
                        for n, (xx, ww, k) in enumerate(terms):
                            last = nc.tensor.matmul(ps_g[:, u, b], xx[:, u, k, b * P:b * P + P], ww[:, k, 2 * D:3 * D],
                                                    start=False, stop=(b == 1 and n == len(terms) - 1))
                    last.then_inc(s_gp, 1)

            pipeline(pe, pairs, STAGES, step)


def phase_b(nc, G, x1_t, w_c1, w_c2, bn1, bn2, xc_t):
    B = 8
    HB = B // 2
    T, HT = B * P, HB * P
    groups = G // B
    TAPS = w_c2.shape[2]
    PAD = (TAPS - 1) // 2
    Q = (TAPS + 2) // 3
    HALF = P // 2
    HW = HALF + PAD
    SW = HW - 1
    EDGE = PAD // 2
    assert TAPS == 3 * Q - 1 and PAD % 2 == 0
    PRODUCTS = ((0, 0, Q), (0, 1, Q - 1), (1, 0, Q), (2, 0, Q))
    BASE = (0, Q, 2 * Q - 1, 3 * Q - 1)
    NW = 4 * Q - 1
    NSEQ = 3
    with ExitStack() as ctx:
        def sb(name, shape, dt=F32):
            return ctx.enter_context(nc.sbuf_tensor("b_" + name, shape, dt))

        def sem(name):
            return ctx.enter_context(nc.semaphore("b_" + name))

        w2_h = sb("w2_h", [P, NW, KD, D], F32R)
        w2_l = sb("w2_l", [P, NW, KD, D], F32R)
        w1_h = sb("w1_h", [P, KD, D], F32R)
        w1_l = sb("w1_l", [P, KD, D], F32R)
        seq_h = sb("seq_h", [P, NSEQ, KD, 2, B, SW], F32R)
        seq_l = sb("seq_l", [P, NSEQ, KD, 2, B, SW], F32R)
        hp = sb("hp", [P, KD, 2, B, HW])
        seq = sb("seq", [P, 2, B, SW])
        x = sb("x", [P, 2, KD, HT])
        xh = sb("xh", [P, KD, HT], F32R)
        xl = sb("xl", [P, KD, HT], F32R)
        acc = sb("acc", [P, KD, 2, B, HALF])
        t = sb("t", [P, KD, T])
        xr = sb("xr", [P, KD, T])
        raw = xr[:, :, :].rearrange("p u (z o) -> p u z o", o=D)
        fsum = t[:, :, :].rearrange("p u (z o) -> p u z o", o=D)
        bn = sb("bn", [P, 2, 4, KD])
        ve = sb("ve", [P, 2, KD])
        rs = sb("rs", [P, 2, KD])
        scale = sb("scale", [P, 2, KD])
        mscale = sb("mscale", [P, 2, KD])
        shift = sb("shift", [P, 2, KD])
        neg_half = sb("neg_half", [P, 2, KD])

        ps_c1 = ctx.enter_context(nc.psum_tensor("b_ps_c1", [P, KD, HT], F32))
        ps_c2 = ctx.enter_context(nc.psum_tensor("b_ps_c2", [P, 4, B * HALF], F32))

        s_w1 = sem("conv1_weights_loaded")
        s_bnl = sem("bn_loaded")
        s_raw = [sem("taps_loaded0"), sem("taps_loaded1")]
        s_half = sem("half_ready")
        s_pad = sem("padding_zeroed")
        s_c = sem("bn_steps")
        s_rs = sem("bn_rsqrt")
        s_w1h = sem("conv1_weights_high")
        s_w1l = sem("conv1_weights_low")
        s_f02 = sem("taps_0_2_summed")
        s_fpm = sem("filter_sums")
        s_fh = sem("filter_high")
        s_fl = sem("filter_low")
        s_x = [sem("x1_half0_loaded"), sem("x1_half1_loaded")]
        s_xh = sem("x1_high")
        s_xl = sem("x1_low")
        s_c1 = sem("conv1_done")
        s_hp = sem("conv1_activated")
        s_seq = sem("sequence_made")
        s_sh = sem("sequence_high")
        s_sl = sem("sequence_low")
        s_c2 = sem("conv2_product_done")
        s_ev = sem("even_started")
        s_od = sem("odd_started")
        s_m1 = sem("m1_added")
        s_m2 = sem("m2_added")
        s_xr = sem("residual_loaded")
        s_t = sem("residual_added")
        s_xc = sem("xconv_ready")
        s_out = [sem("xconv_stored0"), sem("xconv_stored1")]
        block = ctx.enter_context(nc.Block())

        SEQ_FREE = (4, 6, 8)

        @block.sync
        def _(sp):
            sp.dma_start(x[:, 0, :, 0:D], w_c1).then_inc(s_w1, 16)
            for n, vectors in enumerate((bn1, bn2)):
                sp.dma_start(bn[:, n], vectors).then_inc(s_bnl, 16)
            for n in range(Q * KD):
                q, k = n // KD, n % KD
                taps = min(3, TAPS - 3 * q)
                reached(sp, s_fl, 4 * (n - 1))
                sp.dma_start(raw[:, n % 2, 0:taps, :], w_c2[:, k, 3 * q:3 * q + taps, :]).then_inc(s_raw[n % 2], 16)
            sp.wait_ge(s_fl, 4 * Q * KD)
            sp.wait_ge(s_w1l, 1)

            def step(i, u, live):
                if live(0):
                    g = i
                    reached(sp, s_xl, 2 * g - 1)
                    sp.dma_start(x[:, 0], x1_t[:, :, bass.ds(g * T, HT)]).then_inc(s_x[0], 16)
                if live(2):
                    g = i - 2
                    reached(sp, s_t, 4 * g)
                    sp.dma_start(xr[:, :, :], x1_t[:, :, bass.ts(g, T)]).then_inc(s_xr, 16)
                if live(0):
                    g = i
                    reached(sp, s_xl, 2 * g)
                    sp.dma_start(x[:, 1], x1_t[:, :, bass.ds(g * T + HT, HT)]).then_inc(s_x[1], 16)
                if live(2):
                    g = i - 2
                    for mt in range(KD):
                        reached(sp, s_xc, 2 * g + mt + 1)
                        sp.dma_start(xc_t[:, mt, bass.ts(g, T)], t[:, mt]).then_inc(s_out[mt], 16)

            pipeline(sp, groups, 3, step)
            for mt in range(KD):
                sp.wait_ge(s_out[mt], 16 * groups)

        @block.scalar
        def _(act):
            act.wait_ge(s_w1, 16)
            nc.scalar.activation(w1_h[:, :, :], x[:, 0, :, 0:D], ACT.Copy).then_inc(s_w1h, 1)
            for n in range(Q * KD):
                q, k, w = n // KD, n % KD, n % 2
                act.wait_ge(s_raw[w], 16 * (n // 2 + 1))
                nc.scalar.activation(w2_h[:, BASE[0] + q, k], raw[:, w, 0], ACT.Copy).then_inc(s_fh, 1)
                if q < Q - 1:
                    nc.scalar.activation(w2_h[:, BASE[1] + q, k], raw[:, w, 2], ACT.Copy).then_inc(s_fh, 1)
                for e in range(2):
                    reached(act, s_fpm, 2 * n + e + 1)
                    nc.scalar.activation(w2_h[:, BASE[2 + e] + q, k], fsum[:, w, 1 + e], ACT.Copy, scale=0.5).then_inc(s_fh, 1)
            act.wait_ge(s_c, 5)
            act.wait_ge(s_pad, 1)

            def high(g, n):
                s, k = n // 2, n % 2
                reached(act, s_seq, 6 * g + n + 1)
                reached(act, s_c2, 8 * g - 8 + SEQ_FREE[s])
                nc.scalar.activation(seq_h[:, s, k], seq[:, :, :, :], ACT.Copy).then_inc(s_sh, 1)

            def split_x(g, h):
                reached(act, s_x[h], 16 * g + 16)
                reached(act, s_c1, 2 * (2 * g + h))
                nc.scalar.activation(xh[:, :, :], x[:, h], ACT.Copy).then_inc(s_xh, 1)

            def conv1_out(g, h):
                for mt in range(KD):
                    reached(act, s_c1, 2 * (2 * g + h) + mt + 1)
                    reached(act, s_seq, 6 * g)
                    nc.scalar.activation(hp[:, mt, :, h * HB:h * HB + HB, EDGE:EDGE + HALF],
                                         ps_c1[:, mt].rearrange("p (b i r) -> p r b i", b=HB, r=2), ACT.Relu,
                                         bias=shift[:, 0, mt:mt + 1], scale=scale[:, 0, mt:mt + 1]).then_inc(s_hp, 1)

            def step(i, u, live):
                gf, gc = i - 1, i - 2
                if live(2):
                    for n in (4, 5):
                        high(gc, n)
                    for mt in range(KD):
                        reached(act, s_c2, 8 * gc + mt + 1)
                        reached(act, s_t, 4 * gc - 2 + 2 * mt)
                        nc.scalar.activation(acc[:, mt, 0], ps_c2[:, mt].rearrange("p (b i) -> p b i", b=B), ACT.Copy).then_inc(s_ev, 1)
                if live(1):
                    conv1_out(gf, 0)
                    split_x(gf, 1)
                if live(2):
                    for mt in range(KD):
                        reached(act, s_c2, 8 * gc + 2 + mt + 1)
                        nc.scalar.activation(acc[:, mt, 1], ps_c2[:, 2 + mt].rearrange("p (b i) -> p b i", b=B), ACT.Copy,
                                             scale=-1.0).then_inc(s_od, 1)
                if live(1):
                    conv1_out(gf, 1)
                if live(0):
                    split_x(i, 0)
                if live(1):
                    for n in range(4):
                        high(gf, n)
                if live(2):
                    for mt in range(KD):
                        reached(act, s_t, 4 * gc + 2 * mt + 2)
                        nc.scalar.activation(t[:, mt], t[:, mt], ACT.Relu, bias=shift[:, 1, mt:mt + 1]).then_inc(s_xc, 1)

            pipeline(act, groups, 3, step)

        @block.gpsimd
        def _(pool):
            nc.gpsimd.memset(neg_half[:, :, :], -0.5).then_inc(s_half, 1)
            nc.gpsimd.memset(hp[:, :, :, :, :], 0.0).then_inc(s_pad, 1)
            pool.wait_ge(s_half, 1)
            pool.wait_ge(s_c, 1)
            nc.gpsimd.tensor_tensor(rs[:, :, :], ve[:, :, :], neg_half[:, :, :], ALU.pow).then_inc(s_rs, 1)

        @block.vector
        def _(dve):
            dve.wait_ge(s_bnl, 32)
            nc.vector.tensor_scalar(ve[:, :, :], bn[:, :, 3], EPS, None, ALU.add).then_inc(s_c, 1)
            dve.wait_ge(s_rs, 1)
            nc.vector.tensor_tensor(scale[:, :, :], bn[:, :, 0], rs[:, :, :], ALU.mult).then_inc(s_c, 1)
            dve.wait_ge(s_c, 2)
            nc.vector.tensor_tensor(mscale[:, :, :], bn[:, :, 2], scale[:, :, :], ALU.mult).then_inc(s_c, 1)
            dve.wait_ge(s_c, 3)
            nc.vector.tensor_tensor(shift[:, :, :], bn[:, :, 1], mscale[:, :, :], ALU.subtract).then_inc(s_c, 2)
            dve.wait_ge(s_w1h, 1)
            nc.vector.tensor_tensor(w1_l[:, :, :], x[:, 0, :, 0:D], w1_h[:, :, :].bitcast(F32), ALU.subtract).then_inc(s_w1l, 1)
            highs = 0
            for n in range(Q * KD):
                q, k, w = n // KD, n % KD, n % 2
                last_triple = q == Q - 1
                dve.wait_ge(s_raw[w], 16 * (n // 2 + 1))
                outer = raw[:, w, 0]
                if not last_triple:
                    reached(dve, s_fpm, 2 * n)
                    nc.vector.tensor_tensor(fsum[:, w, 0], raw[:, w, 0], raw[:, w, 2], ALU.add).then_inc(s_f02, 1)
                    dve.wait_ge(s_f02, n + 1)
                    outer = fsum[:, w, 0]
                reached(dve, s_fl, 4 * (n - 1))
                for e, op in enumerate((ALU.add, ALU.subtract)):
                    nc.vector.tensor_tensor(fsum[:, w, 1 + e], outer, raw[:, w, 1], op).then_inc(s_fpm, 1)
                for side, source, factor in ((0, raw[:, w, 0], 1.0), (1, raw[:, w, 2], 1.0), (2, fsum[:, w, 1], 0.5), (3, fsum[:, w, 2], 0.5)):
                    if side == 1 and last_triple:
                        continue
                    highs += 1
                    dve.wait_ge(s_fh, highs)
                    if side >= 2:
                        dve.wait_ge(s_fpm, 2 * n + side - 1)
                    nc.vector.scalar_tensor_tensor(w2_l[:, BASE[side] + q, k], source, factor, w2_h[:, BASE[side] + q, k].bitcast(F32),
                                                   ALU.mult, ALU.subtract).then_inc(s_fl, 2 if last_triple and side == 0 else 1)

            def sequence(g, n):
                s, k = n // 2, n % 2
                reached(dve, s_sl, 6 * g + n)
                even, odd = hp[:, k, 0], hp[:, k, 1]
                if s == 0:
                    nc.vector.tensor_tensor(seq[:, :, :, :], hp[:, k, :, :, 0:SW], hp[:, k, :, :, 1:HW], ALU.subtract).then_inc(s_seq, 1)
                else:
                    op = ALU.add if s == 1 else ALU.subtract
                    nc.vector.tensor_tensor(seq[:, 0], even[:, :, 1:HW], odd[:, :, 0:SW], op)
                    nc.vector.tensor_tensor(seq[:, 1], odd[:, :, 1:HW], even[:, :, 1:HW], op).then_inc(s_seq, 1)
                reached(dve, s_sh, 6 * g + n + 1)
                reached(dve, s_seq, 6 * g + n + 1)
                nc.vector.tensor_tensor(seq_l[:, s, k], seq[:, :, :, :], seq_h[:, s, k].bitcast(F32), ALU.subtract).then_inc(s_sl, 1)

            def x_low(g, h):
                reached(dve, s_xh, 2 * g + h + 1)
                nc.vector.tensor_tensor(xl[:, :, :], x[:, h], xh[:, :, :].bitcast(F32), ALU.subtract).then_inc(s_xl, 1)

            def add_product(gc, pos, mt, signs, done):
                reached(dve, s_c2, 8 * gc + 2 * pos + mt + 1)
                reached(dve, s_ev, 2 * gc + mt + 1)
                reached(dve, s_od, 2 * gc + mt + 1)
                if pos == 3:
                    reached(dve, s_m1, 4 * gc + 2 * mt + 2)
                bank = ps_c2[:, (2 * pos + mt) % 4].rearrange("p (b i) -> p b i", b=B)
                for parity, op in enumerate(signs):
                    nc.vector.tensor_tensor(acc[:, mt, parity], acc[:, mt, parity], bank, op).then_inc(done, 1)

            def step(i, u, live):
                gf, gc = i - 1, i - 2
                if live(2):
                    for n in (4, 5):
                        sequence(gc, n)
                if live(1):
                    x_low(gf, 1)
                    reached(dve, s_hp, 4 * gf + 4)
                    for n in (0, 1):
                        sequence(gf, n)
                if live(2):
                    for mt in range(KD):
                        add_product(gc, 2, mt, (ALU.add, ALU.add), s_m1)
                if live(1):
                    for n in (2, 3):
                        sequence(gf, n)
                if live(0):
                    x_low(i, 0)
                if live(2):
                    reached(dve, s_xr, 16 * gc + 16)
                    for mt in range(KD):
                        add_product(gc, 3, mt, (ALU.add, ALU.subtract), s_m2)
                        reached(dve, s_m2, 4 * gc + 2 * mt + 2)
                        reached(dve, s_out[mt], 16 * gc)
                        for parity in range(2):
                            nc.vector.scalar_tensor_tensor(
                                t[:, mt].rearrange("p (b i r) -> p r (b i)", b=B, r=2)[:, parity],
                                acc[:, mt, parity].rearrange("p b i -> p (b i)"), scale[:, 1, mt:mt + 1],
                                xr[:, mt].rearrange("p (b i r) -> p r (b i)", b=B, r=2)[:, parity],
                                ALU.mult, ALU.add).then_inc(s_t, 1)

            pipeline(dve, groups, 3, step)

        @block.tensor
        def _(pe):
            pe.wait_ge(s_fl, 4 * Q * KD)
            pe.wait_ge(s_w1l, 1)

            def products(out, terms):
                passes = [q for sh, sl, mh, ml in terms for q in ((sl, mh), (sh, ml), (sh, mh))]
                for n, (stationary, moving) in enumerate(passes):
                    last = nc.tensor.matmul(out, stationary, moving, start=(n == 0), stop=(n == len(passes) - 1))
                return last

            def conv1(g, h):
                reached(pe, s_xl, 2 * g + h + 1)
                reached(pe, s_hp, 2 * (2 * g + h))
                for mt in range(KD):
                    cols = slice(mt * P, mt * P + P)
                    products(ps_c1[:, mt], [(w1_h[:, k, cols], w1_l[:, k, cols], xh[:, k], xl[:, k]) for k in range(KD)]).then_inc(s_c1, 1)

            def conv2(g, pos):
                s, first, triples = PRODUCTS[pos]
                reached(pe, s_sl, 6 * g + 2 * s + 2)
                for mt in range(KD):
                    if pos == 0:
                        reached(pe, s_m1, 4 * g - 2 + 2 * mt)
                    elif pos == 1:
                        reached(pe, s_m2, 4 * g - 2 + 2 * mt)
                    else:
                        reached(pe, (s_ev, s_od)[pos - 2], 2 * g + mt + 1)
                    cols = slice(mt * P, mt * P + P)
                    terms = []
                    for q in range(triples):
                        for k in range(KD):
                            parity, at = (3 * q + first) % 2, (3 * q + first) // 2
                            terms.append((w2_h[:, BASE[pos] + q, k, cols], w2_l[:, BASE[pos] + q, k, cols],
                                          seq_h[:, s, k, parity, :, at:at + HALF], seq_l[:, s, k, parity, :, at:at + HALF]))
                    products(ps_c2[:, (2 * pos + mt) % 4].rearrange("p (b i) -> p b i", b=B), terms).then_inc(s_c2, 1)

            def step(i, u, live):
                if live(2):
                    conv2(i - 2, 0)
                if live(1):
                    conv1(i - 1, 0)
                if live(2):
                    conv2(i - 2, 1)
                if live(1):
                    conv1(i - 1, 1)
                if live(2):
                    conv2(i - 2, 2)
                    conv2(i - 2, 3)

            pipeline(pe, groups, 3, step)


def phase_c(nc, G, x1_t, xc_t, adj_t, w_ih, w_hh, w_msg, w_se, b_ih, b_hh, b_msg, b_se, form, y_n):
    B = 4
    T = B * P
    groups = G // B
    NS = w_se.shape[-1]
    with ExitStack() as ctx:
        def sb(name, shape, dt=F32):
            return ctx.enter_context(nc.sbuf_tensor("c_" + name, shape, dt))

        def sem(name):
            return ctx.enter_context(nc.semaphore("c_" + name))

        wi_h = sb("wi_h", [P, 2 * KD, 3 * D], F32R)
        wi_l = sb("wi_l", [P, 2 * KD, 3 * D], F32R)
        wh_h = sb("wh_h", [P, KD, 3 * D], F32R)
        wh_l = sb("wh_l", [P, KD, 3 * D], F32R)
        wm_h = sb("wm_h", [P, KD, D], F32R)
        wm_l = sb("wm_l", [P, KD, D], F32R)
        ws_h = sb("ws_h", [P, KD, NS], F32R)
        ws_l = sb("ws_l", [P, KD, NS], F32R)
        wi_raw = sb("wi_raw", [P, 2 * KD, 3 * D])
        wh_raw = sb("wh_raw", [P, KD, 3 * D])
        wm_raw = sb("wm_raw", [P, KD, D])
        ws_raw = sb("ws_raw", [P, KD, NS])
        bi = sb("bi", [P, 3, KD])
        bh = sb("bh", [P, 3, KD])
        brz = sb("brz", [P, 2, KD])
        bsum = sb("bsum", [P, 2, KD])
        bm_row = sb("bm_row", [P, 2, D])
        bs = sb("bs", [NS, 1])
        fm = sb("fm", [NS, 6])
        lin = sb("lin", [NS, 2])
        con = sb("con", [NS, 2])
        ident = sb("ident", [P, P])
        neg_half = sb("neg_half", [P, B])

        x1 = sb("x1", [P, 2, KD, T])
        xg = sb("xg", [P, 2, KD, T])
        xc = sb("xc", [P, 2, KD, T])
        at = sb("at", [P, 2, B, P])
        xh = sb("xh", [P, 2, KD, T], F32R)
        xl = sb("xl", [P, 2, KD, T], F32R)
        ch = sb("ch", [P, 2, KD, T], F32R)
        cl = sb("cl", [P, 2, KD, T], F32R)
        sq = sb("sq", [NS, T])
        left0 = sb("left0", [NS, T])
        right0 = sb("right0", [NS, T])
        left = sb("left", [NS, T])
        right = sb("right", [NS, T])
        mpre = sb("mpre", [P, B, D])
        mh = sb("mh", [P, B, D], F32R)
        ml = sb("ml", [P, B, D], F32R)
        ea = sb("ea", [P, B, P])
        aa = sb("aa", [P, B, P])
        ah = sb("ah", [P, B, P], F32R)
        al = sb("al", [P, B, P], F32R)
        nh = sb("nh", [P, 2, KD, T], F32R)
        nl = sb("nl", [P, 2, KD, T], F32R)
        tr = sb("tr", [P, T])
        rr = sb("rr", [P, T])
        hn = sb("hn", [P, T])
        npre = sb("npre", [P, T])
        nn = sb("nn", [P, T])
        tz = sb("tz", [P, T])
        zz = sb("zz", [P, T])
        dd = sb("dd", [P, T])
        zd = sb("zd", [P, T])
        nx = sb("nx", [P, T])
        yt = sb("yt", [P, KD, T])
        nmean = sb("nmean", [P, B])
        stats = sb("stats", [P, B, 6])
        mv = sb("mv", [P, B, 2])
        var_eps = sb("var_eps", [P, B])
        rstd = sb("rstd", [P, B])
        shift = sb("shift", [P, B])
        yo = sb("yo", [P, B, D])

        ps_g = ctx.enter_context(nc.psum_tensor("c_ps_g", [P, 3, T], F32))
        ps_s = ctx.enter_context(nc.psum_tensor("c_ps_s", [P, T], F32))
        ps_m = ctx.enter_context(nc.psum_tensor("c_ps_m", [P, 2, T], F32))
        ps_y = ctx.enter_context(nc.psum_tensor("c_ps_y", [P, B, D], F32))

        s_w = sem("weights_loaded")
        s_wh = sem("weights_high")
        s_wl = sem("weights_low")
        s_c = sem("constants")
        s_c1 = sem("constants_first_step")
        s_id0 = sem("identity_zeroed")
        s_id = sem("identity_ready")
        s_half = sem("half_ready")
        s_x = [sem("x1_loaded0"), sem("x1_loaded1")]
        s_at = [sem("adj_loaded0"), sem("adj_loaded1")]
        s_xg = [sem("x1_again_loaded0"), sem("x1_again_loaded1")]
        s_xc = [sem("xconv_loaded0"), sem("xconv_loaded1")]
        s_xh = sem("x1_high")
        s_xl = sem("x1_low")
        s_ch = sem("xconv_high")
        s_cl = sem("xconv_low")
        s_s = sem("similarity_products")
        s_sact = sem("similarity_rows_scaled")
        s_lr = sem("similarity_rows")
        s_m = sem("message_products")
        s_mpre = sem("message_biased")
        s_mh = sem("message_high")
        s_ml = sem("message_low")
        s_d = sem("distances")
        s_ea = sem("similarity_exp")
        s_aa = sem("similarity_masked")
        s_ah = sem("similarity_high")
        s_al = sem("similarity_low")
        s_nm = sem("messages_summed")
        s_nh = sem("message_sum_high")
        s_nl = sem("message_sum_low")
        s_gr = sem("gate_r_product")
        s_gh = sem("gate_hn_product")
        s_gi = sem("gate_in_product")
        s_gz = sem("gate_z_product")
        s_tr = sem("r_tanh")
        s_rr = sem("r_done")
        s_hn = sem("r_times_hn")
        s_np = sem("n_argument")
        s_nn = sem("n_done")
        s_tz = sem("z_tanh")
        s_zz = sem("z_done")
        s_dd = sem("x_minus_n")
        s_zd = sem("z_times_difference")
        s_nx = sem("n_plus_x")
        s_yt = sem("result_transposed_layout")
        s_y = sem("result_on_nodes")
        s_bn = sem("bn_stats_done")
        s_mv = sem("mean_var")
        s_ve = sem("var_eps_done")
        s_rstd = sem("rstd_done")
        s_nmean = sem("mean_negated")
        s_sh = sem("shift_done")
        s_yo = sem("output_ready")
        s_out = sem("output_stored")
        block = ctx.enter_context(nc.Block())

        def loaded(eng, sems, per_group, g, u):
            reached(eng, sems[u], (g + (2 - u)) * (8 * per_group))

        @block.sync
        def _(sp):
            for dst, src in ((wi_raw[:, :, :], w_ih), (wh_raw[:, :, :], w_hh), (wm_raw[:, :, :], w_msg), (ws_raw[:, :, :], w_se),
                             (bi[:, :, :], b_ih), (bh[:, :, :], b_hh), (bs[:, :], b_se), (fm[:, :], form),
                             (bm_row[:, 0, :], b_msg.partition_broadcast(P)), (bm_row[:, 1, :], b_msg.partition_broadcast(P))):
                sp.dma_start(dst, src).then_inc(s_w, 16)

            def step(i, u, live):
                if live(0):
                    g = i
                    reached(sp, s_xl, g - 1)
                    sp.dma_start(x1[:, u], x1_t[:, :, bass.ts(g, T)]).then_inc(s_x[u], 16)
                if live(1):
                    g, v = i - 1, 1 - u
                    reached(sp, s_aa, g - 1)
                    sp.dma_start(at[:, v], adj_t[:, bass.ts(g, T)].rearrange("p (b m) -> p b m", b=B)).then_inc(s_at[v], 16)
                    reached(sp, s_cl, g - 1)
                    sp.dma_start(xc[:, v], xc_t[:, :, bass.ts(g, T)]).then_inc(s_xc[v], 16)
                if live(2):
                    g = i - 2
                    reached(sp, s_nx, 2 * g - 2)
                    sp.dma_start(xg[:, u], x1_t[:, :, bass.ts(g, T)]).then_inc(s_xg[u], 16)
                if live(4):
                    g = i - 4
                    reached(sp, s_yo, B * g + B)
                    sp.dma_start(y_n[:, bass.ts(g, B * D)].rearrange("p (b d) -> p b d", b=B), yo[:, :, :]).then_inc(s_out, 16)

            pipeline(sp, groups, 5, step)
            sp.wait_ge(s_out, 16 * groups)

        R_BANK, HN_BANK, IN_BANK, Z_BANK = (0, 1), (1, 2), (2, 0), (0, 1)

        @block.scalar
        def _(act):
            act.wait_ge(s_w, 160)
            for hi, raw in ((wi_h, wi_raw), (wh_h, wh_raw), (wm_h, wm_raw), (ws_h, ws_raw)):
                nc.scalar.activation(hi[:, :, :], raw[:, :, :], ACT.Copy).then_inc(s_wh, 1)
            act.wait_ge(s_c, 2)

            def r_tanh(g, j):
                reached(act, s_gr, 2 * g + j + 1)
                reached(act, s_rr, 2 * g + j)
                nc.scalar.activation(tr[:, :], ps_g[:, R_BANK[j], :], ACT.Tanh, bias=brz[:, 0, j:j + 1], scale=0.5).then_inc(s_tr, 1)

            def n_tanh(g, j):
                reached(act, s_np, 2 * g + j + 1)
                reached(act, s_dd, 2 * g + j)
                reached(act, s_nx, 2 * g + j)
                nc.scalar.activation(nn[:, :], npre[:, :], ACT.Tanh).then_inc(s_nn, 1)

            def z_tanh(g, j):
                reached(act, s_gz, 2 * g + j + 1)
                reached(act, s_zz, 2 * g + j)
                nc.scalar.activation(tz[:, :], ps_g[:, Z_BANK[j], :], ACT.Tanh, bias=brz[:, 1, j:j + 1], scale=0.5).then_inc(s_tz, 1)

            def step(i, u, live):
                ga, v = i - 2, u
                gg = i - 3
                if live(3):
                    r_tanh(gg, 0)
                if live(2):
                    reached(act, s_s, ga + 1)
                    reached(act, s_lr, 2 * ga)
                    nc.scalar.activation(sq[:, :], ps_s[0:NS, :], ACT.Square, bias=bs[:, 0:1]).then_inc(s_sact, 1)
                    for side, part in ((0, left0), (1, right0)):
                        nc.scalar.activation(part[:, :], ps_s[0:NS, :], ACT.Identity, bias=con[:, side:side + 1],
                                             scale=fm[:, 3 * side + 1:3 * side + 2]).then_inc(s_sact, 1)
                    reached(act, s_mpre, 2 * ga + 2)
                    reached(act, s_nm, ga)
                    nc.scalar.activation(mh[:, :, :], mpre[:, :, :], ACT.Relu).then_inc(s_mh, 1)
                if live(3):
                    n_tanh(gg, 0)
                if live(4):
                    go = i - 4
                    reached(act, s_sh, go + 1)
                    reached(act, s_out, 16 * go)
                    for b in range(B):
                        nc.scalar.activation(yo[:, b], ps_y[:, b], ACT.Identity, bias=shift[:, b:b + 1],
                                             scale=rstd[:, b:b + 1]).then_inc(s_yo, 1)
                if live(3):
                    z_tanh(gg, 0)
                if live(2):
                    loaded(act, s_xc, 1, ga, v)
                    reached(act, s_gz, 2 * ga - 2)
                    nc.scalar.activation(ch[:, v], xc[:, v], ACT.Copy).then_inc(s_ch, 1)
                    reached(act, s_d, ga + 1)
                    reached(act, s_aa, ga)
                    nc.scalar.activation(ea[:, :, :], ps_s[:, :].rearrange("p (b m) -> p b m", b=B), ACT.Exp).then_inc(s_ea, 1)
                    reached(act, s_aa, ga + 1)
                    reached(act, s_nm, ga)
                    nc.scalar.activation(ah[:, :, :], aa[:, :, :], ACT.Copy).then_inc(s_ah, 1)
                if live(3):
                    r_tanh(gg, 1)
                if live(2):
                    reached(act, s_nm, ga + 1)
                    reached(act, s_gz, 2 * ga - 2)
                    nc.scalar.activation(nh[:, v], ps_m[:, :, :], ACT.Copy).then_inc(s_nh, 1)
                if live(3):
                    n_tanh(gg, 1)
                    z_tanh(gg, 1)
                if live(1):
                    g, w = i - 1, 1 - u
                    loaded(act, s_x, 1, g, w)
                    reached(act, s_gz, 2 * g - 2)
                    nc.scalar.activation(xh[:, w], x1[:, w], ACT.Copy).then_inc(s_xh, 1)

            pipeline(act, groups, 5, step)

        @block.gpsimd
        def _(pool):
            nc.gpsimd.memset(ident[:, :], 0.0).then_inc(s_id0, 1)
            nc.gpsimd.memset(neg_half[:, :], -0.5).then_inc(s_half, 1)
            pool.wait_ge(s_id0, 1)
            nc.gpsimd.affine_select(out=ident[:, :], in_=ident[:, :], compare_op=ALU.not_equal, fill=1.0,
                                    base=0, pattern=[[-1, P]], channel_multiplier=1).then_inc(s_id, 1)
            pool.wait_ge(s_half, 1)

            def with_x(g, v, j):
                reached(pool, s_nn, 2 * g + j + 1)
                reached(pool, s_zd, 2 * g + j)
                nc.gpsimd.tensor_tensor(dd[:, :], xg[:, v, j], nn[:, :], ALU.subtract).then_inc(s_dd, 1)
                reached(pool, s_yt, 2 * g + j)
                nc.gpsimd.tensor_tensor(nx[:, :], xg[:, v, j], nn[:, :], ALU.add).then_inc(s_nx, 1)

            def step(i, u, live):
                if live(4):
                    go = i - 4
                    reached(pool, s_ve, go + 1)
                    reached(pool, s_yo, B * go)
                    nc.gpsimd.tensor_tensor(rstd[:, :], var_eps[:, :], neg_half[:, :], ALU.pow).then_inc(s_rstd, 1)
                if live(3):
                    g, w = i - 3, 1 - u
                    loaded(pool, s_xg, 1, g, w)
                    with_x(g, w, 0)
                if live(2):
                    ga, v = i - 2, u
                    reached(pool, s_ch, ga + 1)
                    nc.gpsimd.tensor_tensor(cl[:, v], xc[:, v], ch[:, v].bitcast(F32), ALU.subtract).then_inc(s_cl, 1)
                if live(3):
                    with_x(g, w, 1)

            pipeline(pool, groups, 5, step)

        @block.vector
        def _(dve):
            dve.wait_ge(s_w, 160)
            nc.vector.tensor_tensor(bsum[:, :, :], bi[:, 0:2, :], bh[:, 0:2, :], ALU.add).then_inc(s_c1, 1)
            for side in range(2):
                nc.vector.tensor_tensor(lin[:, side:side + 1], fm[:, 3 * side + 1:3 * side + 2], bs[:, :], ALU.mult).then_inc(s_c1, 1)
            dve.wait_ge(s_c1, 3)
            nc.vector.tensor_scalar(brz[:, :, :], bsum[:, :, :], 0.5, None, ALU.mult).then_inc(s_c, 1)
            for side in range(2):
                last = nc.vector.tensor_tensor(con[:, side:side + 1], lin[:, side:side + 1], fm[:, 3 * side + 2:3 * side + 3], ALU.add)
            last.then_inc(s_c, 1)
            dve.wait_ge(s_wh, 4)
            for lo, hi, raw in ((wi_l, wi_h, wi_raw), (wh_l, wh_h, wh_raw), (wm_l, wm_h, wm_raw), (ws_l, ws_h, ws_raw)):
                nc.vector.tensor_tensor(lo[:, :, :], raw[:, :, :], hi[:, :, :].bitcast(F32), ALU.subtract).then_inc(s_wl, 1)

            def r_and_hn(g, j):
                n = 2 * g + j
                reached(dve, s_tr, n + 1)
                reached(dve, s_hn, n)
                nc.vector.tensor_scalar(rr[:, :], tr[:, :], 0.5, 0.5, ALU.mult, ALU.add).then_inc(s_rr, 1)
                reached(dve, s_gh, n + 1)
                reached(dve, s_np, n)
                reached(dve, s_rr, n + 1)
                nc.vector.scalar_tensor_tensor(hn[:, :], ps_g[:, HN_BANK[j], :], bh[:, 2, j:j + 1], rr[:, :],
                                               ALU.add, ALU.mult).then_inc(s_hn, 1)

            def n_argument(g, j):
                n = 2 * g + j
                reached(dve, s_gi, n + 1)
                reached(dve, s_hn, n + 1)
                reached(dve, s_nn, n)
                nc.vector.scalar_tensor_tensor(npre[:, :], ps_g[:, IN_BANK[j], :], bi[:, 2, j:j + 1], hn[:, :],
                                               ALU.add, ALU.add).then_inc(s_np, 1)

            def result(g, j):
                n = 2 * g + j
                reached(dve, s_tz, n + 1)
                reached(dve, s_zd, n)
                nc.vector.tensor_scalar(zz[:, :], tz[:, :], 0.5, 0.5, ALU.mult, ALU.add).then_inc(s_zz, 1)
                reached(dve, s_dd, n + 1)
                reached(dve, s_zz, n + 1)
                reached(dve, s_yt, n)
                nc.vector.tensor_tensor(zd[:, :], zz[:, :], dd[:, :], ALU.mult).then_inc(s_zd, 1)
                reached(dve, s_nx, n + 1)
                reached(dve, s_zd, n + 1)
                reached(dve, s_y, g)
                nc.vector.tensor_tensor(yt[:, j], zd[:, :], nx[:, :], ALU.add).then_inc(s_yt, 1)

            def step(i, u, live):
                ga, v = i - 2, u
                gg, go = i - 3, i - 4
                if live(3):
                    r_and_hn(gg, 0)
                if live(4):
                    reached(dve, s_sh, go)
                    reached(dve, s_y, go + 1)
                    for b in range(B):
                        last = nc.vector.bn_stats(stats[:, b], ps_y[:, b])
                    last.then_inc(s_bn, 1)
                    dve.wait_ge(s_w, 160)
                    reached(dve, s_bn, go + 1)
                    for b in range(B):
                        last = nc.vector.bn_aggr(mv[:, b], stats[:, b])
                    last.then_inc(s_mv, 1)
                    reached(dve, s_mv, go + 1)
                    nc.vector.tensor_scalar(var_eps[:, :], mv[:, :, 1], EPS, None, ALU.add).then_inc(s_ve, 1)
                    nc.vector.tensor_scalar(nmean[:, :], mv[:, :, 0], -1.0, None, ALU.mult).then_inc(s_nmean, 1)
                if live(2):
                    reached(dve, s_sact, 3 * ga + 3)
                    reached(dve, s_d, ga)
                    for side, (part, row) in enumerate(((left0, left), (right0, right))):
                        nc.vector.scalar_tensor_tensor(row[:, :], sq[:, :], fm[:, 3 * side:3 * side + 1], part[:, :],
                                                       ALU.mult, ALU.add).then_inc(s_lr, 1)
                    reached(dve, s_m, ga + 1)
                    reached(dve, s_ml, ga)
                    for h in range(2):
                        nc.vector.tensor_tensor(mpre[:, 2 * h:2 * h + 2], ps_m[:, h].rearrange("p (b d) -> p b d", b=2),
                                                bm_row[:, :, :], ALU.add).then_inc(s_mpre, 1)
                if live(4):
                    reached(dve, s_rstd, go + 1)
                    reached(dve, s_nmean, go + 1)
                    nc.vector.tensor_tensor(shift[:, :], nmean[:, :], rstd[:, :], ALU.mult).then_inc(s_sh, 1)
                if live(3):
                    n_argument(gg, 0)
                if live(2):
                    reached(dve, s_mh, ga + 1)
                    nc.vector.scalar_tensor_tensor(ml[:, :, :], mpre[:, :, :], 0.0, mh[:, :, :].bitcast(F32),
                                                   ALU.max, ALU.subtract).then_inc(s_ml, 1)
                if live(3):
                    result(gg, 0)
                if live(2):
                    reached(dve, s_ea, ga + 1)
                    loaded(dve, s_at, 1, ga, v)
                    reached(dve, s_al, ga)
                    nc.vector.tensor_tensor(aa[:, :, :], ea[:, :, :], at[:, v], ALU.mult).then_inc(s_aa, 1)
                    reached(dve, s_ah, ga + 1)
                    nc.vector.tensor_tensor(al[:, :, :], aa[:, :, :], ah[:, :, :].bitcast(F32), ALU.subtract).then_inc(s_al, 1)
                if live(3):
                    r_and_hn(gg, 1)
                if live(2):
                    reached(dve, s_nh, ga + 1)
                    nc.vector.tensor_tensor(nl[:, v], ps_m[:, :, :], nh[:, v].bitcast(F32), ALU.subtract).then_inc(s_nl, 1)
                if live(3):
                    n_argument(gg, 1)
                    result(gg, 1)
                if live(1):
                    g, w = i - 1, 1 - u
                    reached(dve, s_xh, g + 1)
                    nc.vector.tensor_tensor(xl[:, w], x1[:, w], xh[:, w].bitcast(F32), ALU.subtract).then_inc(s_xl, 1)

            pipeline(dve, groups, 5, step)

        @block.tensor
        def _(pe):
            pe.wait_ge(s_wl, 4)
            pe.wait_ge(s_id, 1)

            def products(out, terms):
                passes = [q for sh, sl, mh_, ml_ in terms for q in ((sl, mh_), (sh, ml_), (sh, mh_))]
                for n, (stationary, moving) in enumerate(passes):
                    last = nc.tensor.matmul(out, stationary, moving, start=(n == 0), stop=(n == len(passes) - 1))
                return last

            def gate(bank, v, which, j, own, inputs):
                cols = slice(which * D + j * P, which * D + j * P + P)
                terms = []
                if own:
                    terms += [(wh_h[:, k, cols], wh_l[:, k, cols], xh[:, v, k], xl[:, v, k]) for k in range(KD)]
                if inputs:
                    terms += [(wi_h[:, k, cols], wi_l[:, k, cols], ch[:, v, k], cl[:, v, k]) for k in range(KD)]
                    terms += [(wi_h[:, KD + k, cols], wi_l[:, KD + k, cols], nh[:, v, k], nl[:, v, k]) for k in range(KD)]
                return products(ps_g[:, bank, :], terms)

            def step(i, u, live):
                ga, v = i - 2, u
                g, w = i - 3, 1 - u
                if live(3):
                    reached(pe, s_nl, g + 1)
                    reached(pe, s_cl, g + 1)
                    reached(pe, s_np, 2 * g)
                    gate(R_BANK[0], w, 0, 0, True, True).then_inc(s_gr, 1)
                    reached(pe, s_tz, 2 * g)
                    gate(HN_BANK[0], w, 2, 0, True, False).then_inc(s_gh, 1)
                if live(4):
                    go = i - 4
                    reached(pe, s_yt, 2 * go + 2)
                    reached(pe, s_yo, B * go)
                    for b in range(B):
                        for j in range(KD):
                            last = nc.tensor.transpose(ps_y[:, b, j * P:j * P + P], yt[:, j, b * P:b * P + P], ident[:, :])
                    last.then_inc(s_y, 1)
                if live(2):
                    reached(pe, s_xl, ga + 1)
                    reached(pe, s_ea, ga)
                    products(ps_s[0:NS, :], [(ws_h[:, k, :], ws_l[:, k, :], xh[:, v, k], xl[:, v, k]) for k in range(KD)]).then_inc(s_s, 1)
                    reached(pe, s_nl, ga)
                    for b in range(B):
                        cols = slice(b * P, b * P + P)
                        last = products(ps_m[:, b // 2, b % 2 * D:b % 2 * D + D],
                                        [(xh[:, v, k, cols], xl[:, v, k, cols], wm_h[:, k, :], wm_l[:, k, :]) for k in range(KD)])
                    last.then_inc(s_m, 1)
                if live(3):
                    reached(pe, s_hn, 2 * g)
                    gate(IN_BANK[0], w, 2, 0, False, True).then_inc(s_gi, 1)
                    reached(pe, s_tr, 2 * g + 1)
                    gate(Z_BANK[0], w, 1, 0, True, True).then_inc(s_gz, 1)
                if live(2):
                    reached(pe, s_lr, 2 * ga + 2)
                    for b in range(B):
                        cols = slice(b * P, b * P + P)
                        last = nc.tensor.matmul(ps_s[:, cols], left[:, cols], right[:, cols], start=True, stop=True)
                    last.then_inc(s_d, 1)
                if live(3):
                    reached(pe, s_hn, 2 * g + 1)
                    gate(R_BANK[1], w, 0, 1, True, True).then_inc(s_gr, 1)
                    reached(pe, s_np, 2 * g + 1)
                    gate(HN_BANK[1], w, 2, 1, True, False).then_inc(s_gh, 1)
                if live(2):
                    reached(pe, s_al, ga + 1)
                    reached(pe, s_ml, ga + 1)
                    for j in range(KD):
                        for b in range(B):
                            last = products(ps_m[:, j, b * P:b * P + P],
                                            [(mh[:, b, j * P:j * P + P], ml[:, b, j * P:j * P + P], ah[:, b], al[:, b])])
                    last.then_inc(s_nm, 1)
                if live(3):
                    reached(pe, s_tz, 2 * g + 1)
                    gate(IN_BANK[1], w, 2, 1, False, True).then_inc(s_gi, 1)
                    reached(pe, s_tr, 2 * g + 2)
                    gate(Z_BANK[1], w, 1, 1, True, True).then_inc(s_gz, 1)

            pipeline(pe, groups, 5, step)


def similarity_rows():
    rows = np.zeros((9, 6), np.float32)
    rows[0:3, 1], rows[0:3, 4] = 1.0, 2.0
    rows[3:6, 2], rows[3:6, 3] = 1.0, -1.0
    rows[6:9, 0], rows[6:9, 5] = -1.0, 1.0
    return rows


def kernel(**inputs):
    from concourse import bacc
    from concourse.bass_utils import run_bass_kernel_spmd

    a = {name: np.asarray(v) for name, v in inputs.items()}
    x, adj = a["x"], a["adj"]
    G = x.shape[0]

    def tiles(w):
        return w.T.reshape(-1, P, w.shape[0]).transpose(1, 0, 2)

    def vector(b, parts):
        return b.reshape(parts, KD, P).transpose(2, 0, 1)

    def bn(layer):
        return vector(np.concatenate([a[f"L1_gnn_bn{layer}_{v}"] for v in "gbmv"]), 4)

    laid_out = {
        "x_n": x.transpose(1, 0, 2).reshape(P, G * D),
        "x_t": x.transpose(2, 0, 1).reshape(KD, P, G * P).transpose(1, 0, 2),
        "adj_n": adj.transpose(1, 0, 2).reshape(P, G * P),
        "adj_t": adj.transpose(2, 0, 1).reshape(P, G * P),
        "w0": np.concatenate([a["L0_gnn_theta"], a["L0_gnn_W_h"], a["L0_gnn_W_t"]], 1).reshape(KD, P, 3 * D).transpose(1, 0, 2),
        "b_t": a["L0_gnn_b_t"],
        "w_c1": tiles(a["L1_gnn_conv1_w"][:, :, 0]),
        "w_c2": a["L1_gnn_conv2_w"].transpose(1, 2, 0).reshape(KD, P, -1, D).transpose(1, 0, 2, 3),
        "bn1": bn(1),
        "bn2": bn(2),
        "w_ih": tiles(a["L1_gnn_w_ih"]),
        "w_hh": tiles(a["L1_gnn_w_hh"]),
        "w_msg": tiles(a["L1_gnn_w_msg"]),
        "w_se": tiles(np.concatenate([a["L1_gnn_w_se"]] * 3, 0)),
        "b_ih": vector(a["L1_gnn_b_ih"], 3),
        "b_hh": vector(a["L1_gnn_b_hh"], 3),
        "b_msg": a["L1_gnn_b_msg"],
        "b_se": np.concatenate([a["L1_gnn_b_se"]] * 3).reshape(-1, 1),
        "form": similarity_rows(),
    }
    nc = bacc.Bacc("TRN2", target_bir_lowering=False, num_devices=1)
    arrays, d = {}, {}
    for name, v in laid_out.items():
        arrays[f"in_{name}"] = np.ascontiguousarray(v)
        d[name] = nc.dram_tensor(f"in_{name}", v.shape, F32, kind="ExternalInput").ap()
    x1_t = nc.dram_tensor("x1_t", (P, KD, G * P), F32, kind="Internal").ap()
    xc_t = nc.dram_tensor("xc_t", (P, KD, G * P), F32, kind="Internal").ap()
    y_n = nc.dram_tensor("out_y", (P, G * D), F32, kind="ExternalOutput").ap()
    phase_a(nc, G, d["x_n"], d["x_t"], d["adj_n"], d["adj_t"], d["w0"], d["b_t"], x1_t)
    phase_b(nc, G, x1_t, d["w_c1"], d["w_c2"], d["bn1"], d["bn2"], xc_t)
    phase_c(nc, G, x1_t, xc_t, d["adj_t"], d["w_ih"], d["w_hh"], d["w_msg"], d["w_se"], d["b_ih"], d["b_hh"],
            d["b_msg"], d["b_se"], d["form"], y_n)
    r = run_bass_kernel_spmd(nc, [arrays], core_ids=[0])
    return r.results[0]["out_y"].reshape(P, G, D).transpose(1, 0, 2)
```

```python
from contextlib import ExitStack

import numpy as np

import concourse.bass as bass
from concourse import mybir

F32 = mybir.dt.float32
F32R = mybir.dt.float32r
ALU = mybir.AluOpType
ACT = mybir.ActivationFunctionType

P = 128
D = 256
KD = D // P
EPS = 1e-5


def reached(eng, sem, count):
    if isinstance(count, int) and count <= 0:
        return
    eng.wait_ge(sem, count)


def pipeline(eng, units, stages, step, peeled=0):
    first = max(stages, peeled)
    first += first % 2
    for i in range(first):
        step(i, i % 2, lambda s, i=i: 0 <= i - s < units)
    with eng.Fori(first // 2, units // 2) as two:
        step(two * 2, 0, lambda s: True)
        step(two * 2 + 1, 1, lambda s: True)
    for i in range(units, units + stages - 1):
        step(i, i % 2, lambda s, i=i: 0 <= i - s < units)


def phase_a(nc, G, x_n, x_t, adj_n, adj_t, w0, b_t, x1_t, filters):
    pairs = G // 2
    with ExitStack() as ctx:
        def sb(name, shape, dt=F32):
            return ctx.enter_context(nc.sbuf_tensor("a_" + name, shape, dt))

        def sem(name):
            return ctx.enter_context(nc.semaphore("a_" + name))

        w_raw = sb("w_raw", [P, KD, 3 * D])
        w_hi = sb("w_hi", [P, KD, 3 * D], F32R)
        w_lo = sb("w_lo", [P, KD, 3 * D], F32R)
        bt_raw = sb("bt_raw", [2, D])
        bt_h = sb("bt_h", [2, D])
        bt_hr = sb("bt_hr", [2, D], F32R)
        bt_l = sb("bt_l", [2, D])
        bt_rows = sb("bt_rows", [2, D], F32R)
        ones0 = sb("ones0", [2, P])
        ones = sb("ones", [2, P], F32R)
        ident = sb("ident", [P, P])
        neg_half = sb("neg_half", [P, 2])
        filter_rows = sb("filter_rows", [P, 2, 6, D])
        xt = sb("xt", [P, 2, KD, 2 * P])
        at = sb("at", [P, 2, 2, P])
        an = sb("an", [P, 2, 2, P])
        xn = sb("xn", [P, 2, 2, D])
        xh = sb("xh", [P, 2, KD, 2 * P], F32R)
        xl = sb("xl", [P, 2, KD, 2 * P], F32R)
        ah = sb("ah", [P, 2, 2, P], F32R)
        al = sb("al", [P, 2, 2, P], F32R)
        fh = sb("fh", [P, 2, 2, D], F32R)
        fl = sb("fl", [P, 2, 2, D], F32R)
        an_copy = sb("an_copy", [P, 2, 2, P])
        deg = sb("deg", [P, 2, 2])
        deg_eps = sb("deg_eps", [P, 2])
        norm = sb("norm", [P, 2, 2])
        het = sb("het", [P, 2, 2, D])
        gate = sb("gate", [P, 2, 2, D])
        diff = sb("diff", [P, 2, D])
        gd = sb("gd", [P, 2, D])
        mix = sb("mix", [P, 2, 2, D])
        below = sb("below", [P, 2, D])
        ex = sb("ex", [P, 2, D])
        em1 = sb("em1", [P, 2, D])
        res = sb("res", [P, 2, 2, D])
        y = sb("y", [P, 2, 2, D])
        stats = sb("stats", [P, 2, 6])
        mv = sb("mv", [P, 2, 2, 2])
        var_eps = sb("var_eps", [P, 2])
        rstd = sb("rstd", [P, 2, 2])
        x1 = sb("x1", [P, 2, 2, D])
        x1t = sb("x1t", [P, 2, KD, 2 * P])

        ps_hh = ctx.enter_context(nc.psum_tensor("a_ps_hh", [P, 4, 2 * D], F32))
        ps_g = ctx.enter_context(nc.psum_tensor("a_ps_g", [P, 2, 2, D], F32))
        ps_hom = ctx.enter_context(nc.psum_tensor("a_ps_hom", [P, 2, D], F32))
        ps_t = ctx.enter_context(nc.psum_tensor("a_ps_t", [P, KD, 2 * P], F32))

        s_w = sem("weights_loaded")
        s_wh = sem("weights_high")
        s_wl = sem("weights_low")
        s_bt = sem("b_t_rows")
        s_on = sem("ones_ready")
        s_id0 = sem("identity_zeroed")
        s_id = sem("identity_ready")
        s_half = sem("half_ready")
        s_in = [sem("x_adj_loaded0"), sem("x_adj_loaded1")]
        s_xn = [sem("x_nodes_loaded0"), sem("x_nodes_loaded1")]
        s_xh = sem("x_high")
        s_xl = sem("x_low")
        s_ah = sem("adj_high")
        s_al = sem("adj_low")
        s_deg = sem("degree")
        s_dege = sem("degree_eps")
        s_norm = sem("norm")
        s_proj = sem("projected")
        s_gp = sem("gate_projected")
        s_fh = sem("f_high")
        s_fl = sem("f_low")
        s_het = sem("het_copied")
        s_gate = sem("gate_ready")
        s_hom = sem("hom_done")
        s_diff = sem("diff_done")
        s_gd = sem("gated_diff")
        s_mix = sem("mixed")
        s_below = sem("mix_clamped")
        s_ex = sem("exp_done")
        s_em1 = sem("exp_minus_one")
        s_res = sem("residual_added")
        s_y = sem("y_done")
        s_bn = sem("bn_stats_done")
        s_mv = sem("mean_var")
        s_ve = sem("var_eps_done")
        s_rstd = sem("rstd_done")
        s_x1 = sem("x1_done")
        s_tr = sem("transposed")
        s_x1t = sem("x1t_copied")
        s_out = [sem("x1t_stored0"), sem("x1t_stored1")]
        block = ctx.enter_context(nc.Block())

        STAGES = 8
        FILTER_STEPS = filters.units
        PEELED = FILTER_STEPS + 1

        @block.sync
        def _(sp):
            sp.dma_start(w_raw[:, :, :], w0).then_inc(s_w, 16)
            sp.dma_start(bt_raw[:, :], b_t.partition_broadcast(2)).then_inc(s_w, 16)

            def step(i, u, live):
                v = 1 - u
                if live(0):
                    p = i
                    reached(sp, s_xl, p - 1)
                    reached(sp, s_al, p - 1)
                    reached(sp, s_deg, p - 1)
                    sp.dma_start(xt[:, u], x_t[:, :, bass.ts(p, 2 * P)]).then_inc(s_in[u], 16)
                    sp.dma_start(at[:, u], adj_t[:, bass.ts(p, 2 * P)].rearrange("p (b m) -> p b m", b=2)).then_inc(s_in[u], 16)
                    sp.dma_start(an[:, u], adj_n[:, bass.ts(p, 2 * P)].rearrange("p (b m) -> p b m", b=2)).then_inc(s_in[u], 16)
                if isinstance(i, int) and 1 <= i <= FILTER_STEPS:
                    reached(sp, s_wl, 1)
                    filters.load(sp, i - 1, w_raw[:, (i - 1) % 2])
                    if 2 <= i < 2 + filters.triples:
                        filters.store(sp, i - 2)
                if live(3):
                    p = i - 3
                    reached(sp, s_res, p - 1)
                    sp.dma_start(xn[:, v], x_n[:, bass.ts(p, 2 * D)].rearrange("p (b d) -> p b d", b=2)).then_inc(s_xn[v], 16)
                if live(7):
                    p = i - 7
                    reached(sp, s_x1t, p + 1)
                    sp.dma_start(x1_t[:, :, bass.ts(p, 2 * P)], x1t[:, v]).then_inc(s_out[v], 16)

            pipeline(sp, pairs, STAGES, step, PEELED)
            for u in range(2):
                sp.wait_ge(s_out[u], 16 * (pairs // 2))

        def loaded(eng, sems, per_pair, p, u):
            reached(eng, sems[u], (p + (2 - u)) * (8 * per_pair))

        @block.scalar
        def _(act):
            act.wait_ge(s_w, 32)
            nc.scalar.activation(w_hi[:, :, :], w_raw[:, :, :], ACT.Copy).then_inc(s_wh, 1)
            nc.scalar.activation(bt_hr[:, :], bt_raw[:, :], ACT.Copy).then_inc(s_wh, 1)
            act.wait_ge(s_on, 1)
            nc.scalar.activation(ones[:, :], ones0[:, :], ACT.Copy).then_inc(s_wh, 1)

            def step(i, u, live):
                v = 1 - u
                if live(4):
                    p = i - 4
                    reached(act, s_mix, p + 1)
                    reached(act, s_ex, p)
                    nc.scalar.activation(below[:, :, :], mix[:, u], ACT.Relu, scale=-1.0).then_inc(s_below, 1)
                    reached(act, s_below, p + 1)
                    reached(act, s_em1, p)
                    nc.scalar.activation(ex[:, :, :], below[:, :, :], ACT.Exp, scale=-1.0).then_inc(s_ex, 1)
                if live(1):
                    p = i - 1
                    loaded(act, s_in, 3, p, v)
                    reached(act, s_gp, p - 1)
                    nc.scalar.activation(xh[:, v], xt[:, v], ACT.Copy).then_inc(s_xh, 1)
                    reached(act, s_hom, p - 1)
                    nc.scalar.activation(ah[:, v], at[:, v], ACT.Copy).then_inc(s_ah, 1)
                    reached(act, s_dege, p - 1)
                    reached(act, s_deg, p - 1)
                    for b in range(2):
                        last = nc.scalar.activation(an_copy[:, v, b], an[:, v, b], ACT.Copy, accum_out=deg[:, v, b:b + 1])
                    last.then_inc(s_deg, 1)
                if live(4):
                    p = i - 4
                    reached(act, s_ex, p + 1)
                    reached(act, s_res, p)
                    nc.scalar.activation(em1[:, :, :], ex[:, :, :], ACT.Copy, bias=-1.0).then_inc(s_em1, 1)
                if live(2):
                    p = i - 2
                    reached(act, s_hom, p - 1)
                    reached(act, s_norm, p + 1)
                    for b in range(2):
                        reached(act, s_proj, 2 * p + b + 1)
                        nc.scalar.activation(fh[:, u, b], ps_hh[:, 2 * u + b, 0:D], ACT.Copy, scale=norm[:, u, b:b + 1]).then_inc(s_fh, 1)
                    reached(act, s_mix, p - 1)
                    nc.scalar.activation(het[:, u], ps_hh[:, 2 * u:2 * u + 2, D:2 * D], ACT.Copy).then_inc(s_het, 1)
                if live(7):
                    p = i - 7
                    reached(act, s_tr, p + 1)
                    reached(act, s_out[v], (p - v) * 8)
                    nc.scalar.activation(x1t[:, v], ps_t[:, :, :], ACT.Copy).then_inc(s_x1t, 1)
                if live(2):
                    p = i - 2
                    reached(act, s_gp, p + 1)
                    reached(act, s_gd, p - 1)
                    nc.scalar.activation(gate[:, u], ps_g[:, u], ACT.Tanh, scale=0.5).then_inc(s_gate, 1)
                if isinstance(i, int) and 1 <= i <= FILTER_STEPS:
                    filters.high(act, i - 1, w_raw[:, (i - 1) % 2], filter_rows[:, (i - 1) % 2])

            pipeline(act, pairs, STAGES, step, PEELED)

        @block.gpsimd
        def _(pool):
            nc.gpsimd.memset(ones0[:, :], 1.0).then_inc(s_on, 1)
            nc.gpsimd.memset(ident[:, :], 0.0).then_inc(s_id0, 1)
            nc.gpsimd.memset(neg_half[:, :], -0.5).then_inc(s_half, 1)
            pool.wait_ge(s_id0, 1)
            nc.gpsimd.affine_select(out=ident[:, :], in_=ident[:, :], compare_op=ALU.not_equal, fill=1.0,
                                    base=0, pattern=[[-1, P]], channel_multiplier=1).then_inc(s_id, 1)
            pool.wait_ge(s_half, 1)

            def step(i, u, live):
                v = 1 - u
                if live(2):
                    p = i - 2
                    reached(pool, s_dege, p + 1)
                    reached(pool, s_diff, p - 1)
                    reached(pool, s_fl, p - 1)
                    nc.gpsimd.tensor_tensor(norm[:, u], deg_eps[:, :], neg_half[:, :], ALU.pow).then_inc(s_norm, 1)
                if live(1):
                    p = i - 1
                    reached(pool, s_xh, p + 1)
                    reached(pool, s_gp, p - 1)
                    nc.gpsimd.tensor_tensor(xl[:, v], xt[:, v], xh[:, v].bitcast(F32), ALU.subtract).then_inc(s_xl, 1)
                    reached(pool, s_ah, p + 1)
                    reached(pool, s_hom, p - 1)
                    nc.gpsimd.tensor_tensor(al[:, v], at[:, v], ah[:, v].bitcast(F32), ALU.subtract).then_inc(s_al, 1)
                if live(4):
                    p = i - 4
                    loaded(pool, s_xn, 1, p, u)
                    reached(pool, s_em1, p + 1)
                    reached(pool, s_y, p - 1)
                    nc.gpsimd.tensor_tensor(res[:, u], em1[:, :, :], xn[:, u], ALU.add).then_inc(s_res, 1)
                if live(5):
                    p = i - 5
                    reached(pool, s_ve, p + 1)
                    reached(pool, s_x1, p - 1)
                    nc.gpsimd.tensor_tensor(rstd[:, v], var_eps[:, :], neg_half[:, :], ALU.pow).then_inc(s_rstd, 1)

                if isinstance(i, int) and 1 <= i <= FILTER_STEPS:
                    filters.low(pool, i - 1, filter_rows[:, (i - 1) % 2])

            pipeline(pool, pairs, STAGES, step, PEELED)

        @block.vector
        def _(dve):
            dve.wait_ge(s_wh, 3)
            nc.vector.tensor_tensor(w_lo[:, :, :], w_raw[:, :, :], w_hi[:, :, :].bitcast(F32), ALU.subtract).then_inc(s_wl, 1)
            nc.vector.tensor_tensor(bt_l[:, :], bt_raw[:, :], bt_hr[:, :].bitcast(F32), ALU.subtract).then_inc(s_bt, 1)
            dve.wait_ge(s_id, 1)
            nc.vector.tensor_scalar(bt_h[:, :], bt_hr[:, :].bitcast(F32), ident[0:2, 0:1], None, ALU.mult).then_inc(s_bt, 1)
            dve.wait_ge(s_bt, 2)
            nc.vector.scalar_tensor_tensor(bt_rows[:, :], bt_l[:, :], ident[0:2, 1:2], bt_h[:, :], ALU.mult, ALU.add).then_inc(s_bt, 1)

            def step(i, u, live):
                v = 1 - u
                p2, p3, p5, p6 = i - 2, i - 3, i - 5, i - 6
                if live(2):
                    reached(dve, s_deg, p2 + 1)
                    reached(dve, s_norm, p2)
                    nc.vector.tensor_scalar(deg_eps[:, :], deg[:, u], 1e-6, None, ALU.add).then_inc(s_dege, 1)
                if live(5):
                    reached(dve, s_x1, p5 - 1)
                    reached(dve, s_res, p5 + 1)
                    nc.vector.scalar_tensor_tensor(y[:, v], mix[:, v], 0.0, res[:, v], ALU.max, ALU.add).then_inc(s_y, 1)
                if live(3):
                    reached(dve, s_gd, p3)
                    reached(dve, s_hom, p3 + 1)
                    reached(dve, s_het, p3 + 1)
                    for b in range(2):
                        last = nc.vector.scalar_tensor_tensor(diff[:, b], ps_hom[:, b], norm[:, v, b:b + 1], het[:, v, b],
                                                              ALU.mult, ALU.subtract)
                    last.then_inc(s_diff, 1)
                if live(5):
                    reached(dve, s_mv, p5)
                    reached(dve, s_y, p5 + 1)
                    for b in range(2):
                        last = nc.vector.bn_stats(stats[:, b], y[:, v, b])
                    last.then_inc(s_bn, 1)
                if live(3):
                    reached(dve, s_mix, p3)
                    reached(dve, s_gate, p3 + 1)
                    reached(dve, s_diff, p3 + 1)
                    nc.vector.scalar_tensor_tensor(gd[:, :, :], gate[:, v], 1.0, diff[:, :, :], ALU.add, ALU.mult).then_inc(s_gd, 1)
                if live(5):
                    dve.wait_ge(s_wh, 3)
                    reached(dve, s_bn, p5 + 1)
                    for b in range(2):
                        last = nc.vector.bn_aggr(mv[:, v, b], stats[:, b])
                    last.then_inc(s_mv, 1)
                if live(3):
                    reached(dve, s_y, p3 - 1)
                    reached(dve, s_gd, p3 + 1)
                    nc.vector.scalar_tensor_tensor(mix[:, v], gd[:, :, :], 0.5, het[:, v], ALU.mult, ALU.add).then_inc(s_mix, 1)
                if live(5):
                    reached(dve, s_mv, p5 + 1)
                    reached(dve, s_rstd, p5)
                    nc.vector.tensor_scalar(var_eps[:, :], mv[:, v, :, 1], EPS, None, ALU.add).then_inc(s_ve, 1)
                if live(6):
                    reached(dve, s_rstd, p6 + 1)
                    reached(dve, s_tr, p6 - 1)
                    for b in range(2):
                        last = nc.vector.tensor_scalar(x1[:, u, b], y[:, u, b], mv[:, u, b, 0:1], rstd[:, u, b:b + 1],
                                                       ALU.subtract, ALU.mult)
                    last.then_inc(s_x1, 1)
                if live(2):
                    reached(dve, s_het, p2 + 1)
                    reached(dve, s_hom, p2 - 1)
                    for b in range(2):
                        last = nc.vector.scalar_tensor_tensor(fl[:, u, b], ps_hh[:, 2 * u + b, 0:D], norm[:, u, b:b + 1],
                                                              fh[:, u, b].bitcast(F32), ALU.mult, ALU.subtract)
                    last.then_inc(s_fl, 1)
                if isinstance(i, int) and 1 <= i <= FILTER_STEPS:
                    filters.sums_and_low(dve, i - 1, w_raw[:, (i - 1) % 2], filter_rows[:, (i - 1) % 2])

            pipeline(dve, pairs, STAGES, step, PEELED)

        @block.tensor
        def _(pe):
            pe.wait_ge(s_wl, 1)
            pe.wait_ge(s_bt, 3)

            def step(i, u, live):
                v = 1 - u
                if live(3):
                    p = i - 3
                    reached(pe, s_fl, p + 1)
                    reached(pe, s_al, p + 1)
                    reached(pe, s_diff, p)
                    for b in range(2):
                        for n, (aa, ff) in enumerate(((al, fh), (ah, fl), (ah, fh))):
                            last = nc.tensor.matmul(ps_hom[:, b], aa[:, v, b], ff[:, v, b], start=(n == 0), stop=(n == 2))
                    last.then_inc(s_hom, 1)
                if live(2):
                    p = i - 2
                    reached(pe, s_xl, p + 1)
                    reached(pe, s_fl, p - 1)
                    reached(pe, s_gate, p - 1)
                    terms = [(xx, ww, k) for k in range(KD) for xx, ww in ((xl, w_hi), (xh, w_lo), (xh, w_hi))]
                    for b in range(2):
                        for n, (xx, ww, k) in enumerate(terms):
                            last = nc.tensor.matmul(ps_hh[:, 2 * u + b, :], xx[:, u, k, b * P:b * P + P], ww[:, k, 0:2 * D],
                                                    start=(n == 0), stop=(n == len(terms) - 1))
                        last.then_inc(s_proj, 1)
                if live(7):
                    p = i - 7
                    reached(pe, s_x1, p + 1)
                    reached(pe, s_x1t, p)
                    for b in range(2):
                        for k in range(KD):
                            last = nc.tensor.transpose(ps_t[:, k, b * P:b * P + P], x1[:, v, b, k * P:k * P + P], ident[:, :])
                    last.then_inc(s_tr, 1)
                if live(2):
                    p = i - 2
                    for b in range(2):
                        nc.tensor.matmul(ps_g[:, u, b], ones[:, :], bt_rows[:, :], start=True, stop=False)
                        for n, (xx, ww, k) in enumerate(terms):
                            last = nc.tensor.matmul(ps_g[:, u, b], xx[:, u, k, b * P:b * P + P], ww[:, k, 2 * D:3 * D],
                                                    start=False, stop=(n == len(terms) - 1))
                    last.then_inc(s_gp, 1)

            pipeline(pe, pairs, STAGES, step, PEELED)


PA, PB = 0.75, 1.5
PA2, PB2 = PA * PA, PB * PB
FA = 1 / (2 * PA2 * (PA2 - PB2))
FB = 1 / (2 * PB2 * (PB2 - PA2))
F0 = 1 / (PA2 * PB2)
SIDES = 6


class Filters:

    def __init__(self, nc, ctx, w_c2, stored):
        self.nc, self.w_c2, self.stored = nc, w_c2, stored
        self.taps = w_c2.shape[2]
        self.triples = (self.taps + 2) // 3
        assert self.taps == 3 * self.triples - 1 and KD == 2
        self.units = KD * self.triples
        self.per_tile = SIDES * self.triples - 1
        self.parts = [ctx.enter_context(nc.sbuf_tensor(f"filter_{part}", [P, self.per_tile, D], F32R)) for part in ("high", "low")]
        self.high_part, self.low_part = self.parts

        def sem(name):
            return ctx.enter_context(nc.semaphore(f"filter_{name}"))

        self.s_raw = [sem("taps_loaded0"), sem("taps_loaded1")]
        self.s_outer = sem("outer_taps_summed")
        self.s_sums = sem("sums_done")
        self.s_high = sem("high_done")
        self.s_low_outer = sem("low_of_taps_done")
        self.s_low_inner = sem("low_of_sums_done")
        self.s_stored = sem("stored")
        self.s_side = [sem(f"side{s}_loaded") for s in range(SIDES)]

    def made(self, c):
        return self.per_tile * (c // self.triples) + SIDES * (c % self.triples)

    def outer(self, c):
        return 2 * c - c // self.triples

    def load(self, sp, c, raw):
        tile, q = KD - 1 - c // self.triples, c % self.triples
        taps = min(3, self.taps - 3 * q)
        reached(sp, self.s_low_outer, self.outer(c - 1))
        sp.dma_start(raw[:, 0:taps * D].rearrange("p (z o) -> p z o", z=taps),
                     self.w_c2[:, tile, 3 * q:3 * q + taps, :]).then_inc(self.s_raw[c % 2], 16)

    def last_triple(self, c):
        return c % self.triples == self.triples - 1

    def row(self, c, side):
        return side * self.triples + c % self.triples

    def taps_sides(self, c, raw):
        return [(0, raw[:, 0:D])] + ([] if self.last_triple(c) else [(5, raw[:, 2 * D:3 * D])])

    def high(self, act, c, raw, rows):
        act.wait_ge(self.s_raw[c % 2], 16 * (c // 2 + 1))
        if c >= self.triples:
            act.wait_ge(self.s_stored, 32 * (c - self.triples + 1))
        for side, source in self.taps_sides(c, raw):
            self.nc.scalar.activation(self.high_part[:, self.row(c, side)], source, ACT.Copy).then_inc(self.s_high, 1)
        for n in range(4):
            act.wait_ge(self.s_sums, 4 * c + n + 1)
            self.nc.scalar.activation(self.high_part[:, self.row(c, 1 + n)], rows[:, 2 + n], ACT.Copy).then_inc(self.s_high, 1)

    def sums_and_low(self, dve, c, raw, rows):
        dve.wait_ge(self.s_raw[c % 2], 16 * (c // 2 + 1))
        reached(dve, self.s_low_inner, 4 * (c - 1))
        outer = [raw[:, 0:D], raw[:, 0:D]]
        if not self.last_triple(c):
            for n, weight in enumerate((PA2, PB2)):
                outer[n] = rows[:, n]
                self.nc.vector.scalar_tensor_tensor(outer[n], raw[:, 2 * D:3 * D], weight, raw[:, 0:D], ALU.mult, ALU.add).then_inc(self.s_outer, 1)
            dve.wait_ge(self.s_outer, 2 * (c + 1 - c // self.triples))
        for n, weight in enumerate((PA, -PA, PB, -PB)):
            self.nc.vector.scalar_tensor_tensor(rows[:, 2 + n], raw[:, D:2 * D], weight, outer[n // 2], ALU.mult, ALU.add).then_inc(self.s_sums, 1)
        for n, (side, source) in enumerate(self.taps_sides(c, raw)):
            dve.wait_ge(self.s_high, self.made(c) + n + 1)
            self.nc.vector.tensor_tensor(self.low_part[:, self.row(c, side)], source,
                                         self.high_part[:, self.row(c, side)].bitcast(F32), ALU.subtract).then_inc(self.s_low_outer, 1)

    def low(self, pool, c, rows):
        for n in range(4):
            pool.wait_ge(self.s_high, self.made(c + 1) - 3 + n)
            self.nc.gpsimd.tensor_tensor(self.low_part[:, self.row(c, 1 + n)], rows[:, 2 + n],
                                         self.high_part[:, self.row(c, 1 + n)].bitcast(F32), ALU.subtract).then_inc(self.s_low_inner, 1)

    def store(self, sp, c):
        sp.wait_ge(self.s_low_outer, self.outer(c + 1))
        sp.wait_ge(self.s_low_inner, 4 * (c + 1))
        triple = slice(c, self.per_tile, self.triples)
        for n, part in enumerate(self.parts):
            sp.dma_start(self.stored[:, n, triple], part[:, triple].bitcast(F32)).then_inc(self.s_stored, 16)

    def load_stored(self, queue, side):
        first = side * self.triples
        rows = slice(first, min(first + self.triples, self.per_tile))
        for n, part in enumerate(self.parts):
            queue.dma_start(part[:, rows].bitcast(F32), self.stored[:, n, rows]).then_inc(self.s_side[side], 16)


def two_passes(eng, units, stages, step):
    first = stages + stages % 2
    total = 2 * units

    def peeled(i):
        step(i, i % 2, lambda s: 0 <= i - s < total, lambda s: int(i - s >= units))

    for half in range(2):
        for i in range(half * units, half * units + first):
            peeled(i)
        with eng.Fori((half * units + first) // 2, (half + 1) * units // 2) as two:
            for u in range(2):
                step(two * 2 + u, u, lambda s: True, lambda s: half)
    for i in range(total, total + stages - 1):
        peeled(i)


def phase_b(nc, G, x1_t, w_c1, bn1, bn2, part_t, xc_t, filters):
    B = 8
    HB = B // 2
    T, HT = B * P, HB * P
    R = 4
    groups = G // B
    PAD = (filters.taps - 1) // 2
    Q = filters.triples
    QT = P // R
    EDGE = PAD // R
    HW = QT + 2 * EDGE
    SW = HW - 1
    assert PAD % R == 0 and PB2 == 4 * PA2
    NSEQ = 5
    PRODUCTS = ((0, 0, 0, Q), (5, 0, 1, Q - 1), (1, 1, 0, Q), (2, 2, 0, Q), (3, 3, 0, Q), (4, 4, 0, Q))
    MADE = {bank: n + 1 for n, (bank, _, _, _) in enumerate(PRODUCTS)}
    SEQ_READ = (2, 3, 4, 5, 6)
    with ExitStack() as ctx:
        def sb(name, shape, dt=F32):
            return ctx.enter_context(nc.sbuf_tensor("b_" + name, shape, dt))

        def sem(name):
            return ctx.enter_context(nc.semaphore("b_" + name))

        w2_h, w2_l = filters.high_part, filters.low_part
        w1_h = sb("w1_h", [P, KD, D], F32R)
        w1_l = sb("w1_l", [P, KD, D], F32R)
        seq_h = sb("seq_h", [P, NSEQ, R, B, SW], F32R)
        seq_l = sb("seq_l", [P, NSEQ, R, B, SW], F32R)
        hp = sb("hp", [P, R, B, HW])
        hpa = sb("hpa", [P, R, B, HW])
        hpb = sb("hpb", [P, R, B, HW])
        uu = sb("uu", [P, R, B, HW])
        ww = sb("ww", [P, R, B, HW])
        seq = sb("seq", [P, 2, R, B, SW])
        x = sb("x", [P, 2, KD, HT])
        xh = sb("xh", [P, KD, HT], F32R)
        xl = sb("xl", [P, KD, HT], F32R)
        pa = sb("pa", [P, 2, KD, B * QT])
        pb = sb("pb", [P, 2, KD, B * QT])
        y = sb("y", [P, R, KD, B * QT])
        t = sb("t", [P, KD, T])
        bn = sb("bn", [P, 2, 4, KD])
        ve = sb("ve", [P, 2, KD])
        rs = sb("rs", [P, 2, KD])
        scale = sb("scale", [P, 2, KD])
        mscale = sb("mscale", [P, 2, KD])
        shift = sb("shift", [P, 2, KD])
        scale_a2 = sb("scale_a2", [P, KD])
        neg_half = sb("neg_half", [P, 2, KD])

        ps_c1 = ctx.enter_context(nc.psum_tensor("b_ps_c1", [P, 2, HT], F32))
        ps_m = ctx.enter_context(nc.psum_tensor("b_ps_m", [P, SIDES, KD, B * QT], F32))

        s_w1 = sem("conv1_weights_loaded")
        s_bnl = sem("bn_loaded")
        s_half = sem("half_ready")
        s_pad = sem("padding_zeroed")
        s_c = sem("bn_steps")
        s_rs = sem("bn_rsqrt")
        s_w1h = sem("conv1_weights_high")
        s_w1l = sem("conv1_weights_low")
        s_x = [sem("x1_half0_loaded"), sem("x1_half1_loaded")]
        s_xh = sem("x1_high")
        s_xl = sem("x1_low")
        s_c1 = sem("conv1_done")
        s_hp = sem("conv1_activated")
        s_hs = sem("conv1_scaled")
        s_u = sem("u_made")
        s_w = sem("w_made")
        s_seq = sem("sequence_made")
        s_sh = sem("sequence_high")
        s_sl = sem("sequence_low")
        s_m = sem("product_done")
        s_ca = sem("m1_copied")
        s_cb = sem("m3_copied")
        s_pa = sem("m1_m2_combined")
        s_pb = sem("m3_m4_combined")
        s_y0 = sem("y0_started")
        s_y3 = sem("y3_started")
        s_y = sem("outputs_combined")
        s_res = sem("residual_loaded")
        s_t = sem("residual_added")
        s_out = [sem("result_stored0"), sem("result_stored1")]
        s_xc = sem("xconv_ready")
        w1_raw = t[:, 0, 0:KD * D].rearrange("p (c o) -> p c o", c=KD)
        block = ctx.enter_context(nc.Block())

        STAGES = 4

        def is_first(g):
            return isinstance(g, int) and g == 0

        def x_low(eng, ops, g, h):
            reached(eng, s_xh, 2 * g + h + 1)
            ops.tensor_tensor(xl[:, :, :], x[:, h], xh[:, :, :].bitcast(F32), ALU.subtract).then_inc(s_xl, 1)

        def two_apart(eng, ops, g, out, multiple, last_use, done):
            reached(eng, s_pad, 6)
            reached(eng, s_hs, 4 * g + 4)
            reached(eng, s_seq, NSEQ * (g - 1) + last_use)
            ops.tensor_tensor(out[:, 0:2], hp[:, 2:4], multiple[:, 0:2], ALU.subtract)
            ops.tensor_tensor(out[:, 2:4, :, 0:SW], hp[:, 0:2, :, 1:HW], multiple[:, 2:4, :, 0:SW], ALU.subtract).then_inc(done, 1)

        @block.sync
        def _(sp):
            def nodes_of(g, k, first=0, count=T):
                return bass.ds((g - k * groups) * T + first, count)

            def step(i, u, live, tile):
                if live(0):
                    g = i
                    for h in range(2):
                        reached(sp, s_xl, 2 * g - 1 + h)
                        sp.dma_start(x[:, h], x1_t[:, :, nodes_of(g, tile(0), h * HT, HT)]).then_inc(s_x[h], 16)
                if isinstance(i, int) and i == 0:
                    sp.dma_start(w1_raw, w_c1).then_inc(s_w1, 16)
                    for n, vectors in enumerate((bn1, bn2)):
                        sp.dma_start(bn[:, n], vectors).then_inc(s_bnl, 16)
                if live(3):
                    g = i - 3
                    for mt in range(KD):
                        if tile(3) == 0:
                            reached(sp, s_t, 3 * (KD * g + mt + 1))
                        else:
                            reached(sp, s_xc, KD * (g - groups) + mt + 1)
                        out_t = (part_t, xc_t)[tile(3)]
                        sp.dma_start(out_t[:, mt, nodes_of(g, tile(3))], t[:, mt]).then_inc(s_out[mt], 16)
                if live(2):
                    g = i - 2
                    if isinstance(i, int) and i == 2:
                        sp.wait_ge(s_w1l, 1)
                    for mt in range(KD):
                        reached(sp, s_out[mt], 16 * g)
                    sp.dma_start(t[:, :, :], (x1_t, part_t)[tile(2)][:, :, nodes_of(g, tile(2))]).then_inc(s_res, 16)

            two_passes(sp, groups, STAGES, step)
            for mt in range(KD):
                sp.wait_ge(s_out[mt], 16 * KD * groups)

        @block.scalar
        def _(act):
            def high(g, v, s):
                reached(act, s_seq, NSEQ * g + s + 1)
                reached(act, s_m, SIDES * (g - 1) + SEQ_READ[s])
                nc.scalar.activation(seq_h[:, s], seq[:, (v + s) % 2], ACT.Copy).then_inc(s_sh, 1)

            def split_x(g, h):
                reached(act, s_x[h], 16 * g + 16)
                reached(act, s_c1, 2 * g + h)
                nc.scalar.activation(xh[:, :, :], x[:, h], ACT.Copy).then_inc(s_xh, 1)

            def conv1_out(g, h, k):
                graphs = slice(h * HB, h * HB + HB)
                inner = slice(EDGE, EDGE + QT)
                reached(act, s_c1, 2 * g + h + 1)
                reached(act, s_w, g)
                reached(act, s_u, g)
                nc.scalar.activation(hp[:, :, graphs, inner], ps_c1[:, h].rearrange("p (b i r) -> p r b i", b=HB, r=R), ACT.Relu,
                                     bias=shift[:, 0, k:k + 1], scale=scale[:, 0, k:k + 1]).then_inc(s_hp, 1)
                reached(act, s_hp, 2 * g + h + 1)
                for multiple, factor in ((hpb, PB2), (hpa, PA2)):
                    nc.scalar.activation(multiple[:, :, graphs, inner], hp[:, :, graphs, inner], ACT.Copy, scale=factor).then_inc(s_hs, 1)

            def copies(g, bank, pair, factors, done):
                reached(act, s_m, SIDES * g + MADE[bank])
                reached(act, s_y, 4 * g)
                for n, factor in enumerate(factors):
                    nc.scalar.activation(pair[:, n], ps_m[:, bank], ACT.Copy, scale=factor).then_inc(done, 1)

            def next_filters(*banks):
                for bank in banks:
                    act.wait_ge(s_m, SIDES * (groups - 1) + MADE[bank])
                    filters.load_stored(act, bank)

            def step(i, u, live, tile):
                v = 1 - u
                gf, gc, go = i - 1, i - 2, i - 3
                new_filters = i - groups if isinstance(i, int) else 0
                if live(2):
                    for s in (3, 4):
                        high(gc, u, s)
                    if new_filters == 2:
                        next_filters(4)
                if live(1):
                    split_x(gf, 1)
                    conv1_out(gf, 0, tile(1))
                    conv1_out(gf, 1, tile(1))
                if live(0):
                    split_x(i, 0)
                if isinstance(i, int) and i == 0:
                    act.wait_ge(s_w1, 16)
                    nc.scalar.activation(w1_h[:, :, :], w1_raw, ACT.Copy).then_inc(s_w1h, 1)
                    act.wait_ge(s_c, 5)
                if live(3) and tile(3) == 1:
                    for mt in range(KD):
                        reached(act, s_t, 3 * (KD * go + mt + 1))
                        nc.scalar.activation(t[:, mt], t[:, mt], ACT.Relu, bias=shift[:, 1, mt:mt + 1]).then_inc(s_xc, 1)
                if live(2):
                    copies(gc, 1, pa, (FA, FA * PA), s_ca)
                if live(1):
                    for s in (0, 1, 2):
                        high(gf, v, s)
                        if new_filters == 1:
                            next_filters(*((0, 5), (1,), (2,))[s])
                if live(2):
                    copies(gc, 3, pb, (FB, FB * PB), s_cb)
                    if new_filters == 1:
                        next_filters(3)

            two_passes(act, groups, STAGES, step)

        @block.gpsimd
        def _(pool):
            nc.gpsimd.memset(neg_half[:, :, :], -0.5).then_inc(s_half, 1)
            for padded in (hp, hpa, hpb):
                for edge in (slice(0, EDGE), slice(EDGE + QT, HW)):
                    nc.gpsimd.memset(padded[:, :, :, edge], 0.0).then_inc(s_pad, 1)
            pool.wait_ge(s_half, 1)
            pool.wait_ge(s_c, 1)
            nc.gpsimd.tensor_tensor(rs[:, :, :], ve[:, :, :], neg_half[:, :, :], ALU.pow).then_inc(s_rs, 1)

            def step(i, u, live, tile):
                if live(1) and not is_first(i - 1):
                    x_low(pool, nc.gpsimd, i - 1, 1)
                    two_apart(pool, nc.gpsimd, i - 1, uu, hpb, 3, s_u)
                    two_apart(pool, nc.gpsimd, i - 1, ww, hpa, 5, s_w)
                if live(0) and not is_first(i):
                    x_low(pool, nc.gpsimd, i, 0)

            two_passes(pool, groups, STAGES, step)

        @block.vector
        def _(dve):
            dve.wait_ge(s_bnl, 32)
            nc.vector.tensor_scalar(ve[:, :, :], bn[:, :, 3], EPS, None, ALU.add).then_inc(s_c, 1)
            dve.wait_ge(s_rs, 1)
            nc.vector.tensor_tensor(scale[:, :, :], bn[:, :, 0], rs[:, :, :], ALU.mult).then_inc(s_c, 1)
            dve.wait_ge(s_c, 2)
            nc.vector.tensor_tensor(mscale[:, :, :], bn[:, :, 2], scale[:, :, :], ALU.mult).then_inc(s_c, 1)
            nc.vector.tensor_scalar(scale_a2[:, :], scale[:, 1], PA2, None, ALU.mult).then_inc(s_c, 1)
            dve.wait_ge(s_c, 4)
            nc.vector.tensor_tensor(shift[:, :, :], bn[:, :, 1], mscale[:, :, :], ALU.subtract).then_inc(s_c, 1)
            dve.wait_ge(s_w1h, 1)
            nc.vector.tensor_tensor(w1_l[:, :, :], w1_raw, w1_h[:, :, :].bitcast(F32), ALU.subtract).then_inc(s_w1l, 1)

            def sequence(g, v, s):
                reached(dve, s_sl, NSEQ * g + s - 1)
                reached(dve, s_u if s < 3 else s_w, g + 1)
                out = seq[:, (v + s) % 2]
                if s == 0:
                    nc.vector.scalar_tensor_tensor(out[:, 0:2], uu[:, 0:2, :, 0:SW], -PA2, uu[:, 2:4, :, 0:SW], ALU.mult, ALU.add)
                    last = nc.vector.scalar_tensor_tensor(out[:, 2:4], uu[:, 2:4, :, 0:SW], -PA2, uu[:, 0:2, :, 1:HW], ALU.mult, ALU.add)
                else:
                    src, weight = ((uu, PA), (uu, -PA), (ww, PB), (ww, -PB))[s - 1]
                    nc.vector.scalar_tensor_tensor(out[:, 0:2], src[:, 1:3, :, 0:SW], weight, src[:, 2:4, :, 0:SW], ALU.mult, ALU.add)
                    nc.vector.scalar_tensor_tensor(out[:, 2], src[:, 3, :, 0:SW], weight, src[:, 0, :, 1:HW], ALU.mult, ALU.add)
                    last = nc.vector.scalar_tensor_tensor(out[:, 3], src[:, 0, :, 1:HW], weight, src[:, 1, :, 1:HW], ALU.mult, ALU.add)
                last.then_inc(s_seq, 1)

            def sequence_low(g, v, s):
                reached(dve, s_sh, NSEQ * g + s + 1)
                reached(dve, s_seq, NSEQ * g + s + 1)
                nc.vector.tensor_tensor(seq_l[:, s], seq[:, (v + s) % 2], seq_h[:, s].bitcast(F32), ALU.subtract).then_inc(s_sl, 1)

            def start_outputs(g):
                reached(dve, s_ca, 2 * g + 2)
                reached(dve, s_m, SIDES * g + MADE[2])
                nc.vector.scalar_tensor_tensor(pa[:, 0], ps_m[:, 2], FA, pa[:, 0], ALU.mult, ALU.add).then_inc(s_pa, 1)
                nc.vector.scalar_tensor_tensor(pa[:, 1], ps_m[:, 2], -FA * PA, pa[:, 1], ALU.mult, ALU.add).then_inc(s_pa, 1)
                reached(dve, s_t, 6 * g)
                reached(dve, s_pa, 2 * g + 2)
                nc.vector.scalar_tensor_tensor(y[:, 0], ps_m[:, 0], F0, pa[:, 0], ALU.mult, ALU.add).then_inc(s_y0, 1)
                nc.vector.scalar_tensor_tensor(y[:, 3], pa[:, 1], PA2, ps_m[:, 5], ALU.mult, ALU.add).then_inc(s_y3, 1)

            def finish_outputs(g):
                reached(dve, s_cb, 2 * g + 2)
                reached(dve, s_m, SIDES * g + MADE[4])
                nc.vector.scalar_tensor_tensor(pb[:, 0], ps_m[:, 4], FB, pb[:, 0], ALU.mult, ALU.add).then_inc(s_pb, 1)
                nc.vector.scalar_tensor_tensor(pb[:, 1], ps_m[:, 4], -FB * PB, pb[:, 1], ALU.mult, ALU.add).then_inc(s_pb, 1)
                reached(dve, s_pb, 2 * g + 2)
                reached(dve, s_y3, g + 1)
                nc.vector.tensor_tensor(y[:, 0], y[:, 0], pb[:, 0], ALU.add).then_inc(s_y, 1)
                nc.vector.tensor_tensor(y[:, 1], pa[:, 1], pb[:, 1], ALU.add).then_inc(s_y, 1)
                nc.vector.scalar_tensor_tensor(y[:, 2], pb[:, 0], PB2 / PA2, pa[:, 0], ALU.mult, ALU.add).then_inc(s_y, 1)
                nc.vector.scalar_tensor_tensor(y[:, 3], pb[:, 1], PB2, y[:, 3], ALU.mult, ALU.add).then_inc(s_y, 1)
                reached(dve, s_res, 16 * g + 16)
                reached(dve, s_y, 4 * g + 4)
                for mt in range(KD):
                    nodes = t[:, mt].rearrange("p (n r) -> p r n", r=R)
                    for residues, factor in ((slice(0, 2), scale[:, 1, mt:mt + 1]), (slice(2, 3), scale_a2[:, mt:mt + 1]),
                                             (slice(3, 4), scale[:, 1, mt:mt + 1])):
                        nc.vector.scalar_tensor_tensor(nodes[:, residues], y[:, residues, mt], factor, nodes[:, residues],
                                                       ALU.mult, ALU.add).then_inc(s_t, 1)

            def step(i, u, live, tile):
                v = 1 - u
                gf, gc, go = i - 1, i - 2, i - 3
                if live(2):
                    for s in (3, 4):
                        sequence(gc, u, s)
                    for s in (3, 4):
                        sequence_low(gc, u, s)
                if live(3):
                    finish_outputs(go)
                if live(1):
                    if is_first(gf):
                        x_low(dve, nc.vector, gf, 1)
                        two_apart(dve, nc.vector, gf, uu, hpb, 3, s_u)
                        two_apart(dve, nc.vector, gf, ww, hpa, 5, s_w)
                    for s in (0, 1):
                        sequence(gf, v, s)
                    for s in (0, 1):
                        sequence_low(gf, v, s)
                    sequence(gf, v, 2)
                if live(2):
                    start_outputs(gc)
                if live(1):
                    sequence_low(gf, v, 2)
                if live(0) and is_first(i):
                    x_low(dve, nc.vector, i, 0)

            dve.wait_ge(s_c, 5)
            two_passes(dve, groups, STAGES, step)

        @block.tensor
        def _(pe):
            pe.wait_ge(s_w1l, 1)
            pe.wait_ge(filters.s_low_outer, filters.outer(filters.units))
            pe.wait_ge(filters.s_low_inner, 4 * filters.units)

            def three_passes(out, terms):
                passes = [pair for sh, sl, mh, ml in terms for pair in ((sl, mh), (sh, ml), (sh, mh))]
                for n, (stationary, moving) in enumerate(passes):
                    last = nc.tensor.matmul(out, stationary, moving, start=(n == 0), stop=(n == len(passes) - 1))
                return last

            def conv1(g, h, k):
                cols = slice(k * P, k * P + P)
                reached(pe, s_xl, 2 * g + h + 1)
                reached(pe, s_hp, 2 * (g - 1) + h + 1)
                three_passes(ps_c1[:, h], [(w1_h[:, c, cols], w1_l[:, c, cols], xh[:, c], xl[:, c]) for c in range(KD)]).then_inc(s_c1, 1)

            def conv2(g, n):
                bank, s, first, triples = PRODUCTS[n]
                s_read, reads = ((s_y0, 1), (s_ca, 2), (s_pa, 2), (s_cb, 2), (s_pb, 2), (s_y3, 1))[bank]
                reached(pe, s_read, reads * g)
                reached(pe, s_sl, NSEQ * g + s + 1)
                if isinstance(g, int) and g == groups:
                    pe.wait_ge(filters.s_side[bank], 32)
                for mt in range(KD):
                    cols = slice(mt * P, mt * P + P)
                    terms = []
                    for q in range(triples):
                        residue, at = (3 * q + first) % R, (3 * q + first) // R
                        terms.append([w[:, bank * Q + q, cols] for w in (w2_h, w2_l)]
                                     + [d[:, s, residue, :, at:at + QT] for d in (seq_h, seq_l)])
                    last = three_passes(ps_m[:, bank, mt].rearrange("p (b i) -> p b i", b=B), terms)
                last.then_inc(s_m, 1)

            def step(i, u, live, tile):
                gf, gc = i - 1, i - 2
                if live(1):
                    conv1(gf, 0, tile(1))
                if live(2):
                    conv2(gc, 0)
                    conv2(gc, 1)
                if live(1):
                    conv1(gf, 1, tile(1))
                if live(2):
                    for n in range(2, SIDES):
                        conv2(gc, n)

            two_passes(pe, groups, STAGES, step)


def phase_c(nc, G, x1_t, xc_t, adj_t, w_ih, w_hh, w_msg, w_se, b_ih, b_hh, b_msg, b_se, form, y_n):
    B = 4
    T = B * P
    groups = G // B
    NS = w_se.shape[-1]
    with ExitStack() as ctx:
        def sb(name, shape, dt=F32):
            return ctx.enter_context(nc.sbuf_tensor("c_" + name, shape, dt))

        def sem(name):
            return ctx.enter_context(nc.semaphore("c_" + name))

        wi_h = sb("wi_h", [P, 2 * KD, 3 * D], F32R)
        wi_l = sb("wi_l", [P, 2 * KD, 3 * D], F32R)
        wh_h = sb("wh_h", [P, KD, 3 * D], F32R)
        wh_l = sb("wh_l", [P, KD, 3 * D], F32R)
        wm_h = sb("wm_h", [P, KD, D], F32R)
        wm_l = sb("wm_l", [P, KD, D], F32R)
        ws_h = sb("ws_h", [P, KD, NS], F32R)
        ws_l = sb("ws_l", [P, KD, NS], F32R)
        wi_raw = sb("wi_raw", [P, 2 * KD, 3 * D])
        wh_raw = sb("wh_raw", [P, KD, 3 * D])
        wm_raw = sb("wm_raw", [P, KD, D])
        ws_raw = sb("ws_raw", [P, KD, NS])
        bi = sb("bi", [P, 3, KD])
        bh = sb("bh", [P, 3, KD])
        brz = sb("brz", [P, 2, KD])
        bsum = sb("bsum", [P, 2, KD])
        bm_row = sb("bm_row", [P, 2, D])
        bs = sb("bs", [NS, 1])
        fm = sb("fm", [NS, 6])
        lin = sb("lin", [NS, 2])
        con = sb("con", [NS, 2])
        ident = sb("ident", [P, P])
        neg_half = sb("neg_half", [P, B])

        x1 = sb("x1", [P, 2, KD, T])
        xg = sb("xg", [P, 2, KD, T])
        xc = sb("xc", [P, 2, KD, T])
        at = sb("at", [P, 2, B, P])
        xh = sb("xh", [P, 2, KD, T], F32R)
        xl = sb("xl", [P, 2, KD, T], F32R)
        ch = sb("ch", [P, 2, KD, T], F32R)
        cl = sb("cl", [P, 2, KD, T], F32R)
        sq = sb("sq", [NS, T])
        left0 = sb("left0", [NS, T])
        right0 = sb("right0", [NS, T])
        left = sb("left", [NS, T])
        right = sb("right", [NS, T])
        mpre = sb("mpre", [P, B, D])
        mh = sb("mh", [P, B, D], F32R)
        ml = sb("ml", [P, B, D], F32R)
        ea = sb("ea", [P, B, P])
        aa = sb("aa", [P, B, P])
        ahl = sb("ahl", [P, B, 2, P], F32R)
        nsum = sb("nsum", [P, KD, B, P])
        nh = sb("nh", [P, 2, KD, T], F32R)
        nl = sb("nl", [P, 2, KD, T], F32R)
        tr = sb("tr", [P, T])
        rr = sb("rr", [P, T])
        hn = sb("hn", [P, T])
        npre = sb("npre", [P, T])
        nn = sb("nn", [P, T])
        tz = sb("tz", [P, T])
        zz = sb("zz", [P, T])
        dd = sb("dd", [P, T])
        zd = sb("zd", [P, T])
        nx = sb("nx", [P, T])
        yt = sb("yt", [P, KD, T])
        nmean = sb("nmean", [P, B])
        stats = sb("stats", [P, B, 6])
        mv = sb("mv", [P, B, 2])
        var_eps = sb("var_eps", [P, B])
        rstd = sb("rstd", [P, B])
        shift = sb("shift", [P, B])
        yo = sb("yo", [P, B, D])

        ps_g = ctx.enter_context(nc.psum_tensor("c_ps_g", [P, 3, T], F32))
        ps_s = ctx.enter_context(nc.psum_tensor("c_ps_s", [P, T], F32))
        ps_m = ctx.enter_context(nc.psum_tensor("c_ps_m", [P, 2, T], F32))
        ps_y = ctx.enter_context(nc.psum_tensor("c_ps_y", [P, B, D], F32))

        s_w = sem("message_weights_loaded")
        s_wg = [sem("w_hh_loaded"), sem("w_ih_loaded")]
        s_b = sem("biases_loaded")
        s_wh = sem("weights_high")
        s_wl = sem("weights_low")
        s_c = sem("constants")
        s_c1 = sem("constants_first_step")
        s_id0 = sem("identity_zeroed")
        s_id = sem("identity_ready")
        s_half = sem("half_ready")
        s_x = [sem("x1_loaded0"), sem("x1_loaded1")]
        s_at = [sem("adj_loaded0"), sem("adj_loaded1")]
        s_xg = [sem("x1_again_loaded0"), sem("x1_again_loaded1")]
        s_xc = [sem("xconv_loaded0"), sem("xconv_loaded1")]
        s_xh = sem("x1_high")
        s_xl = sem("x1_low")
        s_ch = sem("xconv_high")
        s_cl = sem("xconv_low")
        s_s = sem("similarity_products")
        s_sact = sem("similarity_rows_scaled")
        s_lr = sem("similarity_rows")
        s_m = sem("message_products")
        s_mpre = sem("message_biased")
        s_mh = sem("message_high")
        s_ml = sem("message_low")
        s_d = sem("distances")
        s_ea = sem("similarity_exp")
        s_aa = sem("similarity_masked")
        s_ah = sem("similarity_high")
        s_al = sem("similarity_low")
        s_nm = sem("messages_summed")
        s_n2 = sem("high_low_sums_copied")
        s_ns = sem("message_sums_added")
        s_nh = sem("message_sum_high")
        s_nl = sem("message_sum_low")
        s_gr = sem("gate_r_product")
        s_gh = sem("gate_hn_product")
        s_gi = sem("gate_in_product")
        s_gz = sem("gate_z_product")
        s_tr = sem("r_tanh")
        s_rr = sem("r_done")
        s_hn = sem("r_times_hn")
        s_np = sem("n_argument")
        s_nn = sem("n_done")
        s_tz = sem("z_tanh")
        s_zz = sem("z_done")
        s_dd = sem("x_minus_n")
        s_zd = sem("z_times_difference")
        s_nx = sem("n_plus_x")
        s_yt = sem("result_transposed_layout")
        s_y = sem("result_on_nodes")
        s_bn = sem("bn_stats_done")
        s_mv = sem("mean_var")
        s_ve = sem("var_eps_done")
        s_rstd = sem("rstd_done")
        s_nmean = sem("mean_negated")
        s_sh = sem("shift_done")
        s_yo = sem("output_ready")
        s_out = sem("output_stored")
        ah, al = ahl[:, :, 0], ahl[:, :, 1]
        ps_sums = (ps_m.rearrange("p h (b n) -> p (h b) n", b=2), ps_y)
        block = ctx.enter_context(nc.Block())

        def loaded(eng, sems, per_group, g, u):
            reached(eng, sems[u], (g + (2 - u)) * (8 * per_group))

        @block.sync
        def _(sp):
            for dst, src in ((ws_raw[:, :, :], w_se), (wm_raw[:, :, :], w_msg)):
                sp.dma_start(dst, src).then_inc(s_w, 16)

            def rest():
                for dst, src in ((bs[:, :], b_se), (fm[:, :], form), (bm_row[:, 0, :], b_msg.partition_broadcast(P)),
                                 (bm_row[:, 1, :], b_msg.partition_broadcast(P)), (bi[:, :, :], b_ih), (bh[:, :, :], b_hh)):
                    sp.dma_start(dst, src).then_inc(s_b, 16)
                for n, (dst, src) in enumerate(((wh_raw[:, :, :], w_hh), (wi_raw[:, :, :], w_ih))):
                    sp.dma_start(dst, src).then_inc(s_wg[n], 16)

            def step(i, u, live):
                if live(0):
                    g = i
                    reached(sp, s_xl, g - 1)
                    sp.dma_start(x1[:, u], x1_t[:, :, bass.ts(g, T)]).then_inc(s_x[u], 16)
                    if isinstance(i, int) and i == 0:
                        rest()
                if live(1):
                    g, v = i - 1, 1 - u
                    reached(sp, s_aa, g - 1)
                    sp.dma_start(at[:, v], adj_t[:, bass.ts(g, T)].rearrange("p (b m) -> p b m", b=B)).then_inc(s_at[v], 16)
                    reached(sp, s_cl, g - 1)
                    sp.dma_start(xc[:, v], xc_t[:, :, bass.ts(g, T)]).then_inc(s_xc[v], 16)
                if live(2):
                    g = i - 2
                    reached(sp, s_nx, 2 * g - 2)
                    sp.dma_start(xg[:, u], x1_t[:, :, bass.ts(g, T)]).then_inc(s_xg[u], 16)
                if live(4):
                    g = i - 4
                    reached(sp, s_yo, B * g + B)
                    sp.dma_start(y_n[:, bass.ts(g, B * D)].rearrange("p (b d) -> p b d", b=B), yo[:, :, :]).then_inc(s_out, 16)

            pipeline(sp, groups, 5, step)
            sp.wait_ge(s_out, 16 * groups)

        R_BANK, HN_BANK, IN_BANK, Z_BANK = (0, 1), (1, 2), (2, 0), (0, 1)

        @block.scalar
        def _(act):
            act.wait_ge(s_w, 32)
            for hi, raw in ((ws_h, ws_raw), (wm_h, wm_raw)):
                nc.scalar.activation(hi[:, :, :], raw[:, :, :], ACT.Copy).then_inc(s_wh, 1)

            def r_tanh(g, j):
                reached(act, s_gr, 2 * g + j + 1)
                reached(act, s_rr, 2 * g + j)
                nc.scalar.activation(tr[:, :], ps_g[:, R_BANK[j], :], ACT.Tanh, bias=brz[:, 0, j:j + 1], scale=0.5).then_inc(s_tr, 1)

            def n_tanh(g, j):
                reached(act, s_np, 2 * g + j + 1)
                reached(act, s_dd, 2 * g + j)
                reached(act, s_nx, 2 * g + j)
                nc.scalar.activation(nn[:, :], npre[:, :], ACT.Tanh).then_inc(s_nn, 1)

            def z_tanh(g, j):
                reached(act, s_gz, 2 * g + j + 1)
                reached(act, s_zz, 2 * g + j)
                nc.scalar.activation(tz[:, :], ps_g[:, Z_BANK[j], :], ACT.Tanh, bias=brz[:, 1, j:j + 1], scale=0.5).then_inc(s_tz, 1)

            def step(i, u, live):
                ga, v = i - 2, u
                gg = i - 3
                if isinstance(i, int) and i == 2:
                    act.wait_ge(s_wg[0], 16)
                    nc.scalar.activation(wh_h[:, :, :], wh_raw[:, :, :], ACT.Copy).then_inc(s_wh, 1)
                    act.wait_ge(s_c, 2)
                if live(3):
                    r_tanh(gg, 0)
                if live(2):
                    reached(act, s_s, ga + 1)
                    reached(act, s_lr, 2 * ga)
                    nc.scalar.activation(sq[:, :], ps_s[0:NS, :], ACT.Square, bias=bs[:, 0:1]).then_inc(s_sact, 1)
                    for side, part in ((0, left0), (1, right0)):
                        nc.scalar.activation(part[:, :], ps_s[0:NS, :], ACT.Identity, bias=con[:, side:side + 1],
                                             scale=fm[:, 3 * side + 1:3 * side + 2]).then_inc(s_sact, 1)
                    reached(act, s_mpre, 2 * ga + 2)
                    reached(act, s_nm, KD * ga)
                    nc.scalar.activation(mh[:, :, :], mpre[:, :, :], ACT.Relu).then_inc(s_mh, 1)
                if live(3):
                    n_tanh(gg, 0)
                if live(4):
                    go = i - 4
                    reached(act, s_sh, go + 1)
                    reached(act, s_out, 16 * go)
                    for b in range(B):
                        nc.scalar.activation(yo[:, b], ps_y[:, b], ACT.Identity, bias=shift[:, b:b + 1],
                                             scale=rstd[:, b:b + 1]).then_inc(s_yo, 1)
                if live(3):
                    z_tanh(gg, 0)
                if live(2):
                    loaded(act, s_xc, 1, ga, v)
                    reached(act, s_gz, 2 * ga - 2)
                    nc.scalar.activation(ch[:, v], xc[:, v], ACT.Copy).then_inc(s_ch, 1)
                    reached(act, s_d, ga + 1)
                    reached(act, s_aa, ga)
                    nc.scalar.activation(ea[:, :, :], ps_s[:, :].rearrange("p (b m) -> p b m", b=B), ACT.Exp).then_inc(s_ea, 1)
                    reached(act, s_aa, ga + 1)
                    reached(act, s_nm, KD * ga)
                    nc.scalar.activation(ah, aa[:, :, :], ACT.Copy).then_inc(s_ah, 1)
                if isinstance(i, int) and i == 2:
                    act.wait_ge(s_wg[1], 16)
                    nc.scalar.activation(wi_h[:, :, :], wi_raw[:, :, :], ACT.Copy).then_inc(s_wh, 1)
                if live(3):
                    r_tanh(gg, 1)
                if live(2):
                    reached(act, s_nl, ga)
                    for j in range(KD):
                        reached(act, s_nm, KD * ga + j + 1)
                        nc.scalar.activation(nsum[:, j], ps_sums[j][:, :, P:2 * P], ACT.Copy).then_inc(s_n2, 1)
                    reached(act, s_ns, KD * ga + KD)
                    reached(act, s_gz, 2 * ga - 2)
                    nc.scalar.activation(nh[:, v], nsum.rearrange("p j b n -> p j (b n)"), ACT.Copy).then_inc(s_nh, 1)
                if live(3):
                    n_tanh(gg, 1)
                    z_tanh(gg, 1)
                if live(1):
                    g, w = i - 1, 1 - u
                    loaded(act, s_x, 1, g, w)
                    reached(act, s_gz, 2 * g - 2)
                    nc.scalar.activation(xh[:, w], x1[:, w], ACT.Copy).then_inc(s_xh, 1)

            pipeline(act, groups, 5, step)

        @block.gpsimd
        def _(pool):
            nc.gpsimd.memset(ident[:, :], 0.0).then_inc(s_id0, 1)
            nc.gpsimd.memset(neg_half[:, :], -0.5).then_inc(s_half, 1)
            pool.wait_ge(s_id0, 1)
            nc.gpsimd.affine_select(out=ident[:, :], in_=ident[:, :], compare_op=ALU.not_equal, fill=1.0,
                                    base=0, pattern=[[-1, P]], channel_multiplier=1).then_inc(s_id, 1)
            pool.wait_ge(s_half, 1)

            def with_x(g, v, j):
                reached(pool, s_nn, 2 * g + j + 1)
                reached(pool, s_zd, 2 * g + j)
                nc.gpsimd.tensor_tensor(dd[:, :], xg[:, v, j], nn[:, :], ALU.subtract).then_inc(s_dd, 1)
                reached(pool, s_yt, 2 * g + j)
                nc.gpsimd.tensor_tensor(nx[:, :], xg[:, v, j], nn[:, :], ALU.add).then_inc(s_nx, 1)

            def step(i, u, live):
                if live(4):
                    go = i - 4
                    reached(pool, s_ve, go + 1)
                    reached(pool, s_yo, B * go)
                    nc.gpsimd.tensor_tensor(rstd[:, :], var_eps[:, :], neg_half[:, :], ALU.pow).then_inc(s_rstd, 1)
                if live(3):
                    g, w = i - 3, 1 - u
                    loaded(pool, s_xg, 1, g, w)
                    with_x(g, w, 0)
                if live(2):
                    ga, v = i - 2, u
                    reached(pool, s_ch, ga + 1)
                    nc.gpsimd.tensor_tensor(cl[:, v], xc[:, v], ch[:, v].bitcast(F32), ALU.subtract).then_inc(s_cl, 1)
                if live(3):
                    with_x(g, w, 1)

            pipeline(pool, groups, 5, step)

        @block.vector
        def _(dve):
            dve.wait_ge(s_wh, 2)
            for lo, hi, raw in ((ws_l, ws_h, ws_raw), (wm_l, wm_h, wm_raw)):
                nc.vector.tensor_tensor(lo[:, :, :], raw[:, :, :], hi[:, :, :].bitcast(F32), ALU.subtract).then_inc(s_wl, 1)

            def constants():
                dve.wait_ge(s_b, 96)
                nc.vector.tensor_tensor(bsum[:, :, :], bi[:, 0:2, :], bh[:, 0:2, :], ALU.add).then_inc(s_c1, 1)
                for side in range(2):
                    nc.vector.tensor_tensor(lin[:, side:side + 1], fm[:, 3 * side + 1:3 * side + 2], bs[:, :], ALU.mult).then_inc(s_c1, 1)
                dve.wait_ge(s_c1, 3)
                nc.vector.tensor_scalar(brz[:, :, :], bsum[:, :, :], 0.5, None, ALU.mult).then_inc(s_c, 1)
                for side in range(2):
                    last = nc.vector.tensor_tensor(con[:, side:side + 1], lin[:, side:side + 1], fm[:, 3 * side + 2:3 * side + 3], ALU.add)
                last.then_inc(s_c, 1)

            def r_and_hn(g, j):
                n = 2 * g + j
                reached(dve, s_tr, n + 1)
                reached(dve, s_hn, n)
                nc.vector.tensor_scalar(rr[:, :], tr[:, :], 0.5, 0.5, ALU.mult, ALU.add).then_inc(s_rr, 1)
                reached(dve, s_gh, n + 1)
                reached(dve, s_np, n)
                reached(dve, s_rr, n + 1)
                nc.vector.scalar_tensor_tensor(hn[:, :], ps_g[:, HN_BANK[j], :], bh[:, 2, j:j + 1], rr[:, :],
                                               ALU.add, ALU.mult).then_inc(s_hn, 1)

            def n_argument(g, j):
                n = 2 * g + j
                reached(dve, s_gi, n + 1)
                reached(dve, s_hn, n + 1)
                reached(dve, s_nn, n)
                nc.vector.scalar_tensor_tensor(npre[:, :], ps_g[:, IN_BANK[j], :], bi[:, 2, j:j + 1], hn[:, :],
                                               ALU.add, ALU.add).then_inc(s_np, 1)

            def result(g, j):
                n = 2 * g + j
                reached(dve, s_tz, n + 1)
                reached(dve, s_zd, n)
                nc.vector.tensor_scalar(zz[:, :], tz[:, :], 0.5, 0.5, ALU.mult, ALU.add).then_inc(s_zz, 1)
                reached(dve, s_dd, n + 1)
                reached(dve, s_zz, n + 1)
                reached(dve, s_yt, n)
                nc.vector.tensor_tensor(zd[:, :], zz[:, :], dd[:, :], ALU.mult).then_inc(s_zd, 1)
                reached(dve, s_nx, n + 1)
                reached(dve, s_zd, n + 1)
                reached(dve, s_y, g)
                nc.vector.tensor_tensor(yt[:, j], zd[:, :], nx[:, :], ALU.add).then_inc(s_yt, 1)

            def step(i, u, live):
                ga, v = i - 2, u
                gg, go = i - 3, i - 4
                if isinstance(i, int) and i == 2:
                    constants()
                    dve.wait_ge(s_wh, 3)
                    nc.vector.tensor_tensor(wh_l[:, :, :], wh_raw[:, :, :], wh_h[:, :, :].bitcast(F32), ALU.subtract).then_inc(s_wl, 1)
                if live(3):
                    r_and_hn(gg, 0)
                if live(4):
                    reached(dve, s_sh, go)
                    reached(dve, s_y, go + 1)
                    for b in range(B):
                        last = nc.vector.bn_stats(stats[:, b], ps_y[:, b])
                    last.then_inc(s_bn, 1)
                    dve.wait_ge(s_b, 96)
                    reached(dve, s_bn, go + 1)
                    for b in range(B):
                        last = nc.vector.bn_aggr(mv[:, b], stats[:, b])
                    last.then_inc(s_mv, 1)
                    reached(dve, s_mv, go + 1)
                    nc.vector.tensor_scalar(var_eps[:, :], mv[:, :, 1], EPS, None, ALU.add).then_inc(s_ve, 1)
                    nc.vector.tensor_scalar(nmean[:, :], mv[:, :, 0], -1.0, None, ALU.mult).then_inc(s_nmean, 1)
                if live(2):
                    reached(dve, s_sact, 3 * ga + 3)
                    reached(dve, s_d, ga)
                    for side, (part, row) in enumerate(((left0, left), (right0, right))):
                        nc.vector.scalar_tensor_tensor(row[:, :], sq[:, :], fm[:, 3 * side:3 * side + 1], part[:, :],
                                                       ALU.mult, ALU.add).then_inc(s_lr, 1)
                    reached(dve, s_m, ga + 1)
                    reached(dve, s_ml, ga)
                    for h in range(2):
                        nc.vector.tensor_tensor(mpre[:, 2 * h:2 * h + 2], ps_m[:, h].rearrange("p (b d) -> p b d", b=2),
                                                bm_row[:, :, :], ALU.add).then_inc(s_mpre, 1)
                if live(4):
                    reached(dve, s_rstd, go + 1)
                    reached(dve, s_nmean, go + 1)
                    nc.vector.tensor_tensor(shift[:, :], nmean[:, :], rstd[:, :], ALU.mult).then_inc(s_sh, 1)
                if live(3):
                    n_argument(gg, 0)
                if live(2):
                    reached(dve, s_mh, ga + 1)
                    nc.vector.scalar_tensor_tensor(ml[:, :, :], mpre[:, :, :], 0.0, mh[:, :, :].bitcast(F32),
                                                   ALU.max, ALU.subtract).then_inc(s_ml, 1)
                if live(3):
                    result(gg, 0)
                if live(2):
                    reached(dve, s_ea, ga + 1)
                    loaded(dve, s_at, 1, ga, v)
                    reached(dve, s_al, ga)
                    nc.vector.tensor_tensor(aa[:, :, :], ea[:, :, :], at[:, v], ALU.mult).then_inc(s_aa, 1)
                    reached(dve, s_ah, ga + 1)
                    nc.vector.tensor_tensor(al, aa[:, :, :], ah.bitcast(F32), ALU.subtract).then_inc(s_al, 1)
                if isinstance(i, int) and i == 2:
                    dve.wait_ge(s_wh, 4)
                    nc.vector.tensor_tensor(wi_l[:, :, :], wi_raw[:, :, :], wi_h[:, :, :].bitcast(F32), ALU.subtract).then_inc(s_wl, 1)
                if live(3):
                    r_and_hn(gg, 1)
                if live(2):
                    for j in range(KD):
                        reached(dve, s_n2, KD * ga + j + 1)
                        nc.vector.tensor_tensor(nsum[:, j], nsum[:, j], ps_sums[j][:, :, 0:P], ALU.add).then_inc(s_ns, 1)
                    reached(dve, s_ns, KD * ga + KD)
                    reached(dve, s_nh, ga + 1)
                    nc.vector.tensor_tensor(nl[:, v], nsum.rearrange("p j b n -> p j (b n)"), nh[:, v].bitcast(F32), ALU.subtract).then_inc(s_nl, 1)
                if live(3):
                    n_argument(gg, 1)
                    result(gg, 1)
                if live(1):
                    g, w = i - 1, 1 - u
                    reached(dve, s_xh, g + 1)
                    nc.vector.tensor_tensor(xl[:, w], x1[:, w], xh[:, w].bitcast(F32), ALU.subtract).then_inc(s_xl, 1)

            pipeline(dve, groups, 5, step)

        @block.tensor
        def _(pe):
            pe.wait_ge(s_wl, 2)
            pe.wait_ge(s_id, 1)

            def products(out, terms):
                passes = [q for sh, sl, mh_, ml_ in terms for q in ((sl, mh_), (sh, ml_), (sh, mh_))]
                for n, (stationary, moving) in enumerate(passes):
                    last = nc.tensor.matmul(out, stationary, moving, start=(n == 0), stop=(n == len(passes) - 1))
                return last

            def gate(bank, v, which, j, own, inputs):
                cols = slice(which * D + j * P, which * D + j * P + P)
                terms = []
                if own:
                    terms += [(wh_h[:, k, cols], wh_l[:, k, cols], xh[:, v, k], xl[:, v, k]) for k in range(KD)]
                if inputs:
                    terms += [(wi_h[:, k, cols], wi_l[:, k, cols], ch[:, v, k], cl[:, v, k]) for k in range(KD)]
                    terms += [(wi_h[:, KD + k, cols], wi_l[:, KD + k, cols], nh[:, v, k], nl[:, v, k]) for k in range(KD)]
                return products(ps_g[:, bank, :], terms)

            def step(i, u, live):
                ga, v = i - 2, u
                g, w = i - 3, 1 - u
                if isinstance(i, int) and i == 3:
                    pe.wait_ge(s_wl, 4)
                if live(3):
                    reached(pe, s_nl, g + 1)
                    reached(pe, s_cl, g + 1)
                    reached(pe, s_np, 2 * g)
                    gate(R_BANK[0], w, 0, 0, True, True).then_inc(s_gr, 1)
                    reached(pe, s_tz, 2 * g)
                    gate(HN_BANK[0], w, 2, 0, True, False).then_inc(s_gh, 1)
                if live(4):
                    go = i - 4
                    reached(pe, s_yt, 2 * go + 2)
                    reached(pe, s_yo, B * go)
                    for b in range(B):
                        for j in range(KD):
                            last = nc.tensor.transpose(ps_y[:, b, j * P:j * P + P], yt[:, j, b * P:b * P + P], ident[:, :])
                    last.then_inc(s_y, 1)
                if live(2):
                    reached(pe, s_xl, ga + 1)
                    reached(pe, s_ea, ga)
                    products(ps_s[0:NS, :], [(ws_h[:, k, :], ws_l[:, k, :], xh[:, v, k], xl[:, v, k]) for k in range(KD)]).then_inc(s_s, 1)
                    reached(pe, s_nl, ga)
                    for b in range(B):
                        cols = slice(b * P, b * P + P)
                        last = products(ps_m[:, b // 2, b % 2 * D:b % 2 * D + D],
                                        [(xh[:, v, k, cols], xl[:, v, k, cols], wm_h[:, k, :], wm_l[:, k, :]) for k in range(KD)])
                    last.then_inc(s_m, 1)
                if live(3):
                    reached(pe, s_hn, 2 * g)
                    gate(IN_BANK[0], w, 2, 0, False, True).then_inc(s_gi, 1)
                    reached(pe, s_tr, 2 * g + 1)
                    gate(Z_BANK[0], w, 1, 0, True, True).then_inc(s_gz, 1)
                if live(2):
                    reached(pe, s_lr, 2 * ga + 2)
                    for b in range(B):
                        cols = slice(b * P, b * P + P)
                        last = nc.tensor.matmul(ps_s[:, cols], left[:, cols], right[:, cols], start=True, stop=True)
                    last.then_inc(s_d, 1)
                if live(3):
                    reached(pe, s_hn, 2 * g + 1)
                    gate(R_BANK[1], w, 0, 1, True, True).then_inc(s_gr, 1)
                    reached(pe, s_np, 2 * g + 1)
                    gate(HN_BANK[1], w, 2, 1, True, False).then_inc(s_gh, 1)
                if live(2):
                    reached(pe, s_al, ga + 1)
                    reached(pe, s_ml, ga + 1)
                    reached(pe, s_yo, B * (ga - 1))
                    for j in range(KD):
                        for b in range(B):
                            both = ps_sums[j][:, b]
                            nc.tensor.matmul(both, mh[:, b, j * P:j * P + P], ahl[:, b].rearrange("p s n -> p (s n)"), start=True, stop=False)
                            last = nc.tensor.matmul(both[:, 0:P], ml[:, b, j * P:j * P + P], ah[:, b], start=False, stop=True)
                        last.then_inc(s_nm, 1)
                if live(3):
                    reached(pe, s_tz, 2 * g + 1)
                    gate(IN_BANK[1], w, 2, 1, False, True).then_inc(s_gi, 1)
                    reached(pe, s_tr, 2 * g + 2)
                    gate(Z_BANK[1], w, 1, 1, True, True).then_inc(s_gz, 1)

            pipeline(pe, groups, 5, step)


def similarity_rows():
    rows = np.zeros((9, 6), np.float32)
    rows[0:3, 1], rows[0:3, 4] = 1.0, 2.0
    rows[3:6, 2], rows[3:6, 3] = 1.0, -1.0
    rows[6:9, 0], rows[6:9, 5] = -1.0, 1.0
    return rows


def kernel(**inputs):
    from concourse import bacc
    from concourse.bass_utils import run_bass_kernel_spmd

    a = {name: np.asarray(v) for name, v in inputs.items()}
    x, adj = a["x"], a["adj"]
    G = x.shape[0]

    def tiles(w):
        return w.T.reshape(-1, P, w.shape[0]).transpose(1, 0, 2)

    def vector(b, parts):
        return b.reshape(parts, KD, P).transpose(2, 0, 1)

    def bn(layer):
        return vector(np.concatenate([a[f"L1_gnn_bn{layer}_{v}"] for v in "gbmv"]), 4)

    laid_out = {
        "x_n": x.transpose(1, 0, 2).reshape(P, G * D),
        "x_t": x.transpose(2, 0, 1).reshape(KD, P, G * P).transpose(1, 0, 2),
        "adj_n": adj.transpose(1, 0, 2).reshape(P, G * P),
        "adj_t": adj.transpose(2, 0, 1).reshape(P, G * P),
        "w0": np.concatenate([a["L0_gnn_theta"], a["L0_gnn_W_h"], a["L0_gnn_W_t"]], 1).reshape(KD, P, 3 * D).transpose(1, 0, 2),
        "b_t": a["L0_gnn_b_t"],
        "w_c1": tiles(a["L1_gnn_conv1_w"][:, :, 0]),
        "w_c2": a["L1_gnn_conv2_w"].transpose(1, 2, 0).reshape(KD, P, -1, D).transpose(1, 0, 2, 3),
        "bn1": bn(1),
        "bn2": bn(2),
        "w_ih": tiles(a["L1_gnn_w_ih"]),
        "w_hh": tiles(a["L1_gnn_w_hh"]),
        "w_msg": tiles(a["L1_gnn_w_msg"]),
        "w_se": tiles(np.concatenate([a["L1_gnn_w_se"]] * 3, 0)),
        "b_ih": vector(a["L1_gnn_b_ih"], 3),
        "b_hh": vector(a["L1_gnn_b_hh"], 3),
        "b_msg": a["L1_gnn_b_msg"],
        "b_se": np.concatenate([a["L1_gnn_b_se"]] * 3).reshape(-1, 1),
        "form": similarity_rows(),
    }
    nc = bacc.Bacc("TRN2", target_bir_lowering=False, num_devices=1)
    arrays, d = {}, {}
    for name, v in laid_out.items():
        arrays[f"in_{name}"] = np.ascontiguousarray(v)
        d[name] = nc.dram_tensor(f"in_{name}", v.shape, F32, kind="ExternalInput").ap()
    x1_t = nc.dram_tensor("x1_t", (P, KD, G * P), F32, kind="Internal").ap()
    sides = SIDES * ((d["w_c2"].shape[2] + 2) // 3) - 1
    stored_filters = nc.dram_tensor("stored_filters", (P, 2, sides, D), F32, kind="Internal").ap()
    part_t = nc.dram_tensor("part_t", (P, KD, G * P), F32, kind="Internal").ap()
    xc_t = nc.dram_tensor("xc_t", (P, KD, G * P), F32, kind="Internal").ap()
    y_n = nc.dram_tensor("out_y", (P, G * D), F32, kind="ExternalOutput").ap()
    with ExitStack() as ctx:
        filters = Filters(nc, ctx, d["w_c2"], stored_filters)
        phase_a(nc, G, d["x_n"], d["x_t"], d["adj_n"], d["adj_t"], d["w0"], d["b_t"], x1_t, filters)
        phase_b(nc, G, x1_t, d["w_c1"], d["bn1"], d["bn2"], part_t, xc_t, filters)
    phase_c(nc, G, x1_t, xc_t, d["adj_t"], d["w_ih"], d["w_hh"], d["w_msg"], d["w_se"], d["b_ih"], d["b_hh"],
            d["b_msg"], d["b_se"], d["form"], y_n)
    r = run_bass_kernel_spmd(nc, [arrays], core_ids=[0])
    return r.results[0]["out_y"].reshape(P, G, D).transpose(1, 0, 2)
```
